# Optimizing a Trainium2 kernel written in Bass

```python
import numpy as np
import jax
import jax.numpy as jnp

def _softmax(x, axis=-1):
    return jax.nn.softmax(x, axis=axis)

def _gelu(x):
    return jax.nn.gelu(x, approximate=True)

def _silu(x):
    return jax.nn.silu(x)

def _sigmoid(x):
    return jax.nn.sigmoid(x)

def _layernorm(x, axis=-1, eps=1e-05):
    m = jnp.mean(x, axis=axis, keepdims=True)
    v = jnp.var(x, axis=axis, keepdims=True)
    return (x - m) / jnp.sqrt(v + eps)

def _scatter_add(tgt, idx, src, axis=0):
    return tgt.at[idx].add(src)

def _segment_sum(src, seg, n):
    return jax.ops.segment_sum(src, seg, n)
kernel_name = 'mk_lm_tower_d2_tok_ids1024_r4_21e85f'

def setup_inputs(seed: int=0):
    np.random.seed(seed)
    _w = jnp.asarray

    def _rec_inputs():
        import jax
        import jax.numpy as jnp
        _rk = jax.random.key(seed)
        x = jax.random.randint(jax.random.fold_in(_rk, 1), (8, 2048), 0, 12564, jnp.int32)
        return x
    x = _rec_inputs()

    def _L0_tok_setup():
        import jax, jax.numpy as jnp
        import numpy as np
        import math
        VOCAB = 50257
        NUM_FREQ = 64
        EMB_DIM = 256
        BATCH, SEQ = (8, 1024)
        key = jax.random.key(seed)
        k1, k2, k3, k4, k5 = jax.random.split(key, 5)
        token_ids = jax.random.randint(k1, (BATCH, SEQ), 0, VOCAB)
        a_n = jax.random.normal(k2, (VOCAB, NUM_FREQ), dtype=jnp.float32)
        b_n = jax.random.normal(k3, (VOCAB, NUM_FREQ), dtype=jnp.float32)
        lim = 1.0 / math.sqrt(NUM_FREQ)
        proj_w = jax.random.uniform(k4, (EMB_DIM, NUM_FREQ), minval=-lim, maxval=lim, dtype=jnp.float32)
        proj_b = jax.random.uniform(k5, (EMB_DIM,), minval=-lim, maxval=lim, dtype=jnp.float32)
        return {'token_ids': token_ids, 'a_n': a_n, 'b_n': b_n, 'proj_w': proj_w, 'proj_b': proj_b}
    _L0_tok_all = _L0_tok_setup()
    _L0_tok_in = {k: v for k, v in _L0_tok_all.items() if k in ('a_n', 'b_n', 'proj_w', 'proj_b')}
    del _L0_tok_all

    def _L0_attn_setup():
        import jax, jax.numpy as jnp
        import numpy as np
        from jax import lax
        B, L, D, H = (4, 512, 256, 16)
        DK = D // H
        DV = D // H
        SCALE = DK ** (-0.5)

        def _gla_forward(hidden_states, Wq, Wf, Wi, Wo):
            b, l, d = hidden_states.shape
            q_logits = hidden_states @ Wq
            f_logits = hidden_states @ Wf
            v = hidden_states @ Wi
            q = jax.nn.softmax(q_logits, axis=-1)
            k = 1.0 - jax.nn.softmax(f_logits, axis=-1)
            g = jax.nn.log_softmax(f_logits, axis=-1)

            def split_heads(x, hd):
                return x.reshape(b, l, H, hd).transpose(1, 0, 2, 3)
            q_t = split_heads(q, DK)
            k_t = split_heads(k, DK)
            g_t = split_heads(g, DK)
            v_t = split_heads(v, DV)

            def step(S, inp):
                qt, kt, vt, gt = inp
                S = S * jnp.exp(gt)[..., None] + kt[..., None] * vt[..., None, :]
                ot = jnp.einsum('bhk,bhkv->bhv', qt * SCALE, S)
                return (S, ot)
            S0 = jnp.zeros((b, H, DK, DV), hidden_states.dtype)
            _, o = lax.scan(step, S0, (q_t, k_t, v_t, g_t))
            o = o.transpose(1, 0, 2, 3).reshape(b, l, d)
            return o @ Wo
        key = jax.random.key(seed)
        ks = jax.random.split(key, 5)
        std = 0.02
        return {'hidden_states': jax.random.normal(ks[0], (B, L, D), jnp.float32), 'Wq': jax.random.normal(ks[1], (D, D), jnp.float32) * std, 'Wf': jax.random.normal(ks[2], (D, D), jnp.float32) * std, 'Wi': jax.random.normal(ks[3], (D, D), jnp.float32) * std, 'Wo': jax.random.normal(ks[4], (D, D), jnp.float32) * std}
    _L0_attn_all = _L0_attn_setup()
    _L0_attn_in = {k: v for k, v in _L0_attn_all.items() if k in ('Wq', 'Wf', 'Wi', 'Wo')}
    del _L0_attn_all

    def _L0_ffn_setup():
        import jax, jax.numpy as jnp
        import numpy as np
        TOP_K = 2
        key = jax.random.key(seed)
        ks = jax.random.split(key, 6)
        B, S, D, BN, E = (32, 512, 256, 64, 8)
        return {'x': jax.random.normal(ks[0], (B, S, D), dtype=jnp.float32), 'gate_w': jax.random.normal(ks[1], (E, D), dtype=jnp.float32) * 0.02, 'down_w': jax.random.normal(ks[2], (E, BN, D), dtype=jnp.float32) * 0.02, 'down_b': jax.random.normal(ks[3], (E, BN), dtype=jnp.float32) * 0.02, 'up_w': jax.random.normal(ks[4], (E, D, BN), dtype=jnp.float32) * 0.02, 'up_b': jax.random.normal(ks[5], (E, D), dtype=jnp.float32) * 0.02}
    _L0_ffn_all = _L0_ffn_setup()
    _L0_ffn_in = {k: v for k, v in _L0_ffn_all.items() if k in ('gate_w', 'down_w', 'down_b', 'up_w', 'up_b')}
    del _L0_ffn_all

    def _L1_attn_setup():
        import jax, jax.numpy as jnp
        import numpy as np
        D_MODEL = 256
        D_STATE = 16
        B, L = (4, 512)

        def _ln(x, g, b, eps=1e-05):
            mu = x.mean(-1, keepdims=True)
            var = ((x - mu) ** 2).mean(-1, keepdims=True)
            return (x - mu) * jax.lax.rsqrt(var + eps) * g + b

        def _selective_ssm(x, dt_w, dt_b, Bp_w, Bp_b, Cp_w, Cp_b, A_log, D_p):
            delta = jax.nn.softplus(x @ dt_w + dt_b)
            Bt = x @ Bp_w + Bp_b
            Ct = x @ Cp_w + Cp_b
            A = -jnp.exp(A_log)

            def step(h, inp):
                xt, dt, bt, ct = inp
                dA = jnp.exp(dt[..., None] * A)
                dBx = dt[..., None] * bt[:, None, :] * xt[..., None]
                h = dA * h + dBx
                y = jnp.einsum('bdn,bn->bd', h, ct)
                return (h, y)
            xs = (jnp.swapaxes(x, 0, 1), jnp.swapaxes(delta, 0, 1), jnp.swapaxes(Bt, 0, 1), jnp.swapaxes(Ct, 0, 1))
            h0 = jnp.zeros((x.shape[0], D_MODEL, D_STATE), dtype=x.dtype)
            _, ys = jax.lax.scan(step, h0, xs)
            return jnp.swapaxes(ys, 0, 1) + D_p * x

        def _forward(x, ln1_g, ln1_b, ln_g, ln_b, w1_w, w1_b, v1_w, v1_b, w2_w, w2_b, conv_w, dt_w, dt_b, Bp_w, Bp_b, Cp_w, Cp_b, A_log, D_p, ln2_g, ln2_b, ff1_w, ff1_b, ff2_w, ff2_b):
            res = x
            xn = _ln(x, ln1_g, ln1_b)
            xm = _ln(xn, ln_g, ln_b)
            x1 = xm @ w1_w + w1_b
            x1t = jnp.swapaxes(x1, 1, 2)
            xc = jax.lax.conv_general_dilated(x1t, conv_w, window_strides=(1,), padding=[(1, 1)], feature_group_count=D_MODEL, dimension_numbers=('NCH', 'OIH', 'NCH'))
            xc = jax.nn.silu(jnp.swapaxes(xc, 1, 2))
            y = _selective_ssm(xc, dt_w, dt_b, Bp_w, Bp_b, Cp_w, Cp_b, A_log, D_p)
            v = jax.nn.silu(xm @ v1_w + v1_b)
            mo = y * v @ w2_w + w2_b
            x = mo + res
            res2 = x
            xn2 = _ln(x, ln2_g, ln2_b)
            h = jax.nn.gelu(xn2 @ ff1_w + ff1_b, approximate=False)
            return h @ ff2_w + ff2_b + res2
        key = jax.random.key(seed)
        ks = jax.random.split(key, 16)
        s = 0.02
        d, n = (D_MODEL, D_STATE)
        inp = {'x': jax.random.normal(ks[0], (B, L, d), jnp.float32), 'ln1_g': jnp.ones((d,), jnp.float32), 'ln1_b': jnp.zeros((d,), jnp.float32), 'ln_g': jnp.ones((d,), jnp.float32), 'ln_b': jnp.zeros((d,), jnp.float32), 'w1_w': jax.random.normal(ks[1], (d, d), jnp.float32) * s, 'w1_b': jnp.zeros((d,), jnp.float32), 'v1_w': jax.random.normal(ks[2], (d, d), jnp.float32) * s, 'v1_b': jnp.zeros((d,), jnp.float32), 'w2_w': jax.random.normal(ks[3], (d, d), jnp.float32) * s, 'w2_b': jnp.zeros((d,), jnp.float32), 'conv_w': jax.random.normal(ks[4], (d, 1, 3), jnp.float32) * s, 'dt_w': jax.random.normal(ks[5], (d, d), jnp.float32) * s, 'dt_b': jnp.zeros((d,), jnp.float32), 'Bp_w': jax.random.normal(ks[6], (d, n), jnp.float32) * s, 'Bp_b': jnp.zeros((n,), jnp.float32), 'Cp_w': jax.random.normal(ks[7], (d, n), jnp.float32) * s, 'Cp_b': jnp.zeros((n,), jnp.float32), 'A_log': jnp.tile(jnp.log(jnp.arange(1, n + 1, dtype=jnp.float32)), (d, 1)), 'D_p': jnp.ones((d,), jnp.float32), 'ln2_g': jnp.ones((d,), jnp.float32), 'ln2_b': jnp.zeros((d,), jnp.float32), 'ff1_w': jax.random.normal(ks[8], (d, 3 * d), jnp.float32) * s, 'ff1_b': jnp.zeros((3 * d,), jnp.float32), 'ff2_w': jax.random.normal(ks[9], (3 * d, d), jnp.float32) * s, 'ff2_b': jnp.zeros((d,), jnp.float32)}
        return inp
    _L1_attn_all = _L1_attn_setup()
    _L1_attn_in = {k: v for k, v in _L1_attn_all.items() if k in ('ln1_g', 'ln1_b', 'ln_g', 'ln_b', 'w1_w', 'w1_b', 'v1_w', 'v1_b', 'w2_w', 'w2_b', 'conv_w', 'dt_w', 'dt_b', 'Bp_w', 'Bp_b', 'Cp_w', 'Cp_b', 'A_log', 'D_p', 'ln2_g', 'ln2_b', 'ff1_w', 'ff1_b', 'ff2_w', 'ff2_b')}
    del _L1_attn_all

    def _L1_ffn_setup():
        import jax, jax.numpy as jnp
        import numpy as np
        SL, BS, HS, FF, E, TOPK = (512, 2, 256, 1024, 8, 2)
        key = jax.random.key(seed)
        ks = jax.random.split(key, 6)
        T = SL * BS
        x = jax.random.normal(ks[0], (SL, BS, HS), jnp.float32)
        scores = jax.random.uniform(ks[1], (T, E), jnp.float32)
        expert_weights = jax.random.uniform(ks[2], (T, TOPK), jnp.float32)
        expert_indices = jax.random.randint(ks[3], (T, TOPK), 0, E, jnp.int32)
        w1 = jax.random.normal(ks[4], (E, HS, FF), jnp.float32) * (1.0 / np.sqrt(HS))
        w2 = jax.random.normal(ks[5], (E, FF, HS), jnp.float32) * (1.0 / np.sqrt(FF))
        bias = jnp.zeros((HS,), jnp.float32)
        return dict(x=x, scores=scores, expert_weights=expert_weights, expert_indices=expert_indices, w1=w1, w2=w2, bias=bias)
    _L1_ffn_all = _L1_ffn_setup()
    _L1_ffn_in = {k: v for k, v in _L1_ffn_all.items() if k in ('scores', 'expert_weights', 'expert_indices', 'w1', 'w2', 'bias')}
    del _L1_ffn_all
    return {'x': x, 'L0_tok_a_n': _L0_tok_in['a_n'], 'L0_tok_b_n': _L0_tok_in['b_n'], 'L0_tok_proj_w': _L0_tok_in['proj_w'], 'L0_tok_proj_b': _L0_tok_in['proj_b'], 'L0_attn_Wq': _L0_attn_in['Wq'], 'L0_attn_Wf': _L0_attn_in['Wf'], 'L0_attn_Wi': _L0_attn_in['Wi'], 'L0_attn_Wo': _L0_attn_in['Wo'], 'L0_ffn_gate_w': _L0_ffn_in['gate_w'], 'L0_ffn_down_w': _L0_ffn_in['down_w'], 'L0_ffn_down_b': _L0_ffn_in['down_b'], 'L0_ffn_up_w': _L0_ffn_in['up_w'], 'L0_ffn_up_b': _L0_ffn_in['up_b'], 'L1_attn_ln1_g': _L1_attn_in['ln1_g'], 'L1_attn_ln1_b': _L1_attn_in['ln1_b'], 'L1_attn_ln_g': _L1_attn_in['ln_g'], 'L1_attn_ln_b': _L1_attn_in['ln_b'], 'L1_attn_w1_w': _L1_attn_in['w1_w'], 'L1_attn_w1_b': _L1_attn_in['w1_b'], 'L1_attn_v1_w': _L1_attn_in['v1_w'], 'L1_attn_v1_b': _L1_attn_in['v1_b'], 'L1_attn_w2_w': _L1_attn_in['w2_w'], 'L1_attn_w2_b': _L1_attn_in['w2_b'], 'L1_attn_conv_w': _L1_attn_in['conv_w'], 'L1_attn_dt_w': _L1_attn_in['dt_w'], 'L1_attn_dt_b': _L1_attn_in['dt_b'], 'L1_attn_Bp_w': _L1_attn_in['Bp_w'], 'L1_attn_Bp_b': _L1_attn_in['Bp_b'], 'L1_attn_Cp_w': _L1_attn_in['Cp_w'], 'L1_attn_Cp_b': _L1_attn_in['Cp_b'], 'L1_attn_A_log': _L1_attn_in['A_log'], 'L1_attn_D_p': _L1_attn_in['D_p'], 'L1_attn_ln2_g': _L1_attn_in['ln2_g'], 'L1_attn_ln2_b': _L1_attn_in['ln2_b'], 'L1_attn_ff1_w': _L1_attn_in['ff1_w'], 'L1_attn_ff1_b': _L1_attn_in['ff1_b'], 'L1_attn_ff2_w': _L1_attn_in['ff2_w'], 'L1_attn_ff2_b': _L1_attn_in['ff2_b'], 'L1_ffn_scores': _L1_ffn_in['scores'], 'L1_ffn_expert_weights': _L1_ffn_in['expert_weights'], 'L1_ffn_expert_indices': _L1_ffn_in['expert_indices'], 'L1_ffn_w1': _L1_ffn_in['w1'], 'L1_ffn_w2': _L1_ffn_in['w2'], 'L1_ffn_bias': _L1_ffn_in['bias']}

def reference(x, L0_tok_a_n, L0_tok_b_n, L0_tok_proj_w, L0_tok_proj_b, L0_attn_Wq, L0_attn_Wf, L0_attn_Wi, L0_attn_Wo, L0_ffn_gate_w, L0_ffn_down_w, L0_ffn_down_b, L0_ffn_up_w, L0_ffn_up_b, L1_attn_ln1_g, L1_attn_ln1_b, L1_attn_ln_g, L1_attn_ln_b, L1_attn_w1_w, L1_attn_w1_b, L1_attn_v1_w, L1_attn_v1_b, L1_attn_w2_w, L1_attn_w2_b, L1_attn_conv_w, L1_attn_dt_w, L1_attn_dt_b, L1_attn_Bp_w, L1_attn_Bp_b, L1_attn_Cp_w, L1_attn_Cp_b, L1_attn_A_log, L1_attn_D_p, L1_attn_ln2_g, L1_attn_ln2_b, L1_attn_ff1_w, L1_attn_ff1_b, L1_attn_ff2_w, L1_attn_ff2_b, L1_ffn_scores, L1_ffn_expert_weights, L1_ffn_expert_indices, L1_ffn_w1, L1_ffn_w2, L1_ffn_bias):
    import jax
    import jax.numpy as jnp

    def _L0_tok_ref(token_ids, a_n, b_n, proj_w, proj_b):
        import jax, jax.numpy as jnp
        import numpy as np
        import math
        VOCAB = 50257
        NUM_FREQ = 64
        EMB_DIM = 256
        BATCH, SEQ = (8, 1024)
        x = token_ids.astype(jnp.float32)[..., None] / VOCAB
        freqs = jnp.linspace(1.0, NUM_FREQ, NUM_FREQ, dtype=jnp.float32)
        phase = 2.0 * jnp.pi * freqs * x
        emb = a_n[token_ids] * jnp.cos(phase) + b_n[token_ids] * jnp.sin(phase)
        return jnp.einsum('bsf,df->bsd', emb, proj_w) + proj_b

    def _L0_attn_ref(hidden_states, Wq, Wf, Wi, Wo):
        import jax, jax.numpy as jnp
        import numpy as np
        from jax import lax
        B, L, D, H = (4, 512, 256, 16)
        DK = D // H
        DV = D // H
        SCALE = DK ** (-0.5)

        def _gla_forward(hidden_states, Wq, Wf, Wi, Wo):
            b, l, d = hidden_states.shape
            q_logits = hidden_states @ Wq
            f_logits = hidden_states @ Wf
            v = hidden_states @ Wi
            q = jax.nn.softmax(q_logits, axis=-1)
            k = 1.0 - jax.nn.softmax(f_logits, axis=-1)
            g = jax.nn.log_softmax(f_logits, axis=-1)

            def split_heads(x, hd):
                return x.reshape(b, l, H, hd).transpose(1, 0, 2, 3)
            q_t = split_heads(q, DK)
            k_t = split_heads(k, DK)
            g_t = split_heads(g, DK)
            v_t = split_heads(v, DV)

            def step(S, inp):
                qt, kt, vt, gt = inp
                S = S * jnp.exp(gt)[..., None] + kt[..., None] * vt[..., None, :]
                ot = jnp.einsum('bhk,bhkv->bhv', qt * SCALE, S)
                return (S, ot)
            S0 = jnp.zeros((b, H, DK, DV), hidden_states.dtype)
            _, o = lax.scan(step, S0, (q_t, k_t, v_t, g_t))
            o = o.transpose(1, 0, 2, 3).reshape(b, l, d)
            return o @ Wo
        return _gla_forward(hidden_states, Wq, Wf, Wi, Wo)

    def _L0_ffn_ref(x, gate_w, down_w, down_b, up_w, up_b):
        import jax, jax.numpy as jnp
        import numpy as np
        TOP_K = 2
        pooled = x.mean(axis=1)
        gate = jax.nn.softmax(pooled @ gate_w.T, axis=-1)
        top_w, top_i = jax.lax.top_k(gate, TOP_K)
        top_w = top_w / (top_w.sum(axis=-1, keepdims=True) + 1e-08)
        Wd = down_w[top_i]
        bd = down_b[top_i]
        Wu = up_w[top_i]
        bu = up_b[top_i]
        h = jax.nn.gelu(jnp.einsum('bsd,bkcd->bksc', x, Wd) + bd[:, :, None, :], approximate=False)
        h = h * top_w[:, :, None, None]
        out = jnp.einsum('bksc,bkdc->bsd', h, Wu)
        out = out + (top_w[:, :, None] * bu).sum(axis=1)[:, None, :]
        return out

    def _L1_attn_ref(x, ln1_g, ln1_b, ln_g, ln_b, w1_w, w1_b, v1_w, v1_b, w2_w, w2_b, conv_w, dt_w, dt_b, Bp_w, Bp_b, Cp_w, Cp_b, A_log, D_p, ln2_g, ln2_b, ff1_w, ff1_b, ff2_w, ff2_b):
        import jax, jax.numpy as jnp
        import numpy as np
        D_MODEL = 256
        D_STATE = 16
        B, L = (4, 512)

        def _ln(x, g, b, eps=1e-05):
            mu = x.mean(-1, keepdims=True)
            var = ((x - mu) ** 2).mean(-1, keepdims=True)
            return (x - mu) * jax.lax.rsqrt(var + eps) * g + b

        def _selective_ssm(x, dt_w, dt_b, Bp_w, Bp_b, Cp_w, Cp_b, A_log, D_p):
            delta = jax.nn.softplus(x @ dt_w + dt_b)
            Bt = x @ Bp_w + Bp_b
            Ct = x @ Cp_w + Cp_b
            A = -jnp.exp(A_log)

            def step(h, inp):
                xt, dt, bt, ct = inp
                dA = jnp.exp(dt[..., None] * A)
                dBx = dt[..., None] * bt[:, None, :] * xt[..., None]
                h = dA * h + dBx
                y = jnp.einsum('bdn,bn->bd', h, ct)
                return (h, y)
            xs = (jnp.swapaxes(x, 0, 1), jnp.swapaxes(delta, 0, 1), jnp.swapaxes(Bt, 0, 1), jnp.swapaxes(Ct, 0, 1))
            h0 = jnp.zeros((x.shape[0], D_MODEL, D_STATE), dtype=x.dtype)
            _, ys = jax.lax.scan(step, h0, xs)
            return jnp.swapaxes(ys, 0, 1) + D_p * x

        def _forward(x, ln1_g, ln1_b, ln_g, ln_b, w1_w, w1_b, v1_w, v1_b, w2_w, w2_b, conv_w, dt_w, dt_b, Bp_w, Bp_b, Cp_w, Cp_b, A_log, D_p, ln2_g, ln2_b, ff1_w, ff1_b, ff2_w, ff2_b):
            res = x
            xn = _ln(x, ln1_g, ln1_b)
            xm = _ln(xn, ln_g, ln_b)
            x1 = xm @ w1_w + w1_b
            x1t = jnp.swapaxes(x1, 1, 2)
            xc = jax.lax.conv_general_dilated(x1t, conv_w, window_strides=(1,), padding=[(1, 1)], feature_group_count=D_MODEL, dimension_numbers=('NCH', 'OIH', 'NCH'))
            xc = jax.nn.silu(jnp.swapaxes(xc, 1, 2))
            y = _selective_ssm(xc, dt_w, dt_b, Bp_w, Bp_b, Cp_w, Cp_b, A_log, D_p)
            v = jax.nn.silu(xm @ v1_w + v1_b)
            mo = y * v @ w2_w + w2_b
            x = mo + res
            res2 = x
            xn2 = _ln(x, ln2_g, ln2_b)
            h = jax.nn.gelu(xn2 @ ff1_w + ff1_b, approximate=False)
            return h @ ff2_w + ff2_b + res2
        return _forward(x, ln1_g, ln1_b, ln_g, ln_b, w1_w, w1_b, v1_w, v1_b, w2_w, w2_b, conv_w, dt_w, dt_b, Bp_w, Bp_b, Cp_w, Cp_b, A_log, D_p, ln2_g, ln2_b, ff1_w, ff1_b, ff2_w, ff2_b)

    def _L1_ffn_ref(x, scores, expert_weights, expert_indices, w1, w2, bias):
        import jax, jax.numpy as jnp
        import numpy as np
        SL, BS, HS, FF, E, TOPK = (512, 2, 256, 1024, 8, 2)
        sl, bs, hs = x.shape
        n_exp = w1.shape[0]
        top_k = expert_indices.shape[-1]
        xf = x.reshape(-1, hs)
        flat_idx = expert_indices.reshape(-1)
        flat_w = expert_weights.reshape(-1)
        order = jnp.argsort(flat_idx)
        tok = order // top_k
        tokens_per_expert = jnp.bincount(flat_idx, length=n_exp).astype(jnp.int32)
        xs = xf[tok]
        h = jax.nn.gelu(jax.lax.ragged_dot(xs, w1, tokens_per_expert), approximate=False)
        ys = jax.lax.ragged_dot(h, w2, tokens_per_expert)
        ys = ys * flat_w[order][:, None]
        out = jnp.zeros_like(xf).at[tok].add(ys)
        return out.reshape(sl, bs, hs) + bias
    h = _L0_tok_ref(x, L0_tok_a_n, L0_tok_b_n, L0_tok_proj_w, L0_tok_proj_b)
    h = h + _L0_attn_ref(_layernorm(h, axis=-1), L0_attn_Wq, L0_attn_Wf, L0_attn_Wi, L0_attn_Wo)
    h = h + _L0_ffn_ref(_layernorm(h, axis=-1), L0_ffn_gate_w, L0_ffn_down_w, L0_ffn_down_b, L0_ffn_up_w, L0_ffn_up_b)
    h = h + _L1_attn_ref(_layernorm(h, axis=-1), L1_attn_ln1_g, L1_attn_ln1_b, L1_attn_ln_g, L1_attn_ln_b, L1_attn_w1_w, L1_attn_w1_b, L1_attn_v1_w, L1_attn_v1_b, L1_attn_w2_w, L1_attn_w2_b, L1_attn_conv_w, L1_attn_dt_w, L1_attn_dt_b, L1_attn_Bp_w, L1_attn_Bp_b, L1_attn_Cp_w, L1_attn_Cp_b, L1_attn_A_log, L1_attn_D_p, L1_attn_ln2_g, L1_attn_ln2_b, L1_attn_ff1_w, L1_attn_ff1_b, L1_attn_ff2_w, L1_attn_ff2_b)
    h = h + _L1_ffn_ref(_layernorm(h, axis=-1), L1_ffn_scores, L1_ffn_expert_weights, L1_ffn_expert_indices, L1_ffn_w1, L1_ffn_w2, L1_ffn_bias)
    return h

_drawn_inputs = setup_inputs


def setup_inputs(seed=0):
    import zlib

    import numpy as np

    out = dict(_drawn_inputs(seed))
    spreads = {'L1_attn_ln1_g': (1.0, 0.6),
     'L1_attn_ln1_b': (0.0, 0.8),
     'L1_attn_ln_g': (1.0, 0.6),
     'L1_attn_ln_b': (0.0, 0.8),
     'L1_attn_w1_b': (0.0, 0.8),
     'L1_attn_v1_b': (0.0, 0.8),
     'L1_attn_w2_b': (0.0, 0.8),
     'L1_attn_dt_b': (0.0, 0.8),
     'L1_attn_Bp_b': (0.0, 0.8),
     'L1_attn_Cp_b': (0.0, 0.8),
     'L1_attn_D_p': (1.0, 0.6),
     'L1_attn_ln2_g': (1.0, 0.6),
     'L1_attn_ln2_b': (0.0, 2.0),
     'L1_attn_ff1_b': (0.0, 2.0),
     'L1_attn_ff2_b': (0.0, 0.8),
     'L1_ffn_bias': (0.0, 0.8)}
    factors = {'L0_attn_Wq': 8.0,
     'L0_attn_Wf': 44.81,
     'L0_attn_Wi': 8.0,
     'L0_attn_Wo': 8.0,
     'L0_ffn_down_b': 23.082,
     'L1_attn_w1_w': 8.0,
     'L1_attn_v1_w': 8.0,
     'L1_attn_w2_w': 8.0,
     'L1_attn_conv_w': 8.0,
     'L1_attn_dt_w': 8.0,
     'L1_attn_Bp_w': 8.0,
     'L1_attn_Cp_w': 8.0,
     'L1_attn_A_log': 8.0,
     'L1_attn_ff1_w': 8.0,
     'L1_attn_ff2_w': 8.0,
     'L1_ffn_expert_weights': 8.0,
     'L1_ffn_w1': 8.0,
     'L1_ffn_w2': 8.0}
    for name, (base, spread) in spreads.items():
        noise = np.random.default_rng([zlib.crc32(name.encode()), seed]).standard_normal(out[name].shape)
        drawn = base * np.exp(spread * noise) if base else spread * noise
        out[name] = jnp.asarray(drawn.astype(out[name].dtype))
    for name, factor in factors.items():
        out[name] = (out[name] * factor).astype(out[name].dtype)
    return out
```

```python
from contextlib import ExitStack

import concourse.bass as bass
from concourse import mybir

F32 = mybir.dt.float32
BF16 = mybir.dt.bfloat16
I32 = mybir.dt.int32
ALU = mybir.AluOpType
ACT = mybir.ActivationFunctionType
AX = mybir.AxisListType

P = 128
D = 256
T = 512
TJ = T // P
EPS = 1e-5
PI = 3.141592653589793


def wait(eng, sem, value):
    if not (isinstance(value, int) and value <= 0):
        eng.wait_ge(sem, value)


def hold(eng, passed):
    eng.sem_inc(passed, 1)


def repeat(eng, n, body):
    body(0)
    if n > 1:
        with eng.Fori(1, n) as i:
            body(i)


def sweep(eng, chunks, front, body):
    front(0, 0)
    body(0, 0, True, False)
    body(1, 1, False, False)
    if chunks > 4:
        with eng.Fori(1, chunks // 2 - 1) as i:
            body(i * 2, 0, False, False)
            body(i * 2 + 1, 1, False, False)
    body(chunks - 2, 0, False, False)
    body(chunks - 1, 1, False, True)


def chunk_view(h):
    return h.rearrange("(c j p) d -> c p j d", j=TJ, p=P)


def one(view, c):
    return view[bass.ds(c, 1), :, :, :].rearrange("o p j d -> p (o j) d")


class Core:

    def __init__(self, nc, ctx, chunks, chunks_per_batch):
        self.nc = nc
        self.chunks = chunks
        self.bank = [ctx.enter_context(nc.psum_tensor(f"bank{i}", [P, T], F32)) for i in range(8)]
        sb = lambda name, shape, dt=F32: ctx.enter_context(nc.sbuf_tensor(name, shape, dt))
        self.ident = sb("ident", [P, P])
        self.ident_b = sb("ident_b", [P, P], BF16)
        self.neg_half = sb("neg_half", [P, 8])
        self.eps = sb("eps", [P, 8])
        self.ones = sb("ones", [P, P])
        self.keep = sb("keep", [P, chunks + 1])
        self.chunks_per_batch = chunks_per_batch


def build_constants(core):
    nc = core.nc
    with ExitStack() as ctx:
        filled = nc.alloc_semaphore(name="const_filled")
        block = ctx.enter_context(nc.Block())

        @block.gpsimd
        def _(pool):
            nc.gpsimd.memset(core.ident[:, :], 0.0).then_inc(filled, 1)
            nc.gpsimd.memset(core.ident_b[:, :], 0.0).then_inc(filled, 1)
            nc.gpsimd.memset(core.ones[:, :], 1.0).then_inc(filled, 1)
            nc.gpsimd.memset(core.neg_half[:, :], -0.5).then_inc(filled, 1)
            nc.gpsimd.memset(core.keep[:, :], 1.0).then_inc(filled, 1)
            nc.gpsimd.memset(core.eps[:, :], EPS).then_inc(filled, 1)
            pool.wait_ge(filled, 6)
            for m in (core.ident, core.ident_b):
                nc.gpsimd.affine_select(out=m[:, :], in_=m[:, :], compare_op=ALU.not_equal, fill=1.0, base=0,
                                        pattern=[[-1, P]], channel_multiplier=1)
            nc.gpsimd.memset(core.keep[:, 0::core.chunks_per_batch], 0.0).then_inc(filled, 1)
            pool.wait_ge(filled, 7)


def embedding_phase(core, ids, a_n, b_n, proj_wT, proj_b, h_out):
    nc, bank, chunks = core.nc, core.bank, core.chunks
    V, NF = a_n.shape
    tiles = ids.shape[0]
    MAGIC = 1.5 * 2.0 ** 23
    with ExitStack() as ctx:
        def sb(name, shape, dt=F32):
            return ctx.enter_context(nc.sbuf_tensor("e_" + name, shape, dt))

        def sem(name):
            return nc.alloc_semaphore(name="e_" + name)

        passed = sem("passed")

        ids_row = sb("ids_row", [tiles, P], I32)
        ids_f = sb("ids_f", [tiles, P])
        idT_f = sb("idT_f", [P, tiles])
        idT_i = sb("idT_i", [P, tiles], I32)
        freq_i = sb("freq_i", [P, NF], I32)
        freq = sb("freq", [P, NF])
        half_pi = sb("half_pi", [P, 1])
        w2 = sb("w2", [2 * NF, D])
        bias = sb("bias", [P, D])
        idx = [sb(f"idx{q}", [P, TJ], I32) for q in range(2)]
        gath = [sb(f"gath{q}", [P, TJ, 2 * NF]) for q in range(2)]
        idc = [sb(f"idc{q}", [P, TJ]) for q in range(2)]
        prod = [sb(f"prod{q}", [P, TJ, NF]) for q in range(2)]
        turns = [sb(f"turns{q}", [P, TJ, NF]) for q in range(2)]
        trig = [sb(f"trig{q}", [P, TJ, 2 * NF]) for q in range(2)]
        emb = [sb(f"emb{q}", [P, TJ, 2 * NF]) for q in range(2)]
        embT = [sb(f"embT{q}", [2 * NF, T]) for q in range(2)]
        hbuf = [sb(f"hbuf{q}", [P, TJ, D]) for q in range(2)]

        loaded, consts, ids_cast, ids_turned, ids_ready = (
            sem("loaded"), sem("consts"), sem("ids_cast"), sem("ids_turned"), sem("ids_ready"))
        idx_ready = sem("idx_ready")
        gathered = [sem(f"gathered{q}") for q in range(2)]
        step_done = sem("step_done")
        phase_ready = sem("phase_ready")
        trig_ready = sem("trig_ready")
        emb_ready = sem("emb_ready")
        embT_psum = sem("embT_psum")
        embT_ready = sem("embT_ready")
        h_psum = sem("h_psum")
        h_ready = sem("h_ready")
        stored = [sem(f"stored{q}") for q in range(2)]
        block = ctx.enter_context(nc.Block())
        hv = chunk_view(h_out)

        @block.sync
        def _(sp):
            sp.dma_start(ids_row[:, :], ids).then_inc(loaded, 16)
            sp.dma_start(w2[0:NF, :], proj_wT).then_inc(loaded, 16)
            sp.dma_start(w2[NF:2 * NF, :], proj_wT).then_inc(loaded, 16)
            sp.dma_start(bias[:, :], proj_b.partition_broadcast(P)).then_inc(loaded, 16)
            def turn(i):
                for q in range(2):
                    c = i * 2 + q
                    wait(sp, h_ready, c * 2 + 2)
                    sp.dma_start(one(hv, c), hbuf[q][:, :, :]).then_inc(stored[q], 16)

            repeat(sp, chunks // 2, turn)
            for q in range(2):
                sp.wait_ge(stored[q], 16 * (chunks // 2))

        @block.gpsimd
        def _(pool):
            nc.gpsimd.iota(freq_i[:, :], pattern=[[1, NF]], base=1, channel_multiplier=0).then_inc(consts, 1)
            nc.gpsimd.memset(half_pi[:, :], PI / 2).then_inc(consts, 1)
            def turn(i):
                for q in range(2):
                    c = i * 2 + q
                    wait(pool, idx_ready, c + 1)
                    if q == 0:
                        wait(pool, emb_ready, i * 2)
                    else:
                        wait(pool, emb_ready, i * 2)
                    hold(pool, passed)
                    for j in range(TJ):
                        off = bass.IndirectOffsetOnAxis(ap=idx[q][:, j:j + 1], axis=0)
                        nc.gpsimd.indirect_dma_start(gath[q][:, j, 0:NF], None, a_n, off).then_inc(gathered[q], 16)
                        off = bass.IndirectOffsetOnAxis(ap=idx[q][:, j:j + 1], axis=0)
                        nc.gpsimd.indirect_dma_start(gath[q][:, j, NF:2 * NF], None, b_n, off).then_inc(gathered[q], 16)

            repeat(pool, chunks // 2, turn)

        @block.vector
        def _(dve):
            dve.wait_ge(loaded, 64)
            nc.vector.tensor_copy(ids_f[:, :], ids_row[:, :]).then_inc(ids_cast, 1)
            dve.wait_ge(consts, 2)
            nc.vector.tensor_copy(freq[:, :], freq_i[:, :])
            dve.wait_ge(ids_turned, 1)
            nc.vector.tensor_copy(idT_f[:, :], bank[0][:, 0:tiles])
            nc.vector.tensor_copy(idT_i[:, :], bank[0][:, 0:tiles]).then_inc(ids_ready, 1)
            dve.wait_ge(ids_ready, 1)
            def turn(i):
                for q in range(2):
                    c = i * 2 + q
                    wait(dve, gathered[q], i * (32 * TJ))
                    nc.vector.tensor_copy(idx[q][:, :], idT_i[:, bass.ds(c * TJ, TJ)]).then_inc(idx_ready, 1)
                    nc.vector.tensor_copy(idc[q][:, :], idT_f[:, bass.ds(c * TJ, TJ)]).then_inc(step_done, 1)
                    wait(dve, step_done, c * 4 + 1)
                    nc.vector.tensor_tensor(prod[q][:, :, :], freq[:, :].unsqueeze(1).to_broadcast([P, TJ, NF]),
                                            idc[q][:, :].unsqueeze(2).to_broadcast([P, TJ, NF]),
                                            ALU.mult).then_inc(step_done, 1)
                    wait(dve, step_done, c * 4 + 2)
                    wait(dve, trig_ready, i * 2)
                    nc.vector.tensor_scalar(turns[q][:, :, :], prod[q][:, :, :], 1.0 / V, MAGIC, ALU.mult,
                                            ALU.add).then_inc(step_done, 1)
                    wait(dve, step_done, c * 4 + 3)
                    nc.vector.tensor_scalar(turns[q][:, :, :], turns[q][:, :, :], MAGIC, float(V), ALU.subtract,
                                            ALU.mult).then_inc(step_done, 1)
                    wait(dve, step_done, c * 4 + 4)
                    nc.vector.tensor_tensor(prod[q][:, :, :], prod[q][:, :, :], turns[q][:, :, :],
                                            ALU.subtract).then_inc(phase_ready, 1)
                    wait(dve, phase_ready, c * 2 + 1)
                    nc.vector.scalar_tensor_tensor(turns[q][:, :, :], prod[q][:, :, :], -1.0, prod[q][:, :, :],
                                                   ALU.mult, ALU.max).then_inc(phase_ready, 1)
                    wait(dve, gathered[q], i * (32 * TJ) + 32 * TJ)
                    wait(dve, trig_ready, c + 1)
                    wait(dve, embT_psum, i * 2)
                    nc.vector.tensor_tensor(emb[q][:, :, :], gath[q][:, :, :], trig[q][:, :, :],
                                            ALU.mult).then_inc(emb_ready, 1)
                    wait(dve, stored[q], i * 16)
                    for m in range(2):
                        wait(dve, h_psum, c * 2 + m + 1)
                        nc.vector.tensor_tensor(hbuf[q][:, 2 * m:2 * m + 2, :],
                                                bank[2 + m][:, :].rearrange("p (j d) -> p j d", j=2),
                                                bias[:, :].unsqueeze(1).to_broadcast([P, 2, D]),
                                                ALU.add).then_inc(h_ready, 1)

            repeat(dve, chunks // 2, turn)

        @block.scalar
        def _(act):
            act.wait_ge(consts, 2)
            def turn(i):
                for q in range(2):
                    c = i * 2 + q
                    wait(act, phase_ready, c * 2 + 2)
                    wait(act, emb_ready, i * 2)
                    nc.scalar.activation(trig[q][:, :, 0:NF], turns[q][:, :, :], ACT.Sin, bias=half_pi[:, :],
                                         scale=-2.0 * PI / V)
                    nc.scalar.activation(trig[q][:, :, NF:2 * NF], prod[q][:, :, :], ACT.Sin,
                                         scale=2.0 * PI / V).then_inc(trig_ready, 1)
                    wait(act, embT_psum, c + 1)
                    wait(act, h_psum, i * 4)
                    nc.scalar.copy(embT[q][:, :], bank[0][:, :]).then_inc(embT_ready, 1)

            repeat(act, chunks // 2, turn)

        @block.tensor
        def _(pe):
            pe.wait_ge(ids_cast, 1)
            nc.tensor.transpose(bank[0][:, 0:tiles], ids_f[:, :], core.ident[0:tiles, 0:tiles]).then_inc(ids_turned, 1)
            pe.wait_ge(loaded, 64)
            pe.wait_ge(ids_ready, 1)
            def turn(i):
                for q in range(2):
                    c = i * 2 + q
                    wait(pe, emb_ready, c + 1)
                    wait(pe, embT_ready, c)
                    for j in range(TJ):
                        last = nc.tensor.transpose(bank[0][:, j * P:(j + 1) * P], emb[q][:, j, :], core.ident[:, :])
                    last.then_inc(embT_psum, 1)
                    wait(pe, embT_ready, c + 1)
                    wait(pe, h_ready, c * 2)
                    for m in range(2):
                        for j in range(2):
                            t0 = (2 * m + j) * P
                            last = nc.tensor.matmul(bank[2 + m][:, j * D:(j + 1) * D], embT[q][:, t0:t0 + P],
                                                    w2[:, :], start=True, stop=True)
                        last.then_inc(h_psum, 1)

            repeat(pe, chunks // 2, turn)


def attention_phase(core, Wq, Wf, Wi, Wo, h_in, h_out):
    nc, bank, chunks = core.nc, core.bank, core.chunks
    H, DK = 16, D // 16
    DV = DK
    SCALE = DK ** -0.5
    HH = H // 2
    with ExitStack() as ctx:
        def sb(name, shape, dt=F32):
            return ctx.enter_context(nc.sbuf_tensor("a_" + name, shape, dt))

        def sem(name):
            return nc.alloc_semaphore(name="a_" + name)

        passed = sem("passed")

        wqf = sb("wqf", [P, 2, 2 * D])
        wi = sb("wi", [P, 2, D])
        wo = sb("wo", [P, 2, D])
        head = sb("head", [P, HH])
        gather = sb("gather", [P, DV, HH, DV])
        head_sq = sb("head_sq", [P, HH, DV])
        pick = sb("pick", [P, DV, HH, DK], BF16)
        hb = [sb(f"hb{q}", [P, TJ, D]) for q in range(2)]
        h_new = sb("h_new", [P, TJ, D])
        bn = sb("bn", [P, TJ, 6])
        mv = sb("mv", [P, TJ, 2])
        rstd = sb("rstd", [P, TJ])
        xh = sb("xh", [P, TJ, D])
        xT = sb("xT", [P, 2, T])
        v = sb("v", [P, 2, T + 1])
        dv = sb("dv", [P, 2, T])
        dvs = [[sb(f"dvs{q}{m}", [P, 2, T], BF16) for m in range(3)] for q in range(2)]
        ex = [sb(f"ex{s}", [P, 2, D]) for s in range(2)]
        nmx = [sb(f"nmx{s}", [P, 2]) for s in range(2)]
        sums = [sb(f"sums{s}", [P, 2]) for s in range(2)]
        rsum = [sb(f"rsum{s}", [P, 2]) for s in range(2)]
        qp = [sb(f"qp{q}", [P, 2, 2, T]) for q in range(2)]
        vq = sb("vq", [P, 2, T])
        z = [sb(f"z{s}", [P, 2, T]) for s in range(2)]
        zlast = sb("zlast", [P, DV, 2])
        carry = sb("carry", [P, DV, 2])
        oT = sb("oT", [P, 2, T])

        bc, op, tp, mm = bank[0:2], bank[2:4], bank[4:6], bank[6:8]

        loaded, sel_step, consts = sem("loaded"), sem("sel_step"), sem("consts")
        h_loaded = [sem(f"h_loaded{q}") for q in range(2)]
        bn_done, stats_ready, var_eps, rstd_ready, xh_ready = (
            sem("bn_done"), sem("stats_ready"), sem("var_eps"), sem("rstd_ready"), sem("xh_ready"))
        xT_psum, xT_ready = sem("xT_psum"), sem("xT_ready")
        vcarry_ready, v_psum, v_ready = sem("vcarry_ready"), sem("v_psum"), sem("v_ready")
        dv_ready, hi_ready, mid_ready, lo_ready = sem("dv_ready"), sem("hi_ready"), sem("mid_ready"), sem("lo_ready")
        rest1_ready, rest2_ready = sem("rest1_ready"), sem("rest2_ready")
        lg_psum = [sem(f"lg_psum{s}") for s in range(2)]
        nmx_ready = sem("nmx_ready")
        exp_done = [sem(f"exp_done{s}") for s in range(2)]
        rsum_ready = sem("rsum_ready")
        qp_ready = sem("qp_ready")
        qpT_psum = [sem(f"qpT_psum{s}") for s in range(2)]
        qpT_ready = [sem(f"qpT_ready{s}") for s in range(2)]
        sumq_psum, vq_ready = sem("sumq_psum"), sem("vq_ready")
        bc_psum = [sem(f"bc_psum{f}") for f in range(2)]
        scan_done = [sem(f"scan_done{f}") for f in range(2)]
        zlast_saved, g_ready = sem("zlast_saved"), sem("g_ready")
        red_done = [sem(f"red_done{s}") for s in range(2)]
        carry_ready = [sem(f"carry_ready{m}") for m in range(2)]
        oT_ready, ap_psum, hnew_ready, h_stored = sem("oT_ready"), sem("ap_psum"), sem("hnew_ready"), sem("h_stored")
        block = ctx.enter_context(nc.Block())
        hin, hout = chunk_view(h_in), chunk_view(h_out)

        @block.sync
        def _(sp):
            for k in range(2):
                sp.dma_start(wqf[:, k, 0:D], Wq[k * P:(k + 1) * P, :]).then_inc(loaded, 16)
                sp.dma_start(wqf[:, k, D:2 * D], Wf[k * P:(k + 1) * P, :]).then_inc(loaded, 16)
                sp.dma_start(wi[:, k, :], Wi[k * P:(k + 1) * P, :]).then_inc(loaded, 16)
                sp.dma_start(wo[:, k, :], Wo[k * P:(k + 1) * P, :]).then_inc(loaded, 16)

            def load(fc, fq):
                if not isinstance(fc, int) or fc >= 2:
                    sp.wait_ge(hnew_ready, (fc - 1) * 2)
                sp.dma_start(hb[fq][:, :, :], one(hin, fc)).then_inc(h_loaded[fq], 16)

            def store(c):
                sp.wait_ge(hnew_ready, c * 2 + 2)
                sp.dma_start(one(hout, c), h_new[:, :, :]).then_inc(h_stored, 16)

            def body(c, q, first, last):
                if not last:
                    load(c + 1, 1 - q)
                if not first:
                    store(c - 1)

            sweep(sp, chunks, load, body)
            store(chunks - 1)
            sp.wait_ge(h_stored, 16 * chunks)

        @block.gpsimd
        def _(pool):
            nc.gpsimd.memset(head[:, :], 1.0).then_inc(sel_step, 1)
            nc.gpsimd.memset(gather[:, :, :, :], 0.0).then_inc(sel_step, 1)
            nc.gpsimd.memset(pick[:, :, :, :], 0.0).then_inc(sel_step, 1)
            nc.gpsimd.memset(v[:, :, :], 0.0).then_inc(sel_step, 1)
            nc.gpsimd.memset(zlast[:, :, :], 0.0).then_inc(sel_step, 1)
            pool.wait_ge(sel_step, 5)
            nc.gpsimd.affine_select(out=head[:, :], in_=head[:, :], compare_op=ALU.is_ge, fill=0.0, base=0,
                                    pattern=[[-DK, HH]], channel_multiplier=1).then_inc(sel_step, 1)
            pool.wait_ge(sel_step, 6)
            nc.gpsimd.affine_select(out=head[:, :], in_=head[:, :], compare_op=ALU.is_ge, fill=0.0, base=DK - 1,
                                    pattern=[[DK, HH]], channel_multiplier=-1).then_inc(sel_step, 1)
            nc.gpsimd.affine_select(out=pick[:, :, :, :], in_=pick[:, :, :, :], compare_op=ALU.not_equal, fill=1.0,
                                    base=0, pattern=[[-1, DV], [-DK, HH], [0, DK]],
                                    channel_multiplier=1).then_inc(consts, 1)
            pool.wait_ge(sel_step, 7)
            for vi in range(DV):
                nc.gpsimd.tensor_copy(gather[:, vi, :, vi], head[:, :]).then_inc(consts, 1)
            nc.gpsimd.tensor_copy(head_sq[:, :, :],
                                  head[:, :].unsqueeze(2).to_broadcast([P, HH, DV])).then_inc(consts, 1)

            def front(fc, fq, k=None):
                if k in (None, 5):
                    pool.wait_ge(stats_ready, fc + 1)
                    wait(pool, xh_ready, fc)
                    nc.gpsimd.tensor_tensor(rstd[:, :], mv[:, :, 1], core.eps[:, 0:mv.shape[1]], ALU.add).then_inc(var_eps, 1)
                    pool.wait_ge(var_eps, fc + 1)
                    nc.gpsimd.tensor_tensor(rstd[:, :], rstd[:, :], core.neg_half[:, 0:TJ],
                                            ALU.pow).then_inc(rstd_ready, 1)
                if k in (None, 9):
                    pool.wait_ge(hi_ready, fc + 1)
                    nc.gpsimd.tensor_tensor(dv[:, :, :], dv[:, :, :], dvs[fq][0][:, :, :],
                                            ALU.subtract).then_inc(rest1_ready, 1)
                if k in (None, 11):
                    pool.wait_ge(mid_ready, fc + 1)
                    nc.gpsimd.tensor_tensor(dv[:, :, :], dv[:, :, :], dvs[fq][1][:, :, :],
                                            ALU.subtract).then_inc(rest2_ready, 1)

            def body(c, q, first, last):
                for vi in range(DV):
                    for f in range(2):
                        pool.wait_ge(scan_done[f], c * DV + vi + 1)
                    pool.wait_ge(zlast_saved, c * DV + vi + 1)
                    if vi == 0:
                        for s in range(2):
                            pool.wait_ge(qpT_ready[s], c * 2 + 2)
                    nc.gpsimd.tensor_tensor(z[vi % 2][:, :, :], z[vi % 2][:, :, :], qp[q][:, 0, :, :],
                                            ALU.mult).then_inc(g_ready, 1)
                    if not last:
                        front(c + 1, 1 - q, vi)

            sweep(pool, chunks, front, body)

        @block.vector
        def _(dve):
            dve.wait_ge(consts, DV + 2)

            def front(fc, fq, k=None):
                if k in (None, 5):
                    dve.wait_ge(h_loaded[fq], h_count(fc, fq))
                    for j in range(TJ):
                        last = nc.vector.bn_stats(bn[:, j, :], hb[fq][:, j, :])
                    last.then_inc(bn_done, 1)
                    dve.wait_ge(bn_done, fc + 1)
                    wait(dve, rstd_ready, fc)
                    hold(dve, passed)
                    for j in range(TJ):
                        last = nc.vector.bn_aggr(mv[:, j, :], bn[:, j, :])
                    last.then_inc(stats_ready, 1)
                if k in (None, 6):
                    dve.wait_ge(rstd_ready, fc + 1)
                    dve.wait_ge(stats_ready, fc + 1)
                    wait(dve, xT_psum, fc * 2)
                    for j in range(TJ):
                        last = nc.vector.tensor_scalar(xh[:, j, :], hb[fq][:, j, :], mv[:, j, 0:1], rstd[:, j:j + 1],
                                                       ALU.subtract, ALU.mult)
                    last.then_inc(xh_ready, 1)
                    wait(dve, v_ready, fc * 2)
                    nc.vector.tensor_scalar(v[:, :, 0:1], v[:, :, T:T + 1], core.keep[:, bass.ds(fc, 1)], None,
                                            ALU.mult).then_inc(vcarry_ready, 1)
                if k in (None, 8):
                    dve.wait_ge(v_ready, fc * 2 + 2)
                    dve.wait_ge(vcarry_ready, fc + 1)
                    wait(dve, lo_ready, fc)
                    nc.vector.tensor_tensor(dv[:, :, :], v[:, :, 0:T], v[:, :, 1:T + 1],
                                            ALU.subtract).then_inc(dv_ready, 1)
                for j in range(TJ):
                    s = j % 2
                    if k in (None, 8 + 2 * j):
                        dve.wait_ge(lg_psum[s], fc * 2 + j // 2 + 1)
                        wait(dve, exp_done[s], fc * 2 + j // 2)
                        nc.vector.tensor_reduce(nmx[s][:, :], mm[s][:, :].rearrange("p (w d) -> p w d", w=2), AX.X,
                                                ALU.max, negate=True).then_inc(nmx_ready, 1)
                    if k in (None, 9 + 2 * j):
                        dve.wait_ge(exp_done[s], fc * 2 + j // 2 + 1)
                        nc.vector.reciprocal(rsum[s][:, :], sums[s][:, :]).then_inc(rsum_ready, 1)
                        dve.wait_ge(rsum_ready, fc * TJ + j + 1)
                        nc.vector.tensor_scalar(ex[s][:, 0, :], ex[s][:, 0, :], rsum[s][:, 0:1], SCALE, ALU.mult,
                                                ALU.mult)
                        nc.vector.tensor_scalar(ex[s][:, 1, :], ex[s][:, 1, :], rsum[s][:, 1:2], None,
                                                ALU.mult).then_inc(qp_ready, 1)

            def carry_half(c, m):
                wait(dve, zlast_saved, (c - 1) * DV + DV // 2 * (m + 1) if m == 0 else c * DV)
                nc.vector.tensor_scalar(carry[:, m * 8:(m + 1) * 8, :], zlast[:, m * 8:(m + 1) * 8, :],
                                        core.keep[:, bass.ds(c, 1)], None, ALU.mult).then_inc(carry_ready[m], 1)

            def finish_scan(c):
                for s in range(2):
                    dve.wait_ge(red_done[s], (c + 1) * (DV // 2))
                wait(dve, ap_psum, c * 2)
                for f in range(2):
                    last = nc.vector.tensor_tensor(oT[:, f, :], op[f][:, :], vq[:, f, :], ALU.add)
                last.then_inc(oT_ready, 1)

            def finish_rows(c, q):
                wait(dve, h_stored, c * 16)
                for m in range(2):
                    dve.wait_ge(ap_psum, c * 2 + m + 1)
                    nc.vector.tensor_tensor(h_new[:, 2 * m:2 * m + 2, :],
                                            mm[m][:, :].rearrange("p (j d) -> p j d", j=2),
                                            hb[q][:, 2 * m:2 * m + 2, :], ALU.add).then_inc(hnew_ready, 1)

            def body(c, q, first, last):
                for vi in range(DV):
                    s = vi % 2
                    if vi == 0:
                        for s2 in range(2):
                            dve.wait_ge(qpT_ready[s2], c * 2 + 2)
                    wait(dve, red_done[s], c * (DV // 2) + vi // 2)
                    if vi in (0, 8):
                        dve.wait_ge(carry_ready[vi // 8], c + 1)
                    for f in range(2):
                        dve.wait_ge(bc_psum[f], c * DV + vi + 1)
                        nc.vector.tensor_tensor_scan(z[s][:, f, :], bc[f][:, :], qp[q][:, 1, f, :],
                                                     carry[:, vi, f:f + 1], ALU.add,
                                                     ALU.mult).then_inc(scan_done[f], 1)
                    if vi == 1 and not first:
                        finish_scan(c - 1)
                    if vi == 2:
                        dve.wait_ge(sumq_psum, c * 2 + 2)
                        wait(dve, oT_ready, c)
                        for f in range(2):
                            ins = nc.vector.tensor_tensor(vq[:, f, :], mm[f][:, :], v[:, f, 1:T + 1], ALU.mult)
                        ins.then_inc(vq_ready, 1)
                    if vi == 3 and not first:
                        finish_rows(c - 1, 1 - q)
                    if vi == 4:
                        carry_half(c, 1)
                    if not last:
                        front(c + 1, 1 - q, vi)
                        if vi == 12:
                            carry_half(c + 1, 0)

            def front0(fc, fq):
                front(fc, fq)
                carry_half(0, 0)

            def h_count(fc, fq):
                return (fc - fq) * 8 + 16

            sweep(dve, chunks, front0, body)
            finish_scan(chunks - 1)
            finish_rows(chunks - 1, 1)

        @block.scalar
        def _(act):
            act.wait_ge(consts, DV + 2)

            def front(fc, fq, k=None):
                if k in (None, 6):
                    for f in range(2):
                        act.wait_ge(xT_psum, fc * 2 + f + 1)
                        wait(act, lg_psum[1], fc * 2)
                        nc.scalar.copy(xT[:, f, :], tp[f][:, :]).then_inc(xT_ready, 1)
                if k in (None, 7):
                    act.wait_ge(vcarry_ready, fc + 1)
                    wait(act, vq_ready, fc)
                    for f in range(2):
                        act.wait_ge(v_psum, fc * 2 + f + 1)
                        nc.scalar.copy(v[:, f, 1:T + 1], mm[f][:, :]).then_inc(v_ready, 1)
                if k in (None, 8):
                    act.wait_ge(dv_ready, fc + 1)
                    if not isinstance(fc, int) or fc >= 2:
                        act.wait_ge(bc_psum[1], (fc - 1) * DV)
                    nc.scalar.copy(dvs[fq][0][:, :, :], dv[:, :, :]).then_inc(hi_ready, 1)
                if k in (None, 10):
                    act.wait_ge(rest1_ready, fc + 1)
                    nc.scalar.copy(dvs[fq][1][:, :, :], dv[:, :, :]).then_inc(mid_ready, 1)
                if k in (None, 12):
                    act.wait_ge(rest2_ready, fc + 1)
                    nc.scalar.copy(dvs[fq][2][:, :, :], dv[:, :, :]).then_inc(lo_ready, 1)
                for j in range(TJ):
                    s = j % 2
                    if k in (None, 8 + 2 * j):
                        act.wait_ge(nmx_ready, fc * TJ + j + 1)
                        act.wait_ge(lg_psum[s], fc * 2 + j // 2 + 1)
                        wait(act, qpT_psum[s], fc * 2 + j // 2)
                        wait(act, rsum_ready, fc * TJ + j - 1) if not (isinstance(fc, int) and fc * TJ + j < 2) else None
                        for w in range(2):
                            last = nc.scalar.activation(ex[s][:, w, :], mm[s][:, w * D:(w + 1) * D], ACT.Exp,
                                                        bias=nmx[s][:, w:w + 1], accum_out=sums[s][:, w:w + 1])
                        last.then_inc(exp_done[s], 1)
                    if k in (None, 9 + 2 * j):
                        act.wait_ge(qpT_psum[s], fc * 2 + j // 2 + 1)
                        if j == 0 and (not isinstance(fc, int) or fc >= 2):
                            act.wait_ge(g_ready, (fc - 1) * DV)
                            act.wait_ge(sumq_psum, (fc - 1) * 2)
                        nc.scalar.copy(qp[fq][:, :, :, j * P:(j + 1) * P],
                                       tp[s][:, :].rearrange("p (w f t) -> p w f t", w=2, f=2)
                                       ).then_inc(qpT_ready[s], 1)

            def body(c, q, first, last):
                for vi in range(DV):
                    for f in range(2):
                        act.wait_ge(scan_done[f], c * DV + vi + 1)
                    if vi in (0, 8):
                        act.wait_ge(carry_ready[vi // 8], c + 1)
                    nc.scalar.copy(zlast[:, vi, :], z[vi % 2][:, :, T - 1]).then_inc(zlast_saved, 1)
                    if not last:
                        front(c + 1, 1 - q, vi)

            sweep(act, chunks, front, body)

        @block.tensor
        def _(pe):
            pe.wait_ge(loaded, 8 * 16)
            pe.wait_ge(consts, DV + 2)

            def front(fc, fq, k=None):
                if k in (None, 6):
                    pe.wait_ge(xh_ready, fc + 1)
                    for f in range(2):
                        wait(pe, qpT_ready[f], fc * 2)
                        for j in range(TJ):
                            last = nc.tensor.transpose(tp[f][:, j * P:(j + 1) * P], xh[:, j, f * P:(f + 1) * P],
                                                       core.ident[:, :])
                        last.then_inc(xT_psum, 1)
                if k in (None, 7):
                    pe.wait_ge(xT_ready, fc * 2 + 2)
                    if not isinstance(fc, int) or fc >= 2:
                        pe.wait_ge(hnew_ready, (fc - 1) * 2)
                    elif fc == 1:
                        pe.wait_ge(vq_ready, 1)
                    for f in range(2):
                        for kk in range(2):
                            last = nc.tensor.matmul(mm[f][:, :], wi[:, kk, f * P:(f + 1) * P], xT[:, kk, :],
                                                    start=(kk == 0), stop=(kk == 1))
                        last.then_inc(v_psum, 1)
                for j in range(TJ):
                    s = j % 2
                    if k in (None, 7 + 2 * j):
                        if j < 2:
                            pe.wait_ge(v_ready, fc * 2 + s + 1)
                        wait(pe, exp_done[s], fc * 2 + j // 2)
                        for kk in range(2):
                            last = nc.tensor.matmul(mm[s][:, :], xT[:, kk, j * P:(j + 1) * P], wqf[:, kk, :],
                                                    start=(kk == 0), stop=(kk == 1))
                        last.then_inc(lg_psum[s], 1)
                    if k in (None, 9 + 2 * j):
                        pe.wait_ge(qp_ready, fc * TJ + j + 1)
                        wait(pe, qpT_ready[s], fc * 2 + j // 2)
                        for w in range(2):
                            for f in range(2):
                                last = nc.tensor.transpose(tp[s][:, (2 * w + f) * P:(2 * w + f + 1) * P],
                                                           ex[s][:, w, f * P:(f + 1) * P], core.ident[:, :])
                        last.then_inc(qpT_psum[s], 1)

            def spread_dv(c, q, vi):
                if vi == 0:
                    pe.wait_ge(lo_ready, c + 1)
                for f in range(2):
                    wait(pe, scan_done[f], c * DV + vi)
                    for m in range(3):
                        last = nc.tensor.matmul(bc[f][:, :], pick[:, vi, :, :].rearrange("p h k -> p (h k)"),
                                                dvs[q][m][:, f, :], start=(m == 0), stop=(m == 2))
                    last.then_inc(bc_psum[f], 1)

            def reduce(c, vi):
                if vi == 0:
                    wait(pe, oT_ready, c)
                pe.wait_ge(g_ready, c * DV + vi + 1)
                for f in range(2):
                    last = nc.tensor.matmul(op[f][:, :], gather[:, vi, :, :].rearrange("p h v -> p (h v)"), z[vi % 2][:, f, :],
                                            start=(vi == 0), stop=(vi == DV - 1))
                last.then_inc(red_done[vi % 2], 1)

            def project(c):
                pe.wait_ge(oT_ready, c + 1)
                for m in range(2):
                    for j in range(2):
                        t0 = (2 * m + j) * P
                        for f in range(2):
                            last = nc.tensor.matmul(mm[m][:, j * D:(j + 1) * D], oT[:, f, t0:t0 + P], wo[:, f, :],
                                                    start=(f == 0), stop=(f == 1))
                    last.then_inc(ap_psum, 1)

            def body(c, q, first, last):
                for vi in range(DV):
                    if vi + 1 < DV:
                        spread_dv(c, q, vi + 1)
                    elif not last:
                        front(c + 1, 1 - q, vi)
                        spread_dv(c + 1, 1 - q, 0)
                    if vi > 0:
                        reduce(c, vi - 1)
                    elif not first:
                        reduce(c - 1, DV - 1)
                    if vi == 1:
                        for s in range(2):
                            pe.wait_ge(exp_done[s], c * 2 + 2)
                        for f in range(2):
                            ins = nc.tensor.matmul(mm[f][:, :], head_sq[:, :, :].rearrange("p h v -> p (h v)"),
                                                   qp[q][:, 0, f, :], start=True, stop=True)
                        ins.then_inc(sumq_psum, 2)
                    if vi == 2 and not first:
                        pe.wait_ge(vq_ready, c + 1)
                        project(c - 1)
                    if not last and vi + 1 < DV:
                        front(c + 1, 1 - q, vi)

            def front0(fc, fq):
                front(fc, fq)
                for s in range(2):
                    pe.wait_ge(qpT_ready[s], 2)
                spread_dv(0, 0, 0)

            sweep(pe, chunks, front0, body)
            reduce(chunks - 1, DV - 1)
            project(chunks - 1)


def ffn_phase(core, gate_wT, down_T, down_bT, up_T, up_b, h_in, h_out):
    nc, bank, chunks = core.nc, core.bank, core.chunks
    NC = core.chunks_per_batch
    S = NC * T
    E = gate_wT.shape[1]
    C = down_T.shape[2]
    batches = chunks // NC
    with ExitStack() as ctx:
        def sb(name, shape, dt=F32):
            return ctx.enter_context(nc.sbuf_tensor("f_" + name, shape, dt))

        def sem(name):
            return nc.alloc_semaphore(name="f_" + name)

        passed = sem("passed")

        gw = sb("gw", [P, 2, E])
        dw = sb("dw", [P, 2, E, C])
        db = sb("db", [2 * C, E])
        uw = sb("uw", [2 * C, E, D])
        ub = sb("ub", [E, D])
        lower = sb("lower", [P, E, E])
        hb = [sb(f"hb{m}", [P, TJ, D]) for m in range(NC)]
        bn = sb("bn", [P, TJ, 6])
        mv = sb("mv", [P, TJ, 2])
        rstd = sb("rstd", [P, TJ])
        xh = [sb(f"xh{s}", [P, TJ, D]) for s in range(2)]
        xT = sb("xT", [P, 2, S])
        sums = sb("sums", [P, 2, NC])
        pooled = sb("pooled", [P, 2])
        pooled_b = sb("pooled_b", [P, 2, P])
        g8 = sb("g8", [P, E])
        small = sb("small", [P, 8])
        cmp_a = sb("cmp_a", [P, E, E])
        cmp_b = sb("cmp_b", [P, E, E])
        rank = sb("rank", [P, E])
        sel = sb("sel", [P, 2, E])
        selg = sb("selg", [P, 2, E])
        wsum = sb("wsum", [P, E])
        wsumT = sb("wsumT", [E, P])
        rows = sb("rows", [2 * C, 2, E])
        prod = sb("prod", [2 * C, E])
        bsel = sb("bsel", [2 * C, 1])
        wd = sb("wd", [P, 2, 2, C])
        wu = sb("wu", [2 * C, D])
        hid = [sb(f"hid{s}", [2 * C, T]) for s in range(2)]
        h_new = [sb(f"h_new{s}", [P, TJ, D]) for s in range(2)]

        loaded, lower_step = sem("loaded"), sem("lower_step")
        h_loaded = [sem(f"h_loaded{m}") for m in range(NC)]
        bn_done, stats_ready, var_eps, rstd_ready, xh_ready = (
            sem("bn_done"), sem("stats_ready"), sem("var_eps"), sem("rstd_ready"), sem("xh_ready"))
        xT_psum, xT_ready = sem("xT_psum"), sem("xT_ready")
        gate_step, pooled_ready, gate_psum, gate_exp = (
            sem("gate_step"), sem("pooled_ready"), sem("gate_psum"), sem("gate_exp"))
        wsum_psum, chosen = sem("wsum_psum"), sem("chosen")
        hid_psum, hid_ready, up_psum, hnew_ready = sem("hid_psum"), sem("hid_ready"), sem("up_psum"), sem("hnew_ready")
        stored = [sem(f"stored{s}") for s in range(2)]
        block = ctx.enter_context(nc.Block())
        hin, hout = chunk_view(h_in), chunk_view(h_out)
        GATE_STEPS = 18 + 3 * E

        @block.sync
        def _(sp):
            for k in range(2):
                sp.dma_start(gw[:, k, :], gate_wT[k * P:(k + 1) * P, :]).then_inc(loaded, 16)
                sp.dma_start(dw[:, k, :, :], down_T[k * P:(k + 1) * P, :, :]).then_inc(loaded, 16)
                sp.dma_start(db[k * C:(k + 1) * C, :], down_bT).then_inc(loaded, 16)
                sp.dma_start(uw[k * C:(k + 1) * C, :, :], up_T).then_inc(loaded, 16)
            sp.dma_start(ub[:, :], up_b).then_inc(loaded, 16)

            def load(b):
                for m in range(NC):
                    wait(sp, hnew_ready, b * (2 * NC))
                    sp.dma_start(hb[m][:, :, :], one(hin, b * NC + m)).then_inc(h_loaded[m], 16)

            def turn(b):
                load(b)
                for m in range(NC):
                    wait(sp, hnew_ready, b * (2 * NC) + 2 * m + 2)
                    sp.dma_start(one(hout, b * NC + m), h_new[m % 2][:, :, :]).then_inc(stored[m % 2], 16)

            repeat(sp, batches, turn)
            for s in range(2):
                sp.wait_ge(stored[s], 16 * chunks // 2)

        @block.gpsimd
        def _(pool):
            nc.gpsimd.memset(lower[:, :, :], 1.0).then_inc(lower_step, 1)
            pool.wait_ge(lower_step, 1)
            nc.gpsimd.affine_select(out=lower[:, :, :], in_=lower[:, :, :], compare_op=ALU.is_gt, fill=0.0, base=0,
                                    pattern=[[1, E], [-1, E]], channel_multiplier=0).then_inc(lower_step, 1)
            def turn(b):
                for m in range(NC):
                    c = b * NC + m
                    wait(pool, stats_ready, c + 1)
                    wait(pool, xh_ready, c)
                    nc.gpsimd.tensor_tensor(rstd[:, :], mv[:, :, 1], core.eps[:, 0:mv.shape[1]], ALU.add).then_inc(var_eps, 1)
                    wait(pool, var_eps, c + 1)
                    nc.gpsimd.tensor_tensor(rstd[:, :], rstd[:, :], core.neg_half[:, 0:TJ],
                                            ALU.pow).then_inc(rstd_ready, 1)

            repeat(pool, batches, turn)

        @block.vector
        def _(dve):
            dve.wait_ge(loaded, 9 * 16)
            dve.wait_ge(lower_step, 2)
            def turn(b):
                for m in range(NC):
                    c = b * NC + m
                    wait(dve, h_loaded[m], b * 16 + 16)
                    for j in range(TJ):
                        last = nc.vector.bn_stats(bn[:, j, :], hb[m][:, j, :])
                    last.then_inc(bn_done, 1)
                    wait(dve, bn_done, c + 1)
                    wait(dve, rstd_ready, c)
                    hold(dve, passed)
                    for j in range(TJ):
                        last = nc.vector.bn_aggr(mv[:, j, :], bn[:, j, :])
                    last.then_inc(stats_ready, 1)
                    wait(dve, stats_ready, c + 1)
                    wait(dve, rstd_ready, c + 1)
                    if m >= 2:
                        wait(dve, xT_psum, b * (2 * NC) + 2 * (m - 1))
                    else:
                        wait(dve, xT_psum, b * (2 * NC))
                    for j in range(TJ):
                        last = nc.vector.tensor_scalar(xh[m % 2][:, j, :], hb[m][:, j, :], mv[:, j, 0:1],
                                                       rstd[:, j:j + 1], ALU.subtract, ALU.mult)
                    last.then_inc(xh_ready, 1)

                steps = [0]

                def step(ins):
                    ins.then_inc(gate_step, 1)
                    steps[0] += 1
                    wait(dve, gate_step, b * GATE_STEPS + steps[0])

                wait(dve, xT_ready, b * (2 * NC) + 2 * NC)
                wait(dve, gate_psum, b)
                step(nc.vector.tensor_reduce(pooled[:, :], sums[:, :, :], AX.X, ALU.add))
                for k in range(2):
                    last = nc.vector.tensor_scalar(pooled_b[:, k, :], core.ones[:, :], pooled[:, k:k + 1], 1.0 / S,
                                                   ALU.mult, ALU.mult)
                last.then_inc(pooled_ready, 1)
                wait(dve, gate_psum, b + 1)
                step(nc.vector.tensor_reduce(small[:, 0:1], bank[2][:, 0:E], AX.X, ALU.max, negate=True))
                wait(dve, gate_exp, b + 1)
                step(nc.vector.reciprocal(small[:, 2:3], small[:, 1:2]))
                step(nc.vector.tensor_scalar(g8[:, :], g8[:, :], small[:, 2:3], None, ALU.mult))
                g_of_j = g8[:, :].unsqueeze(1).to_broadcast([P, E, E])
                g_of_e = g8[:, :].unsqueeze(2).to_broadcast([P, E, E])
                nc.vector.tensor_tensor(cmp_a[:, :, :], g_of_j, g_of_e, ALU.is_gt)
                step(nc.vector.tensor_tensor(cmp_b[:, :, :], g_of_j, g_of_e, ALU.is_equal))
                step(nc.vector.tensor_tensor(cmp_b[:, :, :], cmp_b[:, :, :], lower[:, :, :], ALU.mult))
                step(nc.vector.tensor_tensor(cmp_a[:, :, :], cmp_a[:, :, :], cmp_b[:, :, :], ALU.add))
                step(nc.vector.tensor_reduce(rank[:, :], cmp_a[:, :, :], AX.X, ALU.add))
                for k in range(2):
                    last = nc.vector.tensor_scalar(sel[:, k, :], rank[:, :], float(k), None, ALU.is_equal)
                step(last)
                step(nc.vector.tensor_tensor(selg[:, :, :], sel[:, :, :], g8[:, :].unsqueeze(1).to_broadcast([P, 2, E]),
                                             ALU.mult))
                step(nc.vector.tensor_reduce(small[:, 3:5], selg[:, :, :], AX.X, ALU.add))
                step(nc.vector.tensor_tensor(small[:, 5:6], small[:, 3:4], small[:, 4:5], ALU.add))
                step(nc.vector.tensor_scalar(small[:, 5:6], small[:, 5:6], 1e-8, None, ALU.add))
                step(nc.vector.reciprocal(small[:, 6:7], small[:, 5:6]))
                step(nc.vector.tensor_scalar(selg[:, :, :], selg[:, :, :], small[:, 6:7], None, ALU.mult))
                step(nc.vector.tensor_tensor(wsum[:, :], selg[:, 0, :], selg[:, 1, :], ALU.add))
                for k in range(2):
                    nc.vector.tensor_copy(rows[k * C:(k + 1) * C, 0, :], sel[k * C:(k + 1) * C, k, :])
                    last = nc.vector.tensor_copy(rows[k * C:(k + 1) * C, 1, :], selg[k * C:(k + 1) * C, k, :])
                step(last)
                wait(dve, up_psum, b * (2 * NC))
                wait(dve, hid_ready, b * NC)
                for e in range(E):
                    for k in range(2):
                        if e == 0:
                            ins = nc.vector.tensor_scalar(wd[:, :, k, :], dw[:, :, e, :], sel[:, k, e:e + 1], None, ALU.mult)
                        else:
                            ins = nc.vector.scalar_tensor_tensor(wd[:, :, k, :], dw[:, :, e, :], sel[:, k, e:e + 1],
                                                                 wd[:, :, k, :], ALU.mult, ALU.add)
                        step(ins)
                    if e == 0:
                        ins = nc.vector.tensor_scalar(wu[:, :], uw[:, e, :], rows[:, 1, e:e + 1], None, ALU.mult)
                    else:
                        ins = nc.vector.scalar_tensor_tensor(wu[:, :], uw[:, e, :], rows[:, 1, e:e + 1], wu[:, :],
                                                             ALU.mult, ALU.add)
                    step(ins)
                step(nc.vector.tensor_tensor(prod[:, :], rows[:, 0, :], db[:, :], ALU.mult))
                assert steps[0] == GATE_STEPS, steps
                nc.vector.tensor_reduce(bsel[:, :], prod[:, :], AX.X, ALU.add).then_inc(chosen, 1)
                wait(dve, wsum_psum, b + 1)
                nc.vector.tensor_copy(wsumT[:, :], bank[2][0:E, P:2 * P]).then_inc(chosen, 1)

                for m in range(NC):
                    wait(dve, stored[m % 2], b * (8 * NC) + 16 * (m // 2))
                    for r in range(2):
                        wait(dve, up_psum, b * (2 * NC) + 2 * m + r + 1)
                        nc.vector.tensor_tensor(h_new[m % 2][:, 2 * r:2 * r + 2, :],
                                                bank[5 + r][:, :].rearrange("p (j d) -> p j d", j=2),
                                                hb[m][:, 2 * r:2 * r + 2, :], ALU.add).then_inc(hnew_ready, 1)

            repeat(dve, batches, turn)

        @block.scalar
        def _(act):
            def turn(b):
                for m in range(NC):
                    for f in range(2):
                        wait(act, xT_psum, b * (2 * NC) + 2 * m + f + 1)
                        if m == 0:
                            wait(act, hid_psum, b * NC)
                            wait(act, pooled_ready, b)
                        nc.scalar.activation(xT[:, f, m * T:(m + 1) * T], bank[f][:, :], ACT.Copy,
                                             accum_out=sums[:, f, m:m + 1]).then_inc(xT_ready, 1)
                wait(act, gate_step, b * GATE_STEPS + 2)
                wait(act, wsum_psum, b)
                nc.scalar.activation(g8[:, :], bank[2][:, 0:E], ACT.Exp, bias=small[:, 0:1],
                                     accum_out=small[:, 1:2]).then_inc(gate_exp, 1)
                wait(act, chosen, b * 2 + 1)
                for m in range(NC):
                    wait(act, hid_psum, b * NC + m + 1)
                    wait(act, up_psum, b * (2 * NC) + 2 * max(m - 1, 0))
                    nc.scalar.activation(hid[m % 2][:, :], bank[3 + m % 2][:, :], ACT.Gelu,
                                         bias=bsel[:, :]).then_inc(hid_ready, 1)

            repeat(act, batches, turn)

        @block.tensor
        def _(pe):
            pe.wait_ge(loaded, 9 * 16)
            def turn(b):
                for m in range(NC):
                    wait(pe, xh_ready, b * NC + m + 1)
                    for f in range(2):
                        if m:
                            wait(pe, xT_ready, b * (2 * NC) + 2 * m + f - 1)
                        else:
                            wait(pe, xT_ready, b * (2 * NC))
                        for j in range(TJ):
                            last = nc.tensor.transpose(bank[f][:, j * P:(j + 1) * P],
                                                       xh[m % 2][:, j, f * P:(f + 1) * P], core.ident[:, :])
                        last.then_inc(xT_psum, 1)
                wait(pe, pooled_ready, b + 1)
                wait(pe, chosen, b * 2)
                for k in range(2):
                    last = nc.tensor.matmul(bank[2][:, 0:E], pooled_b[:, k, :], gw[:, k, :], start=(k == 0),
                                            stop=(k == 1))
                last.then_inc(gate_psum, 1)
                wait(pe, gate_step, b * GATE_STEPS + 16)
                nc.tensor.transpose(bank[2][0:E, P:2 * P], wsum[:, :], core.ident[:, :]).then_inc(wsum_psum, 1)
                wait(pe, chosen, b * 2 + 2)
                for m in range(NC + 1):
                    if m < NC:
                        wait(pe, hid_ready, b * NC + max(m - 1, 0))
                        for k in range(2):
                            last = nc.tensor.matmul(bank[3 + m % 2][:, :], wd[:, k, :, :].rearrange("p k c -> p (k c)"),
                                                    xT[:, k, m * T:(m + 1) * T], start=(k == 0), stop=(k == 1))
                        last.then_inc(hid_psum, 1)
                    if m == 0:
                        continue
                    u = m - 1
                    wait(pe, hid_ready, b * NC + u + 1)
                    for r in range(2):
                        wait(pe, hnew_ready, b * (2 * NC) + max(2 * u + r - 1, 0))
                        for j in range(2):
                            t0 = (2 * r + j) * P
                            nc.tensor.matmul(bank[5 + r][:, j * D:(j + 1) * D], hid[u % 2][:, t0:t0 + P], wu[:, :],
                                             start=True, stop=False)
                            last = nc.tensor.matmul(bank[5 + r][:, j * D:(j + 1) * D], wsumT[:, :], ub[:, :],
                                                    start=False, stop=True)
                        last.then_inc(up_psum, 1)

            repeat(pe, batches, turn)


def ssm_phase(core, w, h_in, h_out):
    nc, bank, chunks = core.nc, core.bank, core.chunks
    N = w["A_log"].shape[1]
    FB = w["ff1_w"].shape[1] // P
    R = 3 * 2 * N
    with ExitStack() as ctx:
        def sb(name, shape, dt=F32):
            return ctx.enter_context(nc.sbuf_tensor("s_" + name, shape, dt))

        def sem(name):
            return nc.alloc_semaphore(name="s_" + name)

        passed = sem("passed")

        mats = {name: sb(name, [P, 2, D]) for name in ("w1_w", "v1_w", "w2_w", "dt_w")}
        ff1 = sb("ff1", [P, 2, FB * P])
        ff2 = sb("ff2", [P, FB, D])
        bcw = sb("bcw", [P, 2, 3, 2 * N])
        bcb = sb("bcb", [R, 1])
        cols = {name: sb(name, [P, 2]) for name in ("ln_g", "ln_b", "w1_b", "v1_b", "dt_b", "D_p", "ln2_g", "ln2_b")}
        half_v1b = sb("half_v1b", [P, 2])
        conv = sb("conv", [P, 2, 3])
        half_conv = sb("half_conv", [P, 2, 3])
        ff1b = sb("ff1b", [P, FB])
        A_log = sb("A_log", [P, 2, N])
        A = sb("A", [P, 2, N])
        A_neg = sb("A_neg", [P, 2, N])
        g1 = sb("g1", [P, D])
        b1 = sb("b1", [P, D])
        w2b = sb("w2b", [P, D])
        ff2b = sb("ff2b", [P, D])
        moeb = sb("moeb", [P, D])
        endb = sb("endb", [P, D])
        pick = sb("pick", [R, 2 * N, P], BF16)

        hb = [sb(f"hb{q}", [P, TJ + 1, D]) for q in range(2)]
        bn = sb("bn", [P, TJ + 1, 6])
        mv = sb("mv", [P, TJ + 1, 2])
        rstd = sb("rstd", [P, TJ + 1])
        rstd_n = sb("rstd_n", [P, TJ + 1])
        xh = sb("xh", [P, TJ + 1, D])
        xn = sb("xn", [P, TJ + 1, D])
        xres = [sb(f"xres{q}", [P, TJ, D]) for q in range(2)]
        hres = [sb(f"hres{q}", [P, TJ, D]) for q in range(2)]
        xmT = sb("xmT", [P, 2, T + 1])
        x1 = sb("x1", [P, 2, T + 2])
        after = sb("after", [P, 2])
        cv = sb("cv", [P, 2, T])
        th = sb("th", [P, 2, T])
        xc = [sb(f"xc{q}", [P, 2, T]) for q in range(2)]
        xs = sb("xs", [P, 2, T])
        dt = [sb(f"dt{q}", [P, 2, T]) for q in range(2)]
        dtx = [sb(f"dtx{q}", [P, 2, T]) for q in range(2)]
        vg = [sb(f"vg{q}", [P, 2, T]) for q in range(2)]
        bcf = sb("bcf", [R, T])
        bcs = [sb(f"bcs{q}", [R, T], BF16) for q in range(2)]
        a = [sb(f"a{s}", [P, 2, T]) for s in range(2)]
        u = [sb(f"u{s}", [P, 2, T]) for s in range(2)]
        hs = [sb(f"hs{s}", [P, 2, T]) for s in range(2)]
        cb = [sb(f"cb{s}", [P, T]) for s in range(2)]
        zlast = sb("zlast", [P, N, 2])
        carry = sb("carry", [P, N, 2])
        yv = sb("yv", [P, 2, T])
        x2 = sb("x2", [P, TJ, D])
        bn2 = sb("bn2", [P, TJ, 6])
        mv2 = sb("mv2", [P, TJ, 2])
        rstd2 = sb("rstd2", [P, TJ])
        xn2 = sb("xn2", [P, TJ, D])
        xn2T = sb("xn2T", [P, 2, T])
        hid = sb("hid", [P, FB, T])
        h_new = sb("h_new", [P, TJ, D])

        bB, bC, yp, tp, mm = bank[0], bank[1], bank[2:4], bank[4:6], bank[6:8]

        loaded, pick_step, cleared, consts, A_done = (
            sem("loaded"), sem("pick_step"), sem("cleared"), sem("consts"), sem("A_done"))
        h_loaded = [sem(f"h_loaded{q}") for q in range(2)]
        bn_done, stats_ready, rstd_step, xh_ready, xn_ready, affine_ready, res_ready = (
            sem("bn_done"), sem("stats_ready"), sem("rstd_step"), sem("xh_ready"), sem("xn_ready"),
            sem("affine_ready"), sem("res_ready"))
        bnn_done, statsn_ready, xm_ready = sem("bnn_done"), sem("statsn_ready"), sem("xm_ready")
        xmT_psum, xmT_ready = sem("xmT_psum"), sem("xmT_ready")
        x1carry_ready, x1_psum, x1_ready, x1after_ready = (
            sem("x1carry_ready"), sem("x1_psum"), sem("x1_ready"), sem("x1after_ready"))
        conv_step, th_ready, xc_ready = sem("conv_step"), sem("th_ready"), sem("xc_ready")
        dt_psum, xs_ready, na_ready, ln1p_step, dt_ready, dtx_ready = (
            sem("dt_psum"), sem("xs_ready"), sem("na_ready"), sem("ln1p_step"), sem("dt_ready"), sem("dtx_ready"))
        bc_psum, bcf_ready, part_ready, rest_ready = sem("bc_psum"), sem("bcf_ready"), sem("part_ready"), sem("rest_ready")
        vg_psum, vb_ready, vth_ready, vg_ready = sem("vg_psum"), sem("vb_ready"), sem("vth_ready"), sem("vg_ready")
        B_psum, C_psum, u_ready, cb_ready, a_ready = (
            sem("B_psum"), sem("C_psum"), sem("u_ready"), sem("cb_ready"), sem("a_ready"))
        scan_done = [sem(f"scan_done{f}") for f in range(2)]
        zlast_saved, g_ready, red_done = sem("zlast_saved"), sem("g_ready"), sem("red_done")
        carry_ready = [sem(f"carry_ready{m}") for m in range(2)]
        y_ready, yv_ready, mo_psum, x2_ready = sem("y_ready"), sem("yv_ready"), sem("mo_psum"), sem("x2_ready")
        bn2_done, stats2_ready, rstd2_step, xn2_ready, x2res_ready = (
            sem("bn2_done"), sem("stats2_ready"), sem("rstd2_step"), sem("xn2_ready"), sem("x2res_ready"))
        xn2T_psum, xn2T_ready, ff1_psum, hid_ready, ff2_psum, hnew_ready, h_stored = (
            sem("xn2T_psum"), sem("xn2T_ready"), sem("ff1_psum"), sem("hid_ready"), sem("ff2_psum"),
            sem("hnew_ready"), sem("h_stored"))
        block = ctx.enter_context(nc.Block())
        hin, hout = chunk_view(h_in), chunk_view(h_out)
        CONST = 3

        loads = []
        for name in ("w1_w", "v1_w", "w2_w", "dt_w"):
            loads.append((mats[name][:, :, :], w[name].rearrange("(k p) n -> p k n", p=P)))
        loads.append((ff1[:, :, :], w["ff1_w"].rearrange("(k p) n -> p k n", p=P)))
        loads.append((ff2[:, :, :], w["ff2_w"].rearrange("(k p) n -> p k n", p=P)))
        for part in range(3):
            for m, name in enumerate(("Bp", "Cp")):
                loads.append((bcw[:, :, part, m * N:(m + 1) * N], w[name + "_w"].rearrange("(k p) n -> p k n", p=P)))
                r0 = (2 * part + m) * N
                loads.append((bcb[r0:r0 + N, :], w[name + "_b"]))
        for name in cols:
            loads.append((cols[name][:, :], w[name]))
        loads.append((conv[:, :, :], w["conv_w"].rearrange("(k p) o x -> p k (o x)", p=P)))
        loads.append((ff1b[:, :], w["ff1_b"]))
        loads.append((A_log[:, :, :], w["A_log"].rearrange("(k p) n -> p k n", p=P)))
        for tile, name in ((g1, "ln1_g"), (b1, "ln1_b"), (w2b, "w2_b"), (ff2b, "ff2_b"), (moeb, "moe_bias")):
            loads.append((tile[:, :], w[name].partition_broadcast(P)))
        LOADED = 16 * len(loads)

        @block.sync
        def _(sp):
            for dst, src in loads:
                sp.dma_start(dst, src).then_inc(loaded, 16)

            def load(fc, fq):
                wait(sp, res_ready, fc - 1)
                wait(sp, xh_ready, fc - 1)
                sp.dma_start(hb[fq][:, 0:TJ, :], one(hin, fc)).then_inc(h_loaded[fq], 16)
                nxt = one(hin, (fc + 1) % chunks)
                sp.dma_start(hb[fq][0:1, TJ, :], nxt[0:1, 0, :]).then_inc(h_loaded[fq], 16)

            def store(c):
                sp.wait_ge(hnew_ready, c * 2 + 2)
                sp.dma_start(one(hout, c), h_new[:, :, :]).then_inc(h_stored, 16)

            def body(c, q, first, last):
                if not last:
                    load(c + 1, 1 - q)
                if not first:
                    store(c - 1)

            sweep(sp, chunks, load, body)
            store(chunks - 1)
            sp.wait_ge(h_stored, 16 * chunks)

        @block.gpsimd
        def _(pool):
            nc.gpsimd.memset(pick[:, :, :], 0.0).then_inc(pick_step, 1)
            for part in range(3):
                pool.wait_ge(pick_step, part + 1)
                nc.gpsimd.affine_select(out=pick[:, :, :], in_=pick[:, :, :], compare_op=ALU.not_equal, fill=1.0,
                                        base=-2 * N * part, pattern=[[-1, 2 * N], [0, P]],
                                        channel_multiplier=1).then_inc(pick_step, 1)
            pool.wait_ge(pick_step, 4)
            nc.gpsimd.memset(mv[:, :, :], 1.0).then_inc(cleared, 1)
            nc.gpsimd.memset(x1[:, :, :], 0.0).then_inc(cleared, 1)
            nc.gpsimd.memset(zlast[:, :, :], 0.0).then_inc(cleared, 1)
            pool.wait_ge(cleared, 3)
            pool.wait_ge(loaded, LOADED)
            nc.gpsimd.tensor_tensor(endb[:, :], ff2b[:, :], moeb[:, :], ALU.add).then_inc(consts, 1)
            nc.gpsimd.tensor_scalar(half_v1b[:, :], cols["v1_b"][:, :], 0.5, None, ALU.mult).then_inc(consts, 1)
            nc.gpsimd.tensor_scalar(half_conv[:, :, :], conv[:, :, :], 0.5, None, ALU.mult).then_inc(consts, 1)
            pool.wait_ge(consts, 3)

            def front(fc, fq, k=None):
                if k in (None, 0):
                    pool.wait_ge(stats_ready, fc + 1)
                    wait(pool, xn_ready, fc)
                    wait(pool, xm_ready, fc)
                    base = fc * 8
                    seq = [
                        lambda: nc.gpsimd.tensor_tensor(rstd[:, :], mv[:, :, 1], core.eps[:, 0:mv.shape[1]], ALU.add),
                        lambda: nc.gpsimd.tensor_tensor(rstd[:, :], rstd[:, :], core.neg_half[:, 0:TJ + 1], ALU.pow),
                        lambda: nc.gpsimd.tensor_tensor(rstd_n[:, :], mv[:, :, 1], rstd[:, :], ALU.mult),
                        lambda: nc.gpsimd.tensor_tensor(rstd_n[:, :], rstd_n[:, :], rstd[:, :], ALU.mult),
                        lambda: nc.gpsimd.tensor_tensor(rstd_n[:, :], rstd_n[:, :], core.eps[:, 0:TJ + 1], ALU.add),
                        lambda: nc.gpsimd.tensor_tensor(rstd_n[:, :], rstd_n[:, :], core.neg_half[:, 0:TJ + 1], ALU.pow),
                    ]
                    for m, op in enumerate(seq):
                        op().then_inc(rstd_step, 1)
                        if m + 1 < len(seq):
                            pool.wait_ge(rstd_step, base + m + 1)
                if k in (None, 1):
                    pool.wait_ge(xn_ready, fc + 1)
                    nc.gpsimd.tensor_tensor(xn[:, 0:TJ, :], xn[:, 0:TJ, :],
                                            b1[:, :].unsqueeze(1).to_broadcast([P, TJ, D]), ALU.add)
                    nc.gpsimd.tensor_tensor(xn[0:1, TJ, :], xn[0:1, TJ, :], b1[0:1, :], ALU.add).then_inc(affine_ready, 1)
                if k in (None, 5):
                    wait(pool, x2_ready, (fc - 1) * 2)
                    wait(pool, x2res_ready, fc - 1)
                    nc.gpsimd.tensor_tensor(xres[fq][:, :, :], xh[:, 0:TJ, :],
                                            w2b[:, :].unsqueeze(1).to_broadcast([P, TJ, D]), ALU.add)
                    nc.gpsimd.tensor_tensor(hres[fq][:, :, :], hb[fq][:, 0:TJ, :],
                                            endb[:, :].unsqueeze(1).to_broadcast([P, TJ, D]), ALU.add).then_inc(res_ready, 1)
                if k in (None, 2):
                    pool.wait_ge(statsn_ready, fc + 1)
                    nc.gpsimd.tensor_tensor(rstd_n[:, :], mv[:, :, 1], core.eps[:, 0:mv.shape[1]], ALU.add).then_inc(rstd_step, 1)
                    pool.wait_ge(rstd_step, fc * 8 + 7)
                    nc.gpsimd.tensor_tensor(rstd_n[:, :], rstd_n[:, :], core.neg_half[:, 0:TJ + 1],
                                            ALU.pow).then_inc(rstd_step, 1)

            def fin(c, q, k):
                if k == 3:
                    pool.wait_ge(stats2_ready, c + 1)
                    wait(pool, xn2_ready, c)
                    nc.gpsimd.tensor_tensor(rstd2[:, :], mv2[:, :, 1], core.eps[:, 0:mv2.shape[1]], ALU.add).then_inc(rstd2_step, 1)
                    pool.wait_ge(rstd2_step, c * 2 + 1)
                    nc.gpsimd.tensor_tensor(rstd2[:, :], rstd2[:, :], core.neg_half[:, 0:TJ],
                                            ALU.pow).then_inc(rstd2_step, 1)
                if k == 4:
                    pool.wait_ge(xn2_ready, c + 1)
                    pool.wait_ge(res_ready, c + 1)
                    nc.gpsimd.tensor_tensor(x2[:, :, :], x2[:, :, :], hres[q][:, :, :], ALU.add).then_inc(x2res_ready, 1)

            def body(c, q, first, last):
                for n in range(N):
                    for f in range(2):
                        pool.wait_ge(scan_done[f], c * N + n + 1)
                    pool.wait_ge(zlast_saved, c * N + n + 1)
                    pool.wait_ge(cb_ready, c * N + n + 1)
                    nc.gpsimd.tensor_tensor(hs[n % 2][:, :, :], hs[n % 2][:, :, :],
                                            cb[n % 2][:, :].unsqueeze(1).to_broadcast([P, 2, T]),
                                            ALU.mult).then_inc(g_ready, 1)
                    if not first:
                        fin(c - 1, 1 - q, n)
                    if not last:
                        front(c + 1, 1 - q, n)

            sweep(pool, chunks, front, body)
            for k in range(N):
                fin(chunks - 1, 1, k)

        @block.vector
        def _(dve):
            dve.wait_ge(loaded, LOADED)
            dve.wait_ge(consts, CONST)
            dve.wait_ge(A_done, 1)
            nc.vector.tensor_scalar(A_neg[:, :, :], A[:, :, :], -1.0, None, ALU.mult).then_inc(A_done, 1)

            def tiles(t, j):
                return t[:, j, :] if j < TJ else t[0:1, j, :]

            def front(fc, fq, k=None):
                if k in (None, 0):
                    dve.wait_ge(h_loaded[fq], (fc - fq) * 16 + 32)
                    wait(dve, statsn_ready, fc)
                    for j in range(TJ + 1):
                        last = nc.vector.bn_stats(tiles(bn, j), tiles(hb[fq], j))
                    last.then_inc(bn_done, 1)
                    dve.wait_ge(bn_done, fc + 1)
                    wait(dve, rstd_step, fc * 8)
                    hold(dve, passed)
                    for j in range(TJ + 1):
                        last = nc.vector.bn_aggr(tiles(mv, j), tiles(bn, j))
                    last.then_inc(stats_ready, 1)
                if k in (None, 1):
                    dve.wait_ge(stats_ready, fc + 1)
                    dve.wait_ge(rstd_step, fc * 8 + 6)
                    wait(dve, res_ready, fc)
                    wait(dve, xmT_psum, fc * 3)
                    for j in range(TJ + 1):
                        one_row = slice(0, P if j < TJ else 1)
                        last = nc.vector.tensor_scalar(tiles(xh, j), tiles(hb[fq], j), mv[one_row, j, 0:1],
                                                       rstd[one_row, j:j + 1], ALU.subtract, ALU.mult)
                    last.then_inc(xh_ready, 1)
                    dve.wait_ge(xh_ready, fc + 1)
                    for j in range(TJ + 1):
                        one_row = slice(0, P if j < TJ else 1)
                        last = nc.vector.scalar_tensor_tensor(tiles(xn, j), tiles(xh, j), rstd_n[one_row, j:j + 1],
                                                              g1[one_row, :], ALU.mult, ALU.mult)
                    last.then_inc(xn_ready, 1)
                if k in (None, 2):
                    dve.wait_ge(affine_ready, fc + 1)
                    for j in range(TJ + 1):
                        last = nc.vector.bn_stats(tiles(bn, j), tiles(xn, j))
                    last.then_inc(bnn_done, 1)
                    dve.wait_ge(bnn_done, fc + 1)
                    hold(dve, passed)
                    for j in range(TJ + 1):
                        last = nc.vector.bn_aggr(tiles(mv, j), tiles(bn, j))
                    last.then_inc(statsn_ready, 1)
                if k in (None, 3):
                    dve.wait_ge(statsn_ready, fc + 1)
                    dve.wait_ge(rstd_step, fc * 8 + 8)
                    for j in range(TJ + 1):
                        one_row = slice(0, P if j < TJ else 1)
                        last = nc.vector.tensor_scalar(tiles(xn, j), tiles(xn, j), mv[one_row, j, 0:1],
                                                       rstd_n[one_row, j:j + 1], ALU.subtract, ALU.mult)
                    last.then_inc(xm_ready, 1)
                if k in (None, 5):
                    wait(dve, x1_ready, fc * 3)
                    wait(dve, conv_step, fc * 3)
                    nc.vector.tensor_scalar(x1[:, :, 0:1], x1[:, :, T:T + 1], core.keep[:, bass.ds(fc, 1)], None,
                                            ALU.mult).then_inc(x1carry_ready, 1)
                if k in (None, 6):
                    dve.wait_ge(x1_ready, fc * 3 + 3)
                    dve.wait_ge(x1carry_ready, fc + 1)
                    nc.vector.tensor_scalar(x1[:, :, T + 1:T + 2], after[:, :].unsqueeze(2),
                                            core.keep[:, bass.ds(fc + 1, 1)], None, ALU.mult).then_inc(x1after_ready, 1)
                    dve.wait_ge(x1after_ready, fc + 1)
                    wait(dve, xc_ready, fc)
                    for f in range(2):
                        last = nc.vector.tensor_scalar(cv[:, f, :], x1[:, f, 0:T], half_conv[:, f, 0:1], None, ALU.mult)
                    last.then_inc(conv_step, 1)
                    for m in range(1, 3):
                        dve.wait_ge(conv_step, fc * 3 + m)
                        for f in range(2):
                            last = nc.vector.scalar_tensor_tensor(cv[:, f, :], x1[:, f, m:m + T], half_conv[:, f, m:m + 1],
                                                                  cv[:, f, :], ALU.mult, ALU.add)
                        last.then_inc(conv_step, 1)
                if k in (None, 8):
                    dve.wait_ge(th_ready, fc + 1)
                    wait(dve, y_ready, fc - 1)
                    nc.vector.scalar_tensor_tensor(xc[fq][:, :, :], th[:, :, :], 1.0, cv[:, :, :], ALU.add,
                                                   ALU.mult).then_inc(xc_ready, 1)
                if k in (None, 10):
                    dve.wait_ge(xs_ready, fc * 2 + 2)
                    wait(dve, dt_ready, fc)
                    dve.wait_ge(xc_ready, fc + 1)
                    nc.vector.scalar_tensor_tensor(cv[:, :, :], xs[:, :, :], -1.0, xs[:, :, :], ALU.mult,
                                                   ALU.min).then_inc(na_ready, 1)
                if k in (None, 11):
                    dve.wait_ge(ln1p_step, fc * 2 + 2)
                    wait(dve, a_ready, (fc - 1) * N)
                    nc.vector.scalar_tensor_tensor(dt[fq][:, :, :], xs[:, :, :], 0.0, cv[:, :, :], ALU.max,
                                                   ALU.add).then_inc(dt_ready, 1)
                    dve.wait_ge(dt_ready, fc + 1)
                    nc.vector.tensor_tensor(dtx[fq][:, :, :], dt[fq][:, :, :], xc[fq][:, :, :],
                                            ALU.mult).then_inc(dtx_ready, 1)
                if k in (None, 12):
                    dve.wait_ge(part_ready, fc * 3 + 1)
                    lo = 2 * N
                    nc.vector.tensor_tensor(bcf[lo:2 * lo, :], bcf[lo:2 * lo, :], bcs[fq][lo:2 * lo, :], ALU.subtract)
                    nc.vector.tensor_tensor(bcf[2 * lo:R, :], bcf[2 * lo:R, :], bcs[fq][2 * lo:R, :],
                                            ALU.subtract).then_inc(rest_ready, 1)
                if k in (None, 13):
                    dve.wait_ge(vth_ready, fc + 1)
                    wait(dve, yv_ready, fc - 1)
                    nc.vector.scalar_tensor_tensor(vg[fq][:, :, :], th[:, :, :], 1.0, cv[:, :, :], ALU.add,
                                                   ALU.mult).then_inc(vg_ready, 1)
                if k in (None, 14):
                    dve.wait_ge(part_ready, fc * 3 + 2)
                    lo = 4 * N
                    nc.vector.tensor_tensor(bcf[lo:R, :], bcf[lo:R, :], bcs[fq][lo:R, :],
                                            ALU.subtract).then_inc(rest_ready, 1)

            def fin(c, q, k):
                if k == 1:
                    dve.wait_ge(red_done, (c + 1) * N)
                    wait(dve, mo_psum, c * 2)
                    for f in range(2):
                        ins = nc.vector.scalar_tensor_tensor(yv[:, f, :], xc[q][:, f, :], cols["D_p"][:, f:f + 1],
                                                             yp[f][:, :], ALU.mult, ALU.add)
                    ins.then_inc(y_ready, 1)
                    dve.wait_ge(y_ready, c + 1)
                    nc.vector.tensor_tensor(yv[:, :, :], yv[:, :, :], vg[q][:, :, :], ALU.mult).then_inc(yv_ready, 1)
                if k == 3:
                    wait(dve, hnew_ready, c * 2)
                    dve.wait_ge(res_ready, c + 1)
                    for m in range(2):
                        dve.wait_ge(mo_psum, c * 2 + m + 1)
                        nc.vector.tensor_tensor(x2[:, 2 * m:2 * m + 2, :], mm[m][:, :].rearrange("p (j d) -> p j d", j=2),
                                                xres[q][:, 2 * m:2 * m + 2, :], ALU.add).then_inc(x2_ready, 1)
                    dve.wait_ge(x2_ready, c * 2 + 2)
                    for j in range(TJ):
                        ins = nc.vector.bn_stats(bn2[:, j, :], x2[:, j, :])
                    ins.then_inc(bn2_done, 1)
                    dve.wait_ge(bn2_done, c + 1)
                    wait(dve, rstd2_step, c * 2)
                    hold(dve, passed)
                    for j in range(TJ):
                        ins = nc.vector.bn_aggr(mv2[:, j, :], bn2[:, j, :])
                    ins.then_inc(stats2_ready, 1)
                if k == 4:
                    dve.wait_ge(stats2_ready, c + 1)
                    dve.wait_ge(rstd2_step, c * 2 + 2)
                    wait(dve, xn2T_psum, c * 2)
                    for j in range(TJ):
                        ins = nc.vector.tensor_scalar(xn2[:, j, :], x2[:, j, :], mv2[:, j, 0:1], rstd2[:, j:j + 1],
                                                      ALU.subtract, ALU.mult)
                    ins.then_inc(xn2_ready, 1)
                if k == 11:
                    wait(dve, h_stored, c * 16)
                    dve.wait_ge(x2res_ready, c + 1)
                    for m in range(2):
                        dve.wait_ge(ff2_psum, c * 2 + m + 1)
                        nc.vector.tensor_tensor(h_new[:, 2 * m:2 * m + 2, :],
                                                tp[m][:, :].rearrange("p (j d) -> p j d", j=2),
                                                x2[:, 2 * m:2 * m + 2, :], ALU.add).then_inc(hnew_ready, 1)

            def carry_half(c, m):
                wait(dve, zlast_saved, (c - 1) * N + N // 2 if m == 0 else c * N)
                nc.vector.tensor_scalar(carry[:, m * 8:(m + 1) * 8, :], zlast[:, m * 8:(m + 1) * 8, :],
                                        core.keep[:, bass.ds(c, 1)], None, ALU.mult).then_inc(carry_ready[m], 1)

            def body(c, q, first, last):
                for n in range(N):
                    s = n % 2
                    if n in (0, 8):
                        dve.wait_ge(carry_ready[n // 8], c + 1)
                    if n == 0:
                        dve.wait_ge(dtx_ready, c + 1)
                    dve.wait_ge(B_psum, c * N + n + 1)
                    wait(dve, scan_done[1], c * N + n - 1)
                    nc.vector.tensor_tensor(u[s][:, :, :], dtx[q][:, :, :], bB[:, :].unsqueeze(1).to_broadcast([P, 2, T]),
                                            ALU.mult).then_inc(u_ready, 1)
                    dve.wait_ge(u_ready, c * N + n + 1)
                    wait(dve, red_done, c * N + n - 1)
                    dve.wait_ge(a_ready, c * N + n + 1)
                    for f in range(2):
                        nc.vector.tensor_tensor_scan(hs[s][:, f, :], a[s][:, f, :], u[s][:, f, :], carry[:, n, f:f + 1],
                                                     ALU.mult, ALU.add).then_inc(scan_done[f], 1)
                    if not first:
                        fin(c - 1, 1 - q, n)
                    if n == 4:
                        carry_half(c, 1)
                    if not last:
                        front(c + 1, 1 - q, n)
                        if n == 12:
                            carry_half(c + 1, 0)

            def front0(fc, fq):
                front(fc, fq)
                carry_half(0, 0)

            sweep(dve, chunks, front0, body)
            for k in range(N):
                fin(chunks - 1, 1, k)

        @block.scalar
        def _(act):
            act.wait_ge(loaded, LOADED)
            act.wait_ge(consts, CONST)
            nc.scalar.activation(A[:, :, :], A_log[:, :, :], ACT.Exp).then_inc(A_done, 1)
            act.wait_ge(A_done, 2)

            def front(fc, fq, k=None):
                if k in (None, 4):
                    wait(act, vg_psum, fc * 2)
                    for f in range(2):
                        act.wait_ge(xmT_psum, fc * 3 + f + 1)
                        nc.scalar.activation(xmT[:, f, 0:T], tp[f][:, :], ACT.Identity, bias=cols["ln_b"][:, f:f + 1],
                                             scale=cols["ln_g"][:, f:f + 1]).then_inc(xmT_ready, 1)
                    act.wait_ge(xmT_psum, fc * 3 + 3)
                    for f in range(2):
                        last = nc.scalar.activation(xmT[:, f, T:T + 1], mm[0][:, f:f + 1], ACT.Identity,
                                                    bias=cols["ln_b"][:, f:f + 1], scale=cols["ln_g"][:, f:f + 1])
                    last.then_inc(xmT_ready, 1)
                if k in (None, 5):
                    act.wait_ge(x1carry_ready, fc + 1)
                    wait(act, conv_step, fc * 3)
                    wait(act, x1after_ready, fc)
                    for f in range(2):
                        act.wait_ge(x1_psum, fc * 3 + f + 1)
                        nc.scalar.activation(x1[:, f, 1:T + 1], mm[f][:, :], ACT.Identity,
                                             bias=cols["w1_b"][:, f:f + 1]).then_inc(x1_ready, 1)
                    act.wait_ge(x1_psum, fc * 3 + 3)
                    for f in range(2):
                        last = nc.scalar.activation(after[:, f:f + 1], tp[0][:, f:f + 1], ACT.Identity,
                                                    bias=cols["w1_b"][:, f:f + 1])
                    last.then_inc(x1_ready, 1)
                if k in (None, 7):
                    act.wait_ge(conv_step, fc * 3 + 3)
                    wait(act, vg_ready, fc)
                    nc.scalar.activation(th[:, :, :], cv[:, :, :], ACT.Tanh).then_inc(th_ready, 1)
                if k in (None, 9):
                    wait(act, dt_ready, fc)
                    for f in range(2):
                        act.wait_ge(dt_psum, fc * 2 + f + 1)
                        nc.scalar.activation(xs[:, f, :], mm[f][:, :], ACT.Identity,
                                             bias=cols["dt_b"][:, f:f + 1]).then_inc(xs_ready, 1)
                if k in (None, 10):
                    act.wait_ge(bc_psum, fc + 1)
                    wait(act, part_ready, fc * 3)
                    nc.scalar.activation(bcf[:, :], mm[0][0:R, :], ACT.Identity, bias=bcb[:, :]).then_inc(bcf_ready, 1)
                    act.wait_ge(na_ready, fc + 1)
                    nc.scalar.activation(cv[:, :, :], cv[:, :, :], ACT.Exp).then_inc(ln1p_step, 1)
                    act.wait_ge(ln1p_step, fc * 2 + 1)
                    nc.scalar.activation(cv[:, :, :], cv[:, :, :], ACT.Ln, bias=core.ones[:, 0:1]).then_inc(ln1p_step, 1)
                if k in (None, 11):
                    act.wait_ge(bcf_ready, fc + 1)
                    wait(act, C_psum, (fc - 1) * N)
                    nc.scalar.copy(bcs[fq][:, :], bcf[:, :]).then_inc(part_ready, 1)
                if k in (None, 12):
                    act.wait_ge(dt_ready, fc + 1)
                    act.wait_ge(xc_ready, fc + 1)
                    for f in range(2):
                        act.wait_ge(vg_psum, fc * 2 + f + 1)
                        last = nc.scalar.activation(cv[:, f, :], mm[f][:, :], ACT.Identity, bias=half_v1b[:, f:f + 1],
                                                    scale=0.5)
                        last.then_inc(vb_ready, 1)
                    act.wait_ge(vb_ready, fc * 2 + 2)
                    nc.scalar.activation(th[:, :, :], cv[:, :, :], ACT.Tanh).then_inc(vth_ready, 1)
                if k in (None, 13):
                    act.wait_ge(rest_ready, fc * 2 + 1)
                    lo = 2 * N
                    nc.scalar.copy(bcs[fq][lo:2 * lo, :], bcf[lo:2 * lo, :])
                    nc.scalar.copy(bcs[fq][2 * lo:R, :], bcf[2 * lo:R, :]).then_inc(part_ready, 1)
                if k in (None, 15):
                    act.wait_ge(rest_ready, fc * 2 + 2)
                    lo = 4 * N
                    nc.scalar.copy(bcs[fq][lo:R, :], bcf[lo:R, :]).then_inc(part_ready, 1)

            def fin(c, q, k):
                if k == 5:
                    wait(act, ff1_psum, c * FB)
                    for f in range(2):
                        act.wait_ge(xn2T_psum, c * 2 + f + 1)
                        nc.scalar.activation(xn2T[:, f, :], tp[f][:, :], ACT.Identity, bias=cols["ln2_b"][:, f:f + 1],
                                             scale=cols["ln2_g"][:, f:f + 1]).then_inc(xn2T_ready, 1)
                if k == 8:
                    wait(act, ff2_psum, c * 2)
                    for m in range(FB):
                        act.wait_ge(ff1_psum, c * FB + m + 1)
                        nc.scalar.activation(hid[:, m, :], bank[6 - m % 4 // 2 * 2 + m % 2][:, :], ACT.Gelu,
                                             bias=ff1b[:, m:m + 1]).then_inc(hid_ready, 1)

            def decay(c, q, n):
                if n == 0:
                    act.wait_ge(dt_ready, c + 1)
                for f in range(2):
                    wait(act, scan_done[f], c * N + n - 1)
                wait(act, g_ready, c * N + n - 1)
                for f in range(2):
                    last = nc.scalar.activation(a[n % 2][:, f, :], dt[q][:, f, :], ACT.Exp, scale=A_neg[:, f, n:n + 1])
                last.then_inc(a_ready, 1)
                act.wait_ge(C_psum, c * N + n + 1)
                nc.scalar.copy(cb[n % 2][:, :], bC[:, :]).then_inc(cb_ready, 1)

            def body(c, q, first, last):
                for n in range(N):
                    if n + 1 < N:
                        decay(c, q, n + 1)
                    for f in range(2):
                        act.wait_ge(scan_done[f], c * N + n + 1)
                    if n in (0, 8):
                        act.wait_ge(carry_ready[n // 8], c + 1)
                    nc.scalar.copy(zlast[:, n, :], hs[n % 2][:, :, T - 1]).then_inc(zlast_saved, 1)
                    if not last:
                        front(c + 1, 1 - q, n)
                    if not first:
                        fin(c - 1, 1 - q, n)
                    if n + 1 == N and not last:
                        decay(c + 1, 1 - q, 0)

            def front0(fc, fq):
                front(fc, fq)
                decay(0, 0, 0)

            sweep(act, chunks, front0, body)
            for k in range(N):
                fin(chunks - 1, 1, k)

        @block.tensor
        def _(pe):
            pe.wait_ge(loaded, LOADED)
            pe.wait_ge(consts, CONST)

            def widen(name, out, rhs, f):
                for kk in range(2):
                    last = nc.tensor.matmul(out, mats[name][:, kk, f * P:(f + 1) * P], rhs(kk), start=(kk == 0),
                                            stop=(kk == 1))
                return last

            def front(fc, fq, k=None):
                if k in (None, 4):
                    pe.wait_ge(xm_ready, fc + 1)
                    wait(pe, hnew_ready, (fc - 2) * 2)
                    wait(pe, x1_ready, fc * 3)
                    wait(pe, x2_ready, (fc - 1) * 2)
                    wait(pe, vb_ready, fc * 2)
                    for f in range(2):
                        for j in range(TJ):
                            last = nc.tensor.transpose(tp[f][:, j * P:(j + 1) * P], xn[:, j, f * P:(f + 1) * P],
                                                       core.ident[:, :])
                        last.then_inc(xmT_psum, 1)
                    for f in range(2):
                        last = nc.tensor.transpose(mm[0][:, f:f + 1], xn[0:1, TJ, f * P:(f + 1) * P],
                                                   core.ident[0:1, 0:1])
                    last.then_inc(xmT_psum, 1)
                if k in (None, 5):
                    pe.wait_ge(xmT_ready, fc * 3 + 3)
                    for f in range(2):
                        widen("w1_w", mm[f][:, :], lambda kk: xmT[:, kk, 0:T], f).then_inc(x1_psum, 1)
                    for f in range(2):
                        last = widen("w1_w", tp[0][:, f:f + 1], lambda kk: xmT[:, kk, T:T + 1], f)
                    last.then_inc(x1_psum, 1)
                if k in (None, 9):
                    pe.wait_ge(xc_ready, fc + 1)
                    pe.wait_ge(x1_ready, fc * 3 + 3)
                    wait(pe, hid_ready, (fc - 1) * FB)
                    for f in range(2):
                        widen("dt_w", mm[f][:, :], lambda kk: xc[fq][:, kk, :], f).then_inc(dt_psum, 1)
                if k in (None, 10):
                    pe.wait_ge(xs_ready, fc * 2 + 1)
                    for kk in range(2):
                        last = nc.tensor.matmul(mm[0][0:R, :], bcw[:, kk, :, :].rearrange("p a n -> p (a n)"),
                                                xc[fq][:, kk, :], start=(kk == 0), stop=(kk == 1))
                    last.then_inc(bc_psum, 1)
                if k in (None, 11):
                    pe.wait_ge(xs_ready, fc * 2 + 2)
                    pe.wait_ge(bcf_ready, fc + 1)
                    for f in range(2):
                        widen("v1_w", mm[f][:, :], lambda kk: xmT[:, kk, 0:T], f).then_inc(vg_psum, 1)

            def fin(c, q, k, fronts):
                if k == 2:
                    pe.wait_ge(yv_ready, c + 1)
                    pe.wait_ge(vb_ready, min(c + 2, chunks) * 2 if isinstance(c, int) else c * 2 + 4)
                    for m in range(2):
                        for j in range(2):
                            t0 = (2 * m + j) * P
                            for f in range(2):
                                last = nc.tensor.matmul(mm[m][:, j * D:(j + 1) * D], yv[:, f, t0:t0 + P],
                                                        mats["w2_w"][:, f, :], start=(f == 0), stop=(f == 1))
                        last.then_inc(mo_psum, 1)
                if k == 5:
                    pe.wait_ge(xn2_ready, c + 1)
                    pe.wait_ge(x1_ready, fronts * 3)
                    wait(pe, hnew_ready, c * 2)
                    for f in range(2):
                        for j in range(TJ):
                            last = nc.tensor.transpose(tp[f][:, j * P:(j + 1) * P], xn2[:, j, f * P:(f + 1) * P],
                                                       core.ident[:, :])
                        last.then_inc(xn2T_psum, 1)
                if k in (6, 7, 8):
                    pe.wait_ge(xn2T_ready, c * 2 + 2)
                    pe.wait_ge(x2_ready, c * 2 + 2)
                    for m in range(2 * (k - 6), 2 * (k - 6) + 2):
                        wait(pe, hid_ready, c * FB + max(m - 3, 0))
                        for kk in range(2):
                            last = nc.tensor.matmul(bank[6 - m % 4 // 2 * 2 + m % 2][:, :], ff1[:, kk, m * P:(m + 1) * P], xn2T[:, kk, :],
                                                    start=(kk == 0), stop=(kk == 1))
                        last.then_inc(ff1_psum, 1)
                if k in (9, 10):
                    m = k - 9
                    pe.wait_ge(hid_ready, c * FB + FB)
                    for j in range(2):
                        t0 = (2 * m + j) * P
                        for g in range(FB):
                            last = nc.tensor.matmul(tp[m][:, j * D:(j + 1) * D], hid[:, g, t0:t0 + P], ff2[:, g, :],
                                                    start=(g == 0), stop=(g == FB - 1))
                    last.then_inc(ff2_psum, 1)

            def spread(c, q, n):
                if n == 0:
                    pe.wait_ge(part_ready, c * 3 + 3)
                wait(pe, u_ready, c * N + n)
                nc.tensor.matmul(bB[:, :], pick[:, n, :], bcs[q][:, :], start=True, stop=True).then_inc(B_psum, 1)
                wait(pe, cb_ready, c * N + n)
                nc.tensor.matmul(bC[:, :], pick[:, N + n, :], bcs[q][:, :], start=True, stop=True).then_inc(C_psum, 1)

            def reduce(c, n):
                if n == 0:
                    wait(pe, y_ready, c)
                pe.wait_ge(g_ready, c * N + n + 1)
                for f in range(2):
                    last = nc.tensor.matmul(yp[f][:, :], core.ident[:, :], hs[n % 2][:, f, :], start=(n == 0),
                                            stop=(n == N - 1))
                last.then_inc(red_done, 1)

            def body(c, q, first, last):
                fronts = c + 1 if last else c + 2
                for n in range(N):
                    if n + 1 < N:
                        spread(c, q, n + 1)
                    elif not last:
                        front(c + 1, 1 - q, n)
                        spread(c + 1, 1 - q, 0)
                    if n > 0:
                        reduce(c, n - 1)
                    elif not first:
                        reduce(c - 1, N - 1)
                    if not last and n + 1 < N:
                        front(c + 1, 1 - q, n)
                    if not first:
                        fin(c - 1, 1 - q, n, fronts)

            def front0(fc, fq):
                front(fc, fq)
                spread(0, 0, 0)

            sweep(pe, chunks, front0, body)
            reduce(chunks - 1, N - 1)
            for k in range(N):
                fin(chunks - 1, 1, k, chunks)


def moe_phase(core, bias, weights, indices, w1, w2, h_io, h_out):
    nc, bank = core.nc, core.bank
    tokens, K = weights.shape
    E, _, FF = w1.shape
    NT = tokens // P
    NB = tokens // T
    FB = FF // P
    with ExitStack() as ctx:
        def sb(name, shape, dt=F32):
            return ctx.enter_context(nc.sbuf_tensor("m_" + name, shape, dt))

        def sem(name):
            return nc.alloc_semaphore(name="m_" + name)

        passed = sem("passed")

        acc = sb("acc", [P, NT, D])
        bias_b = sb("bias_b", [P, D])
        x = sb("x", [P, NT, D])
        bn = sb("bn", [P, NT, 6])
        mv = sb("mv", [P, NT, 2])
        rstd = sb("rstd", [P, NT])
        xT = sb("xT", [P, 2, tokens])
        wk = sb("wk", [P, NT, K])
        ik = sb("ik", [P, NT, K], I32)
        ikf = sb("ikf", [P, NT, K])
        e_i = sb("e_i", [P, E], I32)
        e_f = sb("e_f", [P, E])
        eq = sb("eq", [P, NT, E])
        cw = sb("cw", [P, NT, E])
        w1s = [sb(f"w1s{s}", [P, 2, FF]) for s in range(2)]
        w2s = [sb(f"w2s{s}", [P, FB, D]) for s in range(2)]
        hid = [sb(f"hid{s}", [P, FB, T]) for s in range(2)]
        cwe = sb("cwe", [P, NT])

        loaded, step_done, iota_done, rstd_step, x_ready, xT_psum, xT_ready, cw_ready = (
            sem("loaded"), sem("step_done"), sem("iota_done"), sem("rstd_step"), sem("x_ready"), sem("xT_psum"),
            sem("xT_ready"), sem("cw_ready"))
        w_loaded = [sem(f"w_loaded{s}") for s in range(2)]
        ff1_psum, hid_ready, ff2_psum, acc_step, cwe_ready, stored = (
            sem("ff1_psum"), sem("hid_ready"), sem("ff2_psum"), sem("acc_step"), sem("cwe_ready"), sem("stored"))
        block = ctx.enter_context(nc.Block())
        rows = h_io[0:tokens, :].rearrange("(j p) d -> p j d", p=P)
        rows_out = h_out[0:tokens, :].rearrange("(j p) d -> p j d", p=P)

        @block.sync
        def _(sp):
            sp.dma_start(acc[:, :, :], rows).then_inc(loaded, 16)
            sp.dma_start(bias_b[:, :], bias.partition_broadcast(P)).then_inc(loaded, 16)
            sp.dma_start(wk[:, :, :], weights.rearrange("(j p) k -> p j k", p=P)).then_inc(loaded, 16)
            sp.dma_start(ik[:, :, :], indices.rearrange("(j p) k -> p j k", p=P)).then_inc(loaded, 16)
            def turn(i):
                for s in range(2):
                    e = i * 2 + s
                    wait(sp, ff2_psum, i * (2 * NT))
                    sp.dma_start(w1s[s][:, :, :], w1[bass.ds(e, 1), :, :].rearrange("o (k p) n -> p (o k) n", p=P)
                                 ).then_inc(w_loaded[s], 16)
                    sp.dma_start(w2s[s][:, :, :], w2[bass.ds(e, 1), :, :].rearrange("o (g p) n -> p (o g) n", p=P)
                                 ).then_inc(w_loaded[s], 16)

            repeat(sp, E // 2, turn)
            sp.wait_ge(acc_step, E * NT)
            sp.dma_start(rows_out, acc[:, :, :]).then_inc(stored, 16)
            sp.wait_ge(stored, 16)

        @block.gpsimd
        def _(pool):
            nc.gpsimd.iota(e_i[:, :], pattern=[[1, E]], base=0, channel_multiplier=0).then_inc(iota_done, 1)
            pool.wait_ge(step_done, 3)
            nc.gpsimd.tensor_tensor(rstd[:, :], mv[:, :, 1], core.eps[:, 0:mv.shape[1]], ALU.add).then_inc(rstd_step, 1)
            pool.wait_ge(rstd_step, 1)
            nc.gpsimd.tensor_tensor(rstd[:, :], rstd[:, :], core.neg_half[:, 0:NT], ALU.pow).then_inc(rstd_step, 1)

        @block.vector
        def _(dve):
            steps = [0]

            def step(ins):
                ins.then_inc(step_done, 1)
                steps[0] += 1
                dve.wait_ge(step_done, steps[0])

            dve.wait_ge(loaded, 64)
            step(nc.vector.tensor_tensor(x[:, :, :], acc[:, :, :], bias_b[:, :].unsqueeze(1).to_broadcast([P, NT, D]),
                                         ALU.subtract))
            for j in range(NT):
                last = nc.vector.bn_stats(bn[:, j, :], x[:, j, :])
            step(last)
            hold(dve, passed)
            for j in range(NT):
                last = nc.vector.bn_aggr(mv[:, j, :], bn[:, j, :])
            step(last)
            dve.wait_ge(rstd_step, 2)
            for j in range(NT):
                last = nc.vector.tensor_scalar(x[:, j, :], x[:, j, :], mv[:, j, 0:1], rstd[:, j:j + 1], ALU.subtract,
                                               ALU.mult)
            last.then_inc(x_ready, 1)
            dve.wait_ge(iota_done, 1)
            nc.vector.tensor_copy(e_f[:, :], e_i[:, :])
            step(nc.vector.tensor_copy(ikf[:, :, :], ik[:, :, :]))
            for k in range(K):
                out = cw if k == 0 else eq
                step(nc.vector.tensor_tensor(out[:, :, :], ikf[:, :, k:k + 1].to_broadcast([P, NT, E]),
                                             e_f[:, :].unsqueeze(1).to_broadcast([P, NT, E]), ALU.is_equal))
                step(nc.vector.tensor_tensor(out[:, :, :], out[:, :, :], wk[:, :, k:k + 1].to_broadcast([P, NT, E]),
                                             ALU.mult))
                if k:
                    step(nc.vector.tensor_tensor(cw[:, :, :], cw[:, :, :], eq[:, :, :], ALU.add))
            def turn(e):
                wait(dve, acc_step, e * NT)
                nc.vector.tensor_copy(cwe[:, :].unsqueeze(2), cw[:, :, bass.ds(e, 1)]).then_inc(cwe_ready, 1)
                wait(dve, cwe_ready, e + 1)
                for j in range(NT):
                    wait(dve, ff2_psum, e * NT + j + 1)
                    nc.vector.scalar_tensor_tensor(acc[:, j, :], bank[4 + j % 4][:, 0:D], cwe[:, j:j + 1], acc[:, j, :],
                                                   ALU.mult, ALU.add).then_inc(acc_step, 1)

            repeat(dve, E, turn)

        @block.scalar
        def _(act):
            for m in range(2 * NB):
                act.wait_ge(xT_psum, m + 1)
                f, b = m % 2, m // 2
                nc.scalar.copy(xT[:, f, b * T:(b + 1) * T], bank[m % 4][:, :]).then_inc(xT_ready, 1)
            def turn(e):
                for b in range(NB):
                    for g in range(FB):
                        t = b * FB + g
                        wait(act, ff1_psum, e * (NB * FB) + t + 1)
                        if g == 0:
                            wait(act, ff2_psum, e * NT)
                        nc.scalar.activation(hid[b][:, g, :], bank[t % 4][:, :], ACT.Gelu).then_inc(hid_ready, 1)

            repeat(act, E, turn)

        @block.tensor
        def _(pe):
            pe.wait_ge(x_ready, 1)
            for m in range(2 * NB):
                f, b = m % 2, m // 2
                for j in range(TJ):
                    last = nc.tensor.transpose(bank[m % 4][:, j * P:(j + 1) * P], x[:, b * TJ + j, f * P:(f + 1) * P],
                                               core.ident[:, :])
                last.then_inc(xT_psum, 1)
            pe.wait_ge(xT_ready, 2 * NB)
            def turn(i):
                for s in range(2):
                    e = i * 2 + s
                    wait(pe, w_loaded[s], i * 32 + 32)
                    for b in range(NB):
                        for g in range(FB):
                            t = b * FB + g
                            if t >= 4:
                                wait(pe, hid_ready, e * (NB * FB) + t - 3)
                            else:
                                wait(pe, hid_ready, e * (NB * FB))
                            for kk in range(2):
                                last = nc.tensor.matmul(bank[t % 4][:, :], w1s[s][:, kk, g * P:(g + 1) * P],
                                                        xT[:, kk, b * T:(b + 1) * T], start=(kk == 0), stop=(kk == 1))
                            last.then_inc(ff1_psum, 1)
                    for j in range(NT):
                        b = j // TJ
                        wait(pe, hid_ready, e * (NB * FB) + (b + 1) * FB)
                        if j >= 4:
                            wait(pe, acc_step, e * NT + j - 3)
                        else:
                            wait(pe, acc_step, e * NT)
                        t0 = (j % TJ) * P
                        for g in range(FB):
                            last = nc.tensor.matmul(bank[4 + j % 4][:, 0:D], hid[b][:, g, t0:t0 + P], w2s[s][:, g, :],
                                                    start=(g == 0), stop=(g == FB - 1))
                        last.then_inc(ff2_psum, 1)

            repeat(pe, E // 2, turn)


def tower(nc, args, out, phases=9):
    ids = args["x"]
    tokens = ids.shape[0] * ids.shape[1]
    chunks = tokens // T
    seq = 2048
    h0 = nc.dram_tensor("h0", (tokens, D), F32, kind="Internal").ap()
    h1 = nc.dram_tensor("h1", (tokens, D), F32, kind="Internal").ap()
    h2 = nc.dram_tensor("h2", (tokens, D), F32, kind="Internal").ap()
    with ExitStack() as ctx:
        core = Core(nc, ctx, chunks, seq // T)
        with nc.cleanup_on_exit():
            build_constants(core)
        with nc.cleanup_on_exit():
            embedding_phase(core, ids, args["L0_tok_a_n"], args["L0_tok_b_n"], args["L0_tok_proj_wT"],
                            args["L0_tok_proj_b"], h0)
        if phases > 1:
            with nc.cleanup_on_exit():
                attention_phase(core, args["L0_attn_Wq"], args["L0_attn_Wf"], args["L0_attn_Wi"],
                                args["L0_attn_Wo"], h0, h1)
        if phases > 2:
            with nc.cleanup_on_exit():
                ffn_phase(core, args["L0_ffn_gate_wT"], args["L0_ffn_down_T"], args["L0_ffn_down_bT"],
                          args["L0_ffn_up_T"], args["L0_ffn_up_b"], h1, h2)
        if phases > 3:
            w = {name[len("L1_attn_"):]: ap for name, ap in args.items() if name.startswith("L1_attn_")}
            w["moe_bias"] = args["L1_ffn_bias"]
            with nc.cleanup_on_exit():
                ssm_phase(core, w, h2, out)
        if phases > 4:
            with nc.cleanup_on_exit():
                moe_phase(core, args["L1_ffn_bias"], args["L1_ffn_expert_weights"], args["L1_ffn_expert_indices"],
                          args["L1_ffn_w1"], args["L1_ffn_w2"], out, out)


def lay_out(inputs):
    import numpy as np

    a = {name: np.asarray(x) for name, x in inputs.items()}
    a["x"] = a["x"].reshape(-1, P)
    a["L0_tok_proj_wT"] = a.pop("L0_tok_proj_w").T
    a["L0_ffn_gate_wT"] = a.pop("L0_ffn_gate_w").T
    a["L0_ffn_down_T"] = a.pop("L0_ffn_down_w").transpose(2, 0, 1)
    a["L0_ffn_down_bT"] = a.pop("L0_ffn_down_b").T
    a["L0_ffn_up_T"] = a.pop("L0_ffn_up_w").transpose(2, 0, 1)
    for name in ("ln_g", "ln_b", "w1_b", "v1_b", "dt_b", "D_p", "ln2_g", "ln2_b", "ff1_b"):
        a["L1_attn_" + name] = a["L1_attn_" + name].reshape(-1, P).T
    for name in ("Bp_b", "Cp_b"):
        a["L1_attn_" + name] = a["L1_attn_" + name].reshape(-1, 1)
    del a["L1_ffn_scores"]
    return {name: np.ascontiguousarray(x) for name, x in a.items()}


def kernel(**inputs):
    import concourse.bacc as bacc
    from concourse.bass_utils import run_bass_kernel_spmd

    batch, seq = inputs["x"].shape
    nc = bacc.Bacc("TRN2", target_bir_lowering=False, num_devices=1)
    arrays, args = {}, {}
    for name, a in lay_out(inputs).items():
        arrays[f"in_{name}"] = a
        args[name] = nc.dram_tensor(f"in_{name}", a.shape, mybir.dt.from_np(a.dtype), kind="ExternalInput").ap()
    out = nc.dram_tensor("out_0", (batch * seq, D), F32, kind="ExternalOutput").ap()
    tower(nc, args, out)
    result = run_bass_kernel_spmd(nc, [arrays], core_ids=[0])
    return result.results[0]["out_0"].reshape(batch, seq, D)
```

```python
from contextlib import ExitStack

import concourse.bass as bass
from concourse import mybir

F32 = mybir.dt.float32
BF16 = mybir.dt.bfloat16
I32 = mybir.dt.int32
ALU = mybir.AluOpType
ACT = mybir.ActivationFunctionType
AX = mybir.AxisListType

P = 128
D = 256
T = 512
TJ = T // P
EPS = 1e-5
PI = 3.141592653589793


def wait(eng, sem, value):
    if not (isinstance(value, int) and value <= 0):
        eng.wait_ge(sem, value)


def hold(eng, passed):
    eng.sem_inc(passed, 1)


def repeat(eng, n, body):
    body(0)
    if n > 1:
        with eng.Fori(1, n) as i:
            body(i)


def sweep(eng, chunks, front, body):
    front(0, 0)
    body(0, 0, True, False)
    body(1, 1, False, False)
    if chunks > 4:
        with eng.Fori(1, chunks // 2 - 1) as i:
            body(i * 2, 0, False, False)
            body(i * 2 + 1, 1, False, False)
    body(chunks - 2, 0, False, False)
    body(chunks - 1, 1, False, True)


def chunk_view(h):
    return h.rearrange("(c j p) d -> c p j d", j=TJ, p=P)


def one(view, c):
    return view[bass.ds(c, 1), :, :, :].rearrange("o p j d -> p (o j) d")


def past(c, n):
    return not isinstance(c, int) or c >= n


class Core:

    def __init__(self, nc, ctx, chunks, chunks_per_batch):
        self.nc = nc
        self.chunks = chunks
        self.bank = [ctx.enter_context(nc.psum_tensor(f"bank{i}", [P, T], F32)) for i in range(8)]
        sb = lambda name, shape, dt=F32: ctx.enter_context(nc.sbuf_tensor(name, shape, dt))
        self.ident = sb("ident", [P, P])
        self.ident_b = sb("ident_b", [P, P], BF16)
        self.neg_half = sb("neg_half", [P, 8])
        self.eps = sb("eps", [P, 8])
        self.ones = sb("ones", [P, P])
        self.keep = sb("keep", [P, chunks + 1])
        self.chunks_per_batch = chunks_per_batch


def build_constants(core):
    nc = core.nc
    with ExitStack() as ctx:
        filled = nc.alloc_semaphore(name="const_filled")
        block = ctx.enter_context(nc.Block())

        @block.gpsimd
        def _(pool):
            nc.gpsimd.memset(core.ident[:, :], 0.0).then_inc(filled, 1)
            nc.gpsimd.memset(core.ident_b[:, :], 0.0).then_inc(filled, 1)
            nc.gpsimd.memset(core.ones[:, :], 1.0).then_inc(filled, 1)
            nc.gpsimd.memset(core.neg_half[:, :], -0.5).then_inc(filled, 1)
            nc.gpsimd.memset(core.keep[:, :], 1.0).then_inc(filled, 1)
            nc.gpsimd.memset(core.eps[:, :], EPS).then_inc(filled, 1)
            pool.wait_ge(filled, 6)
            for m in (core.ident, core.ident_b):
                nc.gpsimd.affine_select(out=m[:, :], in_=m[:, :], compare_op=ALU.not_equal, fill=1.0, base=0,
                                        pattern=[[-1, P]], channel_multiplier=1)
            nc.gpsimd.memset(core.keep[:, 0::core.chunks_per_batch], 0.0).then_inc(filled, 1)
            pool.wait_ge(filled, 7)


def embedding_phase(core, ids, ab_n, proj_wT, proj_b, h_out):
    nc, bank, chunks = core.nc, core.bank, core.chunks
    V, NF = ab_n.shape[0], ab_n.shape[1] // 2
    tiles = ids.shape[0]
    GATHERED = 16 * TJ
    MAGIC = 1.5 * 2.0 ** 23
    with ExitStack() as ctx:
        def sb(name, shape, dt=F32):
            return ctx.enter_context(nc.sbuf_tensor("e_" + name, shape, dt))

        def sem(name):
            return nc.alloc_semaphore(name="e_" + name)

        passed = sem("passed")

        ids_row = sb("ids_row", [tiles, P], I32)
        ids_f = sb("ids_f", [tiles, P])
        idT_f = sb("idT_f", [P, tiles])
        idT_i = sb("idT_i", [P, tiles], I32)
        freq_i = sb("freq_i", [P, NF], I32)
        freq = sb("freq", [P, NF])
        half_pi = sb("half_pi", [P, 1])
        w2 = sb("w2", [2 * NF, D])
        bias = sb("bias", [P, D])
        idx = [sb(f"idx{q}", [P, TJ], I32) for q in range(2)]
        gath = [sb(f"gath{q}", [P, TJ, 2 * NF]) for q in range(2)]
        idc = [sb(f"idc{q}", [P, TJ]) for q in range(2)]
        prod = [sb(f"prod{q}", [P, TJ, NF]) for q in range(2)]
        turns = [sb(f"turns{q}", [P, TJ, NF]) for q in range(2)]
        trig = [sb(f"trig{q}", [P, TJ, 2 * NF]) for q in range(2)]
        emb = [sb(f"emb{q}", [P, TJ, 2 * NF]) for q in range(2)]
        embT = [sb(f"embT{q}", [2 * NF, T]) for q in range(2)]
        hbuf = [sb(f"hbuf{q}", [P, TJ, D]) for q in range(2)]

        loaded, consts, ids_cast, ids_turned, ids_ready = (
            sem("loaded"), sem("consts"), sem("ids_cast"), sem("ids_turned"), sem("ids_ready"))
        idx_ready = sem("idx_ready")
        gathered = [sem(f"gathered{q}") for q in range(2)]
        step_done = sem("step_done")
        phase_ready = sem("phase_ready")
        trig_ready = sem("trig_ready")
        emb_ready = sem("emb_ready")
        embT_psum = sem("embT_psum")
        embT_ready = sem("embT_ready")
        h_psum = sem("h_psum")
        h_ready = sem("h_ready")
        stored = [sem(f"stored{q}") for q in range(2)]
        block = ctx.enter_context(nc.Block())
        hv = chunk_view(h_out)

        @block.sync
        def _(sp):
            sp.dma_start(ids_row[:, :], ids).then_inc(loaded, 16)
            sp.dma_start(w2[0:NF, :], proj_wT).then_inc(loaded, 16)
            sp.dma_start(w2[NF:2 * NF, :], proj_wT).then_inc(loaded, 16)
            sp.dma_start(bias[:, :], proj_b.partition_broadcast(P)).then_inc(loaded, 16)

            def store(c, q):
                sp.wait_ge(h_ready, c * 2 + 2)
                sp.dma_start(one(hv, c), hbuf[q][:, :, :]).then_inc(stored[q], 16)

            def body(c, q, first, last):
                if not first:
                    store(c - 1, 1 - q)

            sweep(sp, chunks, lambda fc, fq: None, body)
            store(chunks - 1, 1)
            for q in range(2):
                sp.wait_ge(stored[q], 8 * chunks)

        @block.gpsimd
        def _(pool):
            nc.gpsimd.iota(freq_i[:, :], pattern=[[1, NF]], base=1, channel_multiplier=0).then_inc(consts, 1)
            nc.gpsimd.memset(half_pi[:, :], PI / 2).then_inc(consts, 1)

            def front(fc, fq):
                pool.wait_ge(idx_ready, fc + 1)
                wait(pool, emb_ready, fc - 1)
                hold(pool, passed)
                for j in range(TJ):
                    off = bass.IndirectOffsetOnAxis(ap=idx[fq][:, j:j + 1], axis=0)
                    nc.gpsimd.indirect_dma_start(gath[fq][:, j, :], None, ab_n, off).then_inc(gathered[fq], 16)

            def body(c, q, first, last):
                if not last:
                    front(c + 1, 1 - q)

            sweep(pool, chunks, front, body)

        @block.vector
        def _(dve):
            dve.wait_ge(loaded, 64)
            nc.vector.tensor_copy(ids_f[:, :], ids_row[:, :]).then_inc(ids_cast, 1)
            dve.wait_ge(consts, 2)
            nc.vector.tensor_copy(freq[:, :], freq_i[:, :])
            dve.wait_ge(ids_turned, 1)
            nc.vector.tensor_copy(idT_f[:, :], bank[0][:, 0:tiles])
            nc.vector.tensor_copy(idT_i[:, :], bank[0][:, 0:tiles]).then_inc(ids_ready, 1)
            dve.wait_ge(ids_ready, 1)

            def front(fc, fq):
                wait(dve, gathered[fq], (fc - fq) * (GATHERED // 2))
                nc.vector.tensor_copy(idx[fq][:, :], idT_i[:, bass.ds(fc * TJ, TJ)]).then_inc(idx_ready, 1)
                nc.vector.tensor_copy(idc[fq][:, :], idT_f[:, bass.ds(fc * TJ, TJ)]).then_inc(step_done, 1)
                dve.wait_ge(step_done, fc * 4 + 1)
                wait(dve, trig_ready, fc - 1)
                nc.vector.tensor_tensor(prod[fq][:, :, :], freq[:, :].unsqueeze(1).to_broadcast([P, TJ, NF]),
                                        idc[fq][:, :].unsqueeze(2).to_broadcast([P, TJ, NF]),
                                        ALU.mult).then_inc(step_done, 1)
                dve.wait_ge(step_done, fc * 4 + 2)
                nc.vector.tensor_scalar(turns[fq][:, :, :], prod[fq][:, :, :], 1.0 / V, MAGIC, ALU.mult,
                                        ALU.add).then_inc(step_done, 1)
                dve.wait_ge(step_done, fc * 4 + 3)
                nc.vector.tensor_scalar(turns[fq][:, :, :], turns[fq][:, :, :], MAGIC, float(V), ALU.subtract,
                                        ALU.mult).then_inc(step_done, 1)
                dve.wait_ge(step_done, fc * 4 + 4)
                nc.vector.tensor_tensor(prod[fq][:, :, :], prod[fq][:, :, :], turns[fq][:, :, :],
                                        ALU.subtract).then_inc(phase_ready, 1)
                dve.wait_ge(phase_ready, fc * 2 + 1)
                nc.vector.scalar_tensor_tensor(turns[fq][:, :, :], prod[fq][:, :, :], -1.0, prod[fq][:, :, :],
                                               ALU.mult, ALU.max).then_inc(phase_ready, 1)

            def finish(c, q):
                wait(dve, stored[q], (c - q) * 8)
                for m in range(2):
                    dve.wait_ge(h_psum, c * 2 + m + 1)
                    nc.vector.tensor_tensor(hbuf[q][:, 2 * m:2 * m + 2, :],
                                            bank[2 + 2 * q + m][:, :].rearrange("p (j d) -> p j d", j=2),
                                            bias[:, :].unsqueeze(1).to_broadcast([P, 2, D]),
                                            ALU.add).then_inc(h_ready, 1)

            def body(c, q, first, last):
                if not last:
                    front(c + 1, 1 - q)
                dve.wait_ge(gathered[q], (c - q) * (GATHERED // 2) + GATHERED)
                dve.wait_ge(trig_ready, c + 1)
                wait(dve, embT_psum, c - 1)
                nc.vector.tensor_tensor(emb[q][:, :, :], gath[q][:, :, :], trig[q][:, :, :],
                                        ALU.mult).then_inc(emb_ready, 1)
                if not first:
                    finish(c - 1, 1 - q)

            sweep(dve, chunks, front, body)
            finish(chunks - 1, 1)

        @block.scalar
        def _(act):
            act.wait_ge(consts, 2)

            def front(fc, fq):
                act.wait_ge(phase_ready, fc * 2 + 2)
                wait(act, emb_ready, fc - 1)
                nc.scalar.activation(trig[fq][:, :, 0:NF], turns[fq][:, :, :], ACT.Sin, bias=half_pi[:, :],
                                     scale=-2.0 * PI / V)
                nc.scalar.activation(trig[fq][:, :, NF:2 * NF], prod[fq][:, :, :], ACT.Sin,
                                     scale=2.0 * PI / V).then_inc(trig_ready, 1)

            def body(c, q, first, last):
                if not last:
                    front(c + 1, 1 - q)
                act.wait_ge(embT_psum, c + 1)
                wait(act, h_psum, (c - 1) * 2)
                nc.scalar.copy(embT[q][:, :], bank[q][:, :]).then_inc(embT_ready, 1)

            sweep(act, chunks, front, body)

        @block.tensor
        def _(pe):
            pe.wait_ge(ids_cast, 1)
            nc.tensor.transpose(bank[0][:, 0:tiles], ids_f[:, :], core.ident[0:tiles, 0:tiles]).then_inc(ids_turned, 1)
            pe.wait_ge(loaded, 64)
            pe.wait_ge(ids_ready, 1)

            def project(c, q):
                pe.wait_ge(embT_ready, c + 1)
                wait(pe, h_ready, (c - 1) * 2)
                for m in range(2):
                    for j in range(2):
                        t0 = (2 * m + j) * P
                        last = nc.tensor.matmul(bank[2 + 2 * q + m][:, j * D:(j + 1) * D], embT[q][:, t0:t0 + P],
                                                w2[:, :], start=True, stop=True)
                    last.then_inc(h_psum, 1)

            def body(c, q, first, last):
                pe.wait_ge(emb_ready, c + 1)
                wait(pe, embT_ready, c - 1)
                for j in range(TJ):
                    last = nc.tensor.transpose(bank[q][:, j * P:(j + 1) * P], emb[q][:, j, :], core.ident[:, :])
                last.then_inc(embT_psum, 1)
                if not first:
                    project(c - 1, 1 - q)

            sweep(pe, chunks, lambda fc, fq: None, body)
            project(chunks - 1, 1)


def attention_phase(core, Wq, Wf, Wi, Wo, h_in, h_out):
    nc, bank, chunks = core.nc, core.bank, core.chunks
    H, DK = 16, D // 16
    DV = DK
    SCALE = DK ** -0.5
    HH = H // 2
    G = 4
    L = DV // G
    GR = HH * L
    RING = 4
    STACKED = 16 * 3 * G
    with ExitStack() as ctx:
        def sb(name, shape, dt=F32):
            return ctx.enter_context(nc.sbuf_tensor("a_" + name, shape, dt))

        def sem(name):
            return nc.alloc_semaphore(name="a_" + name)

        passed = sem("passed")

        wqf = sb("wqf", [P, 2, 2 * D])
        wi = sb("wi", [P, 2, D])
        wo = sb("wo", [P, 2, D])
        head = sb("head", [P, HH])
        gather = sb("gather", [P, DV, G, HH, L])
        head_sq = sb("head_sq", [P, G, HH, L])
        pick = sb("pick", [3 * HH * L, L, HH, DK], BF16)
        hb = [sb(f"hb{q}", [P, TJ, D]) for q in range(2)]
        h_new = sb("h_new", [P, TJ, D])
        bn = sb("bn", [P, TJ, 6])
        mv = sb("mv", [P, TJ, 2])
        rstd = sb("rstd", [P, TJ])
        xh = sb("xh", [P, TJ, D])
        xT = sb("xT", [P, 2, T])
        v = sb("v", [P, 2, T + 1])
        dv = sb("dv", [P, 2, T])
        dvs = [sb(f"dvs{m}", [P, 2, T], BF16) for m in range(3)]
        stack = [sb(f"stack{q}", [3 * GR, G, 2, T], BF16) for q in range(2)]
        ex = [sb(f"ex{s}", [P, 2, D]) for s in range(2)]
        nmx = [sb(f"nmx{s}", [P, 2]) for s in range(2)]
        sums = [sb(f"sums{s}", [P, 2]) for s in range(2)]
        rsum = [sb(f"rsum{s}", [P, 2]) for s in range(2)]
        qp = [sb(f"qp{q}", [P, 2, 2, T]) for q in range(2)]
        vq = sb("vq", [P, 2, T])
        z = [sb(f"z{s}", [P, 2, T]) for s in range(RING)]
        zlast = sb("zlast", [P, DV, 2])
        carry = sb("carry", [P, DV, 2])
        oT = sb("oT", [P, 2, T])

        bc, op, tp, mm = bank[0:2], bank[2:4], bank[4:6], bank[6:8]

        loaded, sel_step, consts = sem("loaded"), sem("sel_step"), sem("consts")
        h_loaded = [sem(f"h_loaded{q}") for q in range(2)]
        bn_done, stats_ready, var_eps, rstd_ready, xh_ready = (
            sem("bn_done"), sem("stats_ready"), sem("var_eps"), sem("rstd_ready"), sem("xh_ready"))
        xT_psum, xT_ready = sem("xT_psum"), sem("xT_ready")
        vcarry_ready, v_psum, v_ready = sem("vcarry_ready"), sem("v_psum"), sem("v_ready")
        dv_ready, hi_ready, mid_ready, lo_ready = sem("dv_ready"), sem("hi_ready"), sem("mid_ready"), sem("lo_ready")
        rest1_ready, rest2_ready = sem("rest1_ready"), sem("rest2_ready")
        lg_psum = [sem(f"lg_psum{s}") for s in range(2)]
        nmx_ready = sem("nmx_ready")
        exp_done = [sem(f"exp_done{s}") for s in range(2)]
        rsum_ready = sem("rsum_ready")
        qp_ready = sem("qp_ready")
        qpT_psum = [sem(f"qpT_psum{s}") for s in range(2)]
        qpT_ready = [sem(f"qpT_ready{s}") for s in range(2)]
        sumq_psum, vq_ready = sem("sumq_psum"), sem("vq_ready")
        bc_psum = [sem(f"bc_psum{f}") for f in range(2)]
        scan_done = [sem(f"scan_done{f}") for f in range(2)]
        zlast_saved, g_ready = sem("zlast_saved"), sem("g_ready")
        red_done = sem("red_done")
        stacked = [sem(f"stacked{q}") for q in range(2)]
        carry_ready = [sem(f"carry_ready{m}") for m in range(2)]
        oT_ready, ap_psum, hnew_ready, h_stored = sem("oT_ready"), sem("ap_psum"), sem("hnew_ready"), sem("h_stored")
        block = ctx.enter_context(nc.Block())
        hin, hout = chunk_view(h_in), chunk_view(h_out)

        @block.sync
        def _(sp):
            for k in range(2):
                sp.dma_start(wqf[:, k, 0:D], Wq[k * P:(k + 1) * P, :]).then_inc(loaded, 16)
                sp.dma_start(wqf[:, k, D:2 * D], Wf[k * P:(k + 1) * P, :]).then_inc(loaded, 16)
                sp.dma_start(wi[:, k, :], Wi[k * P:(k + 1) * P, :]).then_inc(loaded, 16)
                sp.dma_start(wo[:, k, :], Wo[k * P:(k + 1) * P, :]).then_inc(loaded, 16)

            def load(fc, fq):
                if not isinstance(fc, int) or fc >= 2:
                    sp.wait_ge(hnew_ready, (fc - 1) * 2)
                sp.dma_start(hb[fq][:, :, :], one(hin, fc)).then_inc(h_loaded[fq], 16)

            def store(c):
                sp.wait_ge(hnew_ready, c * 2 + 2)
                sp.dma_start(one(hout, c), h_new[:, :, :]).then_inc(h_stored, 16)

            def restack(fc, fq):
                if past(fc, 2):
                    sp.wait_ge(bc_psum[1], (fc - 1) * DV)
                    hold(sp, passed)
                for m, ready in enumerate((hi_ready, mid_ready, lo_ready)):
                    sp.wait_ge(ready, fc + 1)
                    for g in range(G):
                        sp.dma_start(stack[fq][m * GR:(m + 1) * GR, g, :, :],
                                     dvs[m][g * GR:(g + 1) * GR, :, :]).then_inc(stacked[fq], 16)

            def body(c, q, first, last):
                if not last:
                    load(c + 1, 1 - q)
                if not first:
                    store(c - 1)
                if not last:
                    restack(c + 1, 1 - q)

            def front0(fc, fq):
                load(fc, fq)
                restack(fc, fq)

            sweep(sp, chunks, front0, body)
            store(chunks - 1)
            sp.wait_ge(h_stored, 16 * chunks)

        @block.gpsimd
        def _(pool):
            nc.gpsimd.memset(head[:, :], 1.0).then_inc(sel_step, 1)
            nc.gpsimd.memset(gather[:, :, :, :, :], 0.0).then_inc(sel_step, 1)
            nc.gpsimd.memset(pick[:, :, :, :], 0.0).then_inc(sel_step, 1)
            nc.gpsimd.memset(v[:, :, :], 0.0).then_inc(sel_step, 1)
            nc.gpsimd.memset(zlast[:, :, :], 0.0).then_inc(sel_step, 1)
            pool.wait_ge(sel_step, 5)
            nc.gpsimd.affine_select(out=head[:, :], in_=head[:, :], compare_op=ALU.is_ge, fill=0.0, base=0,
                                    pattern=[[-DK, HH]], channel_multiplier=1).then_inc(sel_step, 1)
            pool.wait_ge(sel_step, 6)
            nc.gpsimd.affine_select(out=head[:, :], in_=head[:, :], compare_op=ALU.is_ge, fill=0.0, base=DK - 1,
                                    pattern=[[DK, HH]], channel_multiplier=-1).then_inc(sel_step, 1)
            for m in range(3):
                pool.wait_ge(sel_step, 7 + m)
                nc.gpsimd.affine_select(out=pick[:, :, :, :], in_=pick[:, :, :, :], compare_op=ALU.not_equal,
                                        fill=1.0, base=-m * GR, pattern=[[-1, L], [-L, HH], [0, DK]],
                                        channel_multiplier=1).then_inc(sel_step, 1)
            pool.wait_ge(sel_step, 10)
            for vi in range(DV):
                nc.gpsimd.tensor_copy(gather[:, vi, vi // L, :, vi % L], head[:, :]).then_inc(consts, 1)
            for g in range(G):
                last = nc.gpsimd.tensor_copy(head_sq[:, g, :, :], head[:, :].unsqueeze(2).to_broadcast([P, HH, L]))
            last.then_inc(consts, 1)

            def front(fc, fq, k=None):
                if k in (None, 5):
                    pool.wait_ge(stats_ready, fc + 1)
                    wait(pool, xh_ready, fc)
                    nc.gpsimd.tensor_tensor(rstd[:, :], mv[:, :, 1], core.eps[:, 0:mv.shape[1]], ALU.add).then_inc(var_eps, 1)
                    pool.wait_ge(var_eps, fc + 1)
                    nc.gpsimd.tensor_tensor(rstd[:, :], rstd[:, :], core.neg_half[:, 0:TJ],
                                            ALU.pow).then_inc(rstd_ready, 1)
                if k in (None, 9):
                    pool.wait_ge(hi_ready, fc + 1)
                    nc.gpsimd.tensor_tensor(dv[:, :, :], dv[:, :, :], dvs[0][:, :, :],
                                            ALU.subtract).then_inc(rest1_ready, 1)
                if k in (None, 11):
                    pool.wait_ge(mid_ready, fc + 1)
                    nc.gpsimd.tensor_tensor(dv[:, :, :], dv[:, :, :], dvs[1][:, :, :],
                                            ALU.subtract).then_inc(rest2_ready, 1)

            def body(c, q, first, last):
                for vi in range(DV):
                    for f in range(2):
                        pool.wait_ge(scan_done[f], c * DV + vi + 1)
                    if vi in (0, 8):
                        pool.wait_ge(carry_ready[vi // 8], c + 1)
                    hold(pool, passed)
                    nc.gpsimd.tensor_copy(zlast[:, vi, :], z[vi % RING][:, :, T - 1]).then_inc(zlast_saved, 1)
                    pool.wait_ge(zlast_saved, c * DV + vi + 1)
                    if vi == 0:
                        for s in range(2):
                            pool.wait_ge(qpT_ready[s], c * 2 + 2)
                    nc.gpsimd.tensor_tensor(z[vi % RING][:, :, :], z[vi % RING][:, :, :], qp[q][:, 0, :, :],
                                            ALU.mult).then_inc(g_ready, 1)
                    if not last:
                        front(c + 1, 1 - q, vi)

            sweep(pool, chunks, front, body)

        @block.vector
        def _(dve):
            dve.wait_ge(consts, DV + 1)

            def front(fc, fq, k=None):
                if k in (None, 5):
                    dve.wait_ge(h_loaded[fq], h_count(fc, fq))
                    for j in range(TJ):
                        last = nc.vector.bn_stats(bn[:, j, :], hb[fq][:, j, :])
                    last.then_inc(bn_done, 1)
                    dve.wait_ge(bn_done, fc + 1)
                    wait(dve, rstd_ready, fc)
                    hold(dve, passed)
                    for j in range(TJ):
                        last = nc.vector.bn_aggr(mv[:, j, :], bn[:, j, :])
                    last.then_inc(stats_ready, 1)
                if k in (None, 6):
                    dve.wait_ge(rstd_ready, fc + 1)
                    dve.wait_ge(stats_ready, fc + 1)
                    wait(dve, xT_psum, fc * 2)
                    for j in range(TJ):
                        last = nc.vector.tensor_scalar(xh[:, j, :], hb[fq][:, j, :], mv[:, j, 0:1], rstd[:, j:j + 1],
                                                       ALU.subtract, ALU.mult)
                    last.then_inc(xh_ready, 1)
                    wait(dve, v_ready, fc * 2)
                    nc.vector.tensor_scalar(v[:, :, 0:1], v[:, :, T:T + 1], core.keep[:, bass.ds(fc, 1)], None,
                                            ALU.mult).then_inc(vcarry_ready, 1)
                if k in (None, 8):
                    dve.wait_ge(v_ready, fc * 2 + 2)
                    dve.wait_ge(vcarry_ready, fc + 1)
                    wait(dve, lo_ready, fc)
                    nc.vector.tensor_tensor(dv[:, :, :], v[:, :, 0:T], v[:, :, 1:T + 1],
                                            ALU.subtract).then_inc(dv_ready, 1)
                for j in range(TJ):
                    s = j % 2
                    if k in (None, 8 + 2 * j):
                        dve.wait_ge(lg_psum[s], fc * 2 + j // 2 + 1)
                        wait(dve, exp_done[s], fc * 2 + j // 2)
                        nc.vector.tensor_reduce(nmx[s][:, :], mm[s][:, :].rearrange("p (w d) -> p w d", w=2), AX.X,
                                                ALU.max, negate=True).then_inc(nmx_ready, 1)
                    if k in (None, 9 + 2 * j):
                        dve.wait_ge(exp_done[s], fc * 2 + j // 2 + 1)
                        nc.vector.reciprocal(rsum[s][:, :], sums[s][:, :]).then_inc(rsum_ready, 1)
                        dve.wait_ge(rsum_ready, fc * TJ + j + 1)
                        nc.vector.tensor_scalar(ex[s][:, 0, :], ex[s][:, 0, :], rsum[s][:, 0:1], SCALE, ALU.mult,
                                                ALU.mult)
                        nc.vector.tensor_scalar(ex[s][:, 1, :], ex[s][:, 1, :], rsum[s][:, 1:2], None,
                                                ALU.mult).then_inc(qp_ready, 1)

            def carry_half(c, m):
                wait(dve, zlast_saved, (c - 1) * DV + DV // 2 * (m + 1) if m == 0 else c * DV)
                nc.vector.tensor_scalar(carry[:, m * 8:(m + 1) * 8, :], zlast[:, m * 8:(m + 1) * 8, :],
                                        core.keep[:, bass.ds(c, 1)], None, ALU.mult).then_inc(carry_ready[m], 1)

            def finish_scan(c):
                dve.wait_ge(red_done, (c + 1) * DV)
                wait(dve, ap_psum, c * 2)
                for f in range(2):
                    last = nc.vector.tensor_tensor(oT[:, f, :], op[f][:, :], vq[:, f, :], ALU.add)
                last.then_inc(oT_ready, 1)

            def finish_rows(c, q):
                wait(dve, h_stored, c * 16)
                for m in range(2):
                    dve.wait_ge(ap_psum, c * 2 + m + 1)
                    nc.vector.tensor_tensor(h_new[:, 2 * m:2 * m + 2, :],
                                            mm[m][:, :].rearrange("p (j d) -> p j d", j=2),
                                            hb[q][:, 2 * m:2 * m + 2, :], ALU.add).then_inc(hnew_ready, 1)

            def body(c, q, first, last):
                for vi in range(DV):
                    s = vi % RING
                    if vi == 0:
                        for s2 in range(2):
                            dve.wait_ge(qpT_ready[s2], c * 2 + 2)
                    wait(dve, red_done, c * DV + vi - RING + 1)
                    if vi in (0, 8):
                        dve.wait_ge(carry_ready[vi // 8], c + 1)
                    for f in range(2):
                        dve.wait_ge(bc_psum[f], c * DV + vi + 1)
                        nc.vector.tensor_tensor_scan(z[s][:, f, :], bc[f][:, :], qp[q][:, 1, f, :],
                                                     carry[:, vi, f:f + 1], ALU.add,
                                                     ALU.mult).then_inc(scan_done[f], 1)
                    if vi == 1 and not first:
                        finish_scan(c - 1)
                    if vi == 2:
                        dve.wait_ge(sumq_psum, c * 2 + 2)
                        wait(dve, oT_ready, c)
                        for f in range(2):
                            ins = nc.vector.tensor_tensor(vq[:, f, :], mm[f][:, :], v[:, f, 1:T + 1], ALU.mult)
                        ins.then_inc(vq_ready, 1)
                    if vi == 3 and not first:
                        finish_rows(c - 1, 1 - q)
                    if vi == 4:
                        carry_half(c, 1)
                    if not last:
                        front(c + 1, 1 - q, vi)
                        if vi == 12:
                            carry_half(c + 1, 0)

            def front0(fc, fq):
                front(fc, fq)
                carry_half(0, 0)

            def h_count(fc, fq):
                return (fc - fq) * 8 + 16

            sweep(dve, chunks, front0, body)
            finish_scan(chunks - 1)
            finish_rows(chunks - 1, 1)

        @block.scalar
        def _(act):
            act.wait_ge(consts, DV + 1)

            def front(fc, fq, k=None):
                if k in (None, 6):
                    for f in range(2):
                        act.wait_ge(xT_psum, fc * 2 + f + 1)
                        wait(act, lg_psum[1], fc * 2)
                        nc.scalar.copy(xT[:, f, :], tp[f][:, :]).then_inc(xT_ready, 1)
                if k in (None, 7):
                    act.wait_ge(vcarry_ready, fc + 1)
                    wait(act, vq_ready, fc)
                    for f in range(2):
                        act.wait_ge(v_psum, fc * 2 + f + 1)
                        nc.scalar.copy(v[:, f, 1:T + 1], mm[f][:, :]).then_inc(v_ready, 1)
                if k in (None, 8):
                    act.wait_ge(dv_ready, fc + 1)
                    wait(act, rest2_ready, fc)
                    if past(fc, 1):
                        act.wait_ge(stacked[1 - fq], (fc + fq) * (STACKED // 2))
                    nc.scalar.copy(dvs[0][:, :, :], dv[:, :, :]).then_inc(hi_ready, 1)
                if k in (None, 10):
                    act.wait_ge(rest1_ready, fc + 1)
                    nc.scalar.copy(dvs[1][:, :, :], dv[:, :, :]).then_inc(mid_ready, 1)
                if k in (None, 12):
                    act.wait_ge(rest2_ready, fc + 1)
                    nc.scalar.copy(dvs[2][:, :, :], dv[:, :, :]).then_inc(lo_ready, 1)
                for j in range(TJ):
                    s = j % 2
                    if k in (None, 8 + 2 * j):
                        act.wait_ge(nmx_ready, fc * TJ + j + 1)
                        act.wait_ge(lg_psum[s], fc * 2 + j // 2 + 1)
                        wait(act, qpT_psum[s], fc * 2 + j // 2)
                        wait(act, rsum_ready, fc * TJ + j - 1) if not (isinstance(fc, int) and fc * TJ + j < 2) else None
                        for w in range(2):
                            last = nc.scalar.activation(ex[s][:, w, :], mm[s][:, w * D:(w + 1) * D], ACT.Exp,
                                                        bias=nmx[s][:, w:w + 1], accum_out=sums[s][:, w:w + 1])
                        last.then_inc(exp_done[s], 1)
                    if k in (None, 9 + 2 * j):
                        act.wait_ge(qpT_psum[s], fc * 2 + j // 2 + 1)
                        if j == 0 and (not isinstance(fc, int) or fc >= 2):
                            act.wait_ge(g_ready, (fc - 1) * DV)
                            act.wait_ge(sumq_psum, (fc - 1) * 2)
                        nc.scalar.copy(qp[fq][:, :, :, j * P:(j + 1) * P],
                                       tp[s][:, :].rearrange("p (w f t) -> p w f t", w=2, f=2)
                                       ).then_inc(qpT_ready[s], 1)

            def body(c, q, first, last):
                for vi in range(DV):
                    if not last:
                        front(c + 1, 1 - q, vi)

            sweep(act, chunks, front, body)

        @block.tensor
        def _(pe):
            pe.wait_ge(loaded, 8 * 16)
            pe.wait_ge(consts, DV + 1)

            def front(fc, fq, k=None):
                if k in (None, 6):
                    pe.wait_ge(xh_ready, fc + 1)
                    for f in range(2):
                        wait(pe, qpT_ready[f], fc * 2)
                        for j in range(TJ):
                            last = nc.tensor.transpose(tp[f][:, j * P:(j + 1) * P], xh[:, j, f * P:(f + 1) * P],
                                                       core.ident[:, :])
                        last.then_inc(xT_psum, 1)
                if k in (None, 7):
                    pe.wait_ge(xT_ready, fc * 2 + 2)
                    if not isinstance(fc, int) or fc >= 2:
                        pe.wait_ge(hnew_ready, (fc - 1) * 2)
                    elif fc == 1:
                        pe.wait_ge(vq_ready, 1)
                    for f in range(2):
                        for kk in range(2):
                            last = nc.tensor.matmul(mm[f][:, :], wi[:, kk, f * P:(f + 1) * P], xT[:, kk, :],
                                                    start=(kk == 0), stop=(kk == 1))
                        last.then_inc(v_psum, 1)
                for j in range(TJ):
                    s = j % 2
                    if k in (None, 7 + 2 * j):
                        if j < 2:
                            pe.wait_ge(v_ready, fc * 2 + s + 1)
                        wait(pe, exp_done[s], fc * 2 + j // 2)
                        for kk in range(2):
                            last = nc.tensor.matmul(mm[s][:, :], xT[:, kk, j * P:(j + 1) * P], wqf[:, kk, :],
                                                    start=(kk == 0), stop=(kk == 1))
                        last.then_inc(lg_psum[s], 1)
                    if k in (None, 9 + 2 * j):
                        pe.wait_ge(qp_ready, fc * TJ + j + 1)
                        wait(pe, qpT_ready[s], fc * 2 + j // 2)
                        for w in range(2):
                            for f in range(2):
                                last = nc.tensor.transpose(tp[s][:, (2 * w + f) * P:(2 * w + f + 1) * P],
                                                           ex[s][:, w, f * P:(f + 1) * P], core.ident[:, :])
                        last.then_inc(qpT_psum[s], 1)

            def spread_dv(c, q, vi):
                if vi == 0:
                    pe.wait_ge(stacked[q], (c - q) * (STACKED // 2) + STACKED)
                for f in range(2):
                    wait(pe, scan_done[f], c * DV + vi)
                    nc.tensor.matmul(bc[f][:, :], pick[:, vi % L, :, :].rearrange("p h k -> p (h k)"),
                                     stack[q][:, vi // L, f, :], start=True, stop=True).then_inc(bc_psum[f], 1)

            def reduce(c, vi):
                if vi == 0:
                    wait(pe, oT_ready, c)
                pe.wait_ge(g_ready, c * DV + vi + 1)
                for f in range(2):
                    last = nc.tensor.matmul(op[f][:, :], gather[:, vi, :, :, :].rearrange("p g h l -> p (g h l)"), z[vi % RING][:, f, :],
                                            start=(vi == 0), stop=(vi == DV - 1))
                last.then_inc(red_done, 1)

            def project(c):
                pe.wait_ge(oT_ready, c + 1)
                for m in range(2):
                    for j in range(2):
                        t0 = (2 * m + j) * P
                        for f in range(2):
                            last = nc.tensor.matmul(mm[m][:, j * D:(j + 1) * D], oT[:, f, t0:t0 + P], wo[:, f, :],
                                                    start=(f == 0), stop=(f == 1))
                    last.then_inc(ap_psum, 1)

            def body(c, q, first, last):
                for vi in range(DV):
                    if vi + 1 < DV:
                        spread_dv(c, q, vi + 1)
                    elif not last:
                        front(c + 1, 1 - q, vi)
                        spread_dv(c + 1, 1 - q, 0)
                    if vi > 0:
                        reduce(c, vi - 1)
                    elif not first:
                        reduce(c - 1, DV - 1)
                    if vi == 1:
                        for s in range(2):
                            pe.wait_ge(exp_done[s], c * 2 + 2)
                        for f in range(2):
                            ins = nc.tensor.matmul(mm[f][:, :], head_sq[:, :, :, :].rearrange("p g h l -> p (g h l)"),
                                                   qp[q][:, 0, f, :], start=True, stop=True)
                        ins.then_inc(sumq_psum, 2)
                    if vi == 2 and not first:
                        pe.wait_ge(vq_ready, c + 1)
                        project(c - 1)
                    if not last and vi + 1 < DV:
                        front(c + 1, 1 - q, vi)

            def front0(fc, fq):
                front(fc, fq)
                for s in range(2):
                    pe.wait_ge(qpT_ready[s], 2)
                spread_dv(0, 0, 0)

            sweep(pe, chunks, front0, body)
            reduce(chunks - 1, DV - 1)
            project(chunks - 1)


def ffn_phase(core, gate_wT, down_T, down_bT, up_T, up_b, h_in, h_out):
    nc, bank, chunks = core.nc, core.bank, core.chunks
    NC = core.chunks_per_batch
    S = NC * T
    E = gate_wT.shape[1]
    C = down_T.shape[2]
    batches = chunks // NC
    with ExitStack() as ctx:
        def sb(name, shape, dt=F32):
            return ctx.enter_context(nc.sbuf_tensor("f_" + name, shape, dt))

        def sem(name):
            return nc.alloc_semaphore(name="f_" + name)

        passed = sem("passed")

        gw = sb("gw", [P, 2, E])
        dw = sb("dw", [P, 2, E, C])
        db = sb("db", [2 * C, E])
        uw = sb("uw", [2 * C, E, D])
        ub = sb("ub", [E, D])
        lower = sb("lower", [P, E, E])
        hb = [sb(f"hb{m}", [P, TJ, D]) for m in range(NC)]
        bn = sb("bn", [P, TJ, 6])
        mv = sb("mv", [P, TJ, 2])
        rstd = sb("rstd", [P, TJ])
        xh = [sb(f"xh{s}", [P, TJ, D]) for s in range(2)]
        xT = sb("xT", [P, 2, S])
        sums = sb("sums", [P, 2, NC])
        pooled = sb("pooled", [P, 2])
        pooled_b = sb("pooled_b", [P, 2, P])
        g8 = sb("g8", [P, E])
        small = sb("small", [P, 8])
        cmp_a = sb("cmp_a", [P, E, E])
        cmp_b = sb("cmp_b", [P, E, E])
        rank = sb("rank", [P, E])
        sel = sb("sel", [P, 2, E])
        selg = sb("selg", [P, 2, E])
        wsum = sb("wsum", [P, E])
        wsumT = sb("wsumT", [E, P])
        rows = sb("rows", [2 * C, 2, E])
        prod = sb("prod", [2 * C, E])
        bsel = sb("bsel", [2 * C, 1])
        wd = sb("wd", [P, 2, 2, C])
        wu = sb("wu", [2 * C, D])
        hid = [sb(f"hid{s}", [2 * C, T]) for s in range(2)]
        h_new = [sb(f"h_new{s}", [P, TJ, D]) for s in range(2)]

        loaded, lower_step = sem("loaded"), sem("lower_step")
        h_loaded = [sem(f"h_loaded{m}") for m in range(NC)]
        bn_done, stats_ready, var_eps, rstd_ready, xh_ready = (
            sem("bn_done"), sem("stats_ready"), sem("var_eps"), sem("rstd_ready"), sem("xh_ready"))
        xT_psum, xT_ready = sem("xT_psum"), sem("xT_ready")
        gate_step, pooled_ready, gate_psum, gate_exp = (
            sem("gate_step"), sem("pooled_ready"), sem("gate_psum"), sem("gate_exp"))
        wsum_psum, chosen = sem("wsum_psum"), sem("chosen")
        hid_psum, hid_ready, up_psum, hnew_ready = sem("hid_psum"), sem("hid_ready"), sem("up_psum"), sem("hnew_ready")
        stored = [sem(f"stored{s}") for s in range(2)]
        block = ctx.enter_context(nc.Block())
        hin, hout = chunk_view(h_in), chunk_view(h_out)
        GATE_STEPS = 18 + 3 * E

        @block.sync
        def _(sp):
            for k in range(2):
                sp.dma_start(gw[:, k, :], gate_wT[k * P:(k + 1) * P, :]).then_inc(loaded, 16)
                sp.dma_start(dw[:, k, :, :], down_T[k * P:(k + 1) * P, :, :]).then_inc(loaded, 16)
                sp.dma_start(db[k * C:(k + 1) * C, :], down_bT).then_inc(loaded, 16)
                sp.dma_start(uw[k * C:(k + 1) * C, :, :], up_T).then_inc(loaded, 16)
            sp.dma_start(ub[:, :], up_b).then_inc(loaded, 16)

            def load(b):
                for m in range(NC):
                    wait(sp, hnew_ready, b * (2 * NC))
                    sp.dma_start(hb[m][:, :, :], one(hin, b * NC + m)).then_inc(h_loaded[m], 16)

            def turn(b):
                load(b)
                for m in range(NC):
                    wait(sp, hnew_ready, b * (2 * NC) + 2 * m + 2)
                    sp.dma_start(one(hout, b * NC + m), h_new[m % 2][:, :, :]).then_inc(stored[m % 2], 16)

            repeat(sp, batches, turn)
            for s in range(2):
                sp.wait_ge(stored[s], 16 * chunks // 2)

        @block.gpsimd
        def _(pool):
            nc.gpsimd.memset(lower[:, :, :], 1.0).then_inc(lower_step, 1)
            pool.wait_ge(lower_step, 1)
            nc.gpsimd.affine_select(out=lower[:, :, :], in_=lower[:, :, :], compare_op=ALU.is_gt, fill=0.0, base=0,
                                    pattern=[[1, E], [-1, E]], channel_multiplier=0).then_inc(lower_step, 1)
            def turn(b):
                for m in range(NC):
                    c = b * NC + m
                    wait(pool, stats_ready, c + 1)
                    wait(pool, xh_ready, c)
                    nc.gpsimd.tensor_tensor(rstd[:, :], mv[:, :, 1], core.eps[:, 0:mv.shape[1]], ALU.add).then_inc(var_eps, 1)
                    wait(pool, var_eps, c + 1)
                    nc.gpsimd.tensor_tensor(rstd[:, :], rstd[:, :], core.neg_half[:, 0:TJ],
                                            ALU.pow).then_inc(rstd_ready, 1)

            repeat(pool, batches, turn)

        @block.vector
        def _(dve):
            dve.wait_ge(loaded, 9 * 16)
            dve.wait_ge(lower_step, 2)
            def turn(b):
                for m in range(NC):
                    c = b * NC + m
                    wait(dve, h_loaded[m], b * 16 + 16)
                    for j in range(TJ):
                        last = nc.vector.bn_stats(bn[:, j, :], hb[m][:, j, :])
                    last.then_inc(bn_done, 1)
                    wait(dve, bn_done, c + 1)
                    wait(dve, rstd_ready, c)
                    hold(dve, passed)
                    for j in range(TJ):
                        last = nc.vector.bn_aggr(mv[:, j, :], bn[:, j, :])
                    last.then_inc(stats_ready, 1)
                    wait(dve, stats_ready, c + 1)
                    wait(dve, rstd_ready, c + 1)
                    if m >= 2:
                        wait(dve, xT_psum, b * (2 * NC) + 2 * (m - 1))
                    else:
                        wait(dve, xT_psum, b * (2 * NC))
                    for j in range(TJ):
                        last = nc.vector.tensor_scalar(xh[m % 2][:, j, :], hb[m][:, j, :], mv[:, j, 0:1],
                                                       rstd[:, j:j + 1], ALU.subtract, ALU.mult)
                    last.then_inc(xh_ready, 1)

                steps = [0]

                def step(ins):
                    ins.then_inc(gate_step, 1)
                    steps[0] += 1
                    wait(dve, gate_step, b * GATE_STEPS + steps[0])

                wait(dve, xT_ready, b * (2 * NC) + 2 * NC)
                wait(dve, gate_psum, b)
                step(nc.vector.tensor_reduce(pooled[:, :], sums[:, :, :], AX.X, ALU.add))
                for k in range(2):
                    last = nc.vector.tensor_scalar(pooled_b[:, k, :], core.ones[:, :], pooled[:, k:k + 1], 1.0 / S,
                                                   ALU.mult, ALU.mult)
                last.then_inc(pooled_ready, 1)
                wait(dve, gate_psum, b + 1)
                step(nc.vector.tensor_reduce(small[:, 0:1], bank[2][:, 0:E], AX.X, ALU.max, negate=True))
                wait(dve, gate_exp, b + 1)
                step(nc.vector.reciprocal(small[:, 2:3], small[:, 1:2]))
                step(nc.vector.tensor_scalar(g8[:, :], g8[:, :], small[:, 2:3], None, ALU.mult))
                g_of_j = g8[:, :].unsqueeze(1).to_broadcast([P, E, E])
                g_of_e = g8[:, :].unsqueeze(2).to_broadcast([P, E, E])
                nc.vector.tensor_tensor(cmp_a[:, :, :], g_of_j, g_of_e, ALU.is_gt)
                step(nc.vector.tensor_tensor(cmp_b[:, :, :], g_of_j, g_of_e, ALU.is_equal))
                step(nc.vector.tensor_tensor(cmp_b[:, :, :], cmp_b[:, :, :], lower[:, :, :], ALU.mult))
                step(nc.vector.tensor_tensor(cmp_a[:, :, :], cmp_a[:, :, :], cmp_b[:, :, :], ALU.add))
                step(nc.vector.tensor_reduce(rank[:, :], cmp_a[:, :, :], AX.X, ALU.add))
                for k in range(2):
                    last = nc.vector.tensor_scalar(sel[:, k, :], rank[:, :], float(k), None, ALU.is_equal)
                step(last)
                step(nc.vector.tensor_tensor(selg[:, :, :], sel[:, :, :], g8[:, :].unsqueeze(1).to_broadcast([P, 2, E]),
                                             ALU.mult))
                step(nc.vector.tensor_reduce(small[:, 3:5], selg[:, :, :], AX.X, ALU.add))
                step(nc.vector.tensor_tensor(small[:, 5:6], small[:, 3:4], small[:, 4:5], ALU.add))
                step(nc.vector.tensor_scalar(small[:, 5:6], small[:, 5:6], 1e-8, None, ALU.add))
                step(nc.vector.reciprocal(small[:, 6:7], small[:, 5:6]))
                step(nc.vector.tensor_scalar(selg[:, :, :], selg[:, :, :], small[:, 6:7], None, ALU.mult))
                step(nc.vector.tensor_tensor(wsum[:, :], selg[:, 0, :], selg[:, 1, :], ALU.add))
                for k in range(2):
                    nc.vector.tensor_copy(rows[k * C:(k + 1) * C, 0, :], sel[k * C:(k + 1) * C, k, :])
                    last = nc.vector.tensor_copy(rows[k * C:(k + 1) * C, 1, :], selg[k * C:(k + 1) * C, k, :])
                step(last)
                wait(dve, up_psum, b * (2 * NC))
                wait(dve, hid_ready, b * NC)
                for e in range(E):
                    for k in range(2):
                        if e == 0:
                            ins = nc.vector.tensor_scalar(wd[:, :, k, :], dw[:, :, e, :], sel[:, k, e:e + 1], None, ALU.mult)
                        else:
                            ins = nc.vector.scalar_tensor_tensor(wd[:, :, k, :], dw[:, :, e, :], sel[:, k, e:e + 1],
                                                                 wd[:, :, k, :], ALU.mult, ALU.add)
                        step(ins)
                    if e == 0:
                        ins = nc.vector.tensor_scalar(wu[:, :], uw[:, e, :], rows[:, 1, e:e + 1], None, ALU.mult)
                    else:
                        ins = nc.vector.scalar_tensor_tensor(wu[:, :], uw[:, e, :], rows[:, 1, e:e + 1], wu[:, :],
                                                             ALU.mult, ALU.add)
                    step(ins)
                step(nc.vector.tensor_tensor(prod[:, :], rows[:, 0, :], db[:, :], ALU.mult))
                assert steps[0] == GATE_STEPS, steps
                nc.vector.tensor_reduce(bsel[:, :], prod[:, :], AX.X, ALU.add).then_inc(chosen, 1)
                wait(dve, wsum_psum, b + 1)
                nc.vector.tensor_copy(wsumT[:, :], bank[2][0:E, P:2 * P]).then_inc(chosen, 1)

                for m in range(NC):
                    wait(dve, stored[m % 2], b * (8 * NC) + 16 * (m // 2))
                    for r in range(2):
                        wait(dve, up_psum, b * (2 * NC) + 2 * m + r + 1)
                        nc.vector.tensor_tensor(h_new[m % 2][:, 2 * r:2 * r + 2, :],
                                                bank[5 + r][:, :].rearrange("p (j d) -> p j d", j=2),
                                                hb[m][:, 2 * r:2 * r + 2, :], ALU.add).then_inc(hnew_ready, 1)

            repeat(dve, batches, turn)

        @block.scalar
        def _(act):
            def turn(b):
                for m in range(NC):
                    for f in range(2):
                        wait(act, xT_psum, b * (2 * NC) + 2 * m + f + 1)
                        if m == 0:
                            wait(act, hid_psum, b * NC)
                            wait(act, pooled_ready, b)
                        nc.scalar.activation(xT[:, f, m * T:(m + 1) * T], bank[f][:, :], ACT.Copy,
                                             accum_out=sums[:, f, m:m + 1]).then_inc(xT_ready, 1)
                wait(act, gate_step, b * GATE_STEPS + 2)
                wait(act, wsum_psum, b)
                nc.scalar.activation(g8[:, :], bank[2][:, 0:E], ACT.Exp, bias=small[:, 0:1],
                                     accum_out=small[:, 1:2]).then_inc(gate_exp, 1)
                wait(act, chosen, b * 2 + 1)
                for m in range(NC):
                    wait(act, hid_psum, b * NC + m + 1)
                    wait(act, up_psum, b * (2 * NC) + 2 * max(m - 1, 0))
                    nc.scalar.activation(hid[m % 2][:, :], bank[3 + m % 2][:, :], ACT.Gelu,
                                         bias=bsel[:, :]).then_inc(hid_ready, 1)

            repeat(act, batches, turn)

        @block.tensor
        def _(pe):
            pe.wait_ge(loaded, 9 * 16)
            def turn(b):
                for m in range(NC):
                    wait(pe, xh_ready, b * NC + m + 1)
                    for f in range(2):
                        if m:
                            wait(pe, xT_ready, b * (2 * NC) + 2 * m + f - 1)
                        else:
                            wait(pe, xT_ready, b * (2 * NC))
                        for j in range(TJ):
                            last = nc.tensor.transpose(bank[f][:, j * P:(j + 1) * P],
                                                       xh[m % 2][:, j, f * P:(f + 1) * P], core.ident[:, :])
                        last.then_inc(xT_psum, 1)
                wait(pe, pooled_ready, b + 1)
                wait(pe, chosen, b * 2)
                for k in range(2):
                    last = nc.tensor.matmul(bank[2][:, 0:E], pooled_b[:, k, :], gw[:, k, :], start=(k == 0),
                                            stop=(k == 1))
                last.then_inc(gate_psum, 1)
                wait(pe, gate_step, b * GATE_STEPS + 16)
                nc.tensor.transpose(bank[2][0:E, P:2 * P], wsum[:, :], core.ident[:, :]).then_inc(wsum_psum, 1)
                wait(pe, chosen, b * 2 + 2)
                for m in range(NC + 1):
                    if m < NC:
                        wait(pe, hid_ready, b * NC + max(m - 1, 0))
                        for k in range(2):
                            last = nc.tensor.matmul(bank[3 + m % 2][:, :], wd[:, k, :, :].rearrange("p k c -> p (k c)"),
                                                    xT[:, k, m * T:(m + 1) * T], start=(k == 0), stop=(k == 1))
                        last.then_inc(hid_psum, 1)
                    if m == 0:
                        continue
                    u = m - 1
                    wait(pe, hid_ready, b * NC + u + 1)
                    for r in range(2):
                        wait(pe, hnew_ready, b * (2 * NC) + max(2 * u + r - 1, 0))
                        for j in range(2):
                            t0 = (2 * r + j) * P
                            nc.tensor.matmul(bank[5 + r][:, j * D:(j + 1) * D], hid[u % 2][:, t0:t0 + P], wu[:, :],
                                             start=True, stop=False)
                            last = nc.tensor.matmul(bank[5 + r][:, j * D:(j + 1) * D], wsumT[:, :], ub[:, :],
                                                    start=False, stop=True)
                        last.then_inc(up_psum, 1)

            repeat(pe, batches, turn)


def ssm_phase(core, w, h_in, h_out):
    nc, bank, chunks = core.nc, core.bank, core.chunks
    N = w["A_log"].shape[1]
    FB = w["ff1_w"].shape[1] // P
    R = 3 * 2 * N
    AHEAD = 2
    FF2_AT = (N - 2, N, N + 1, N + 2)
    LATE = N + 2
    RING = 4
    with ExitStack() as ctx:
        def sb(name, shape, dt=F32):
            return ctx.enter_context(nc.sbuf_tensor("s_" + name, shape, dt))

        def sem(name):
            return nc.alloc_semaphore(name="s_" + name)

        passed = sem("passed")

        mats = {name: sb(name, [P, 2, D]) for name in ("w1_w", "v1_w", "w2_w", "dt_w")}
        ff1 = sb("ff1", [P, 2, FB * P])
        ff2 = sb("ff2", [P, FB, D])
        bcw = sb("bcw", [P, 2, 3, 2 * N])
        bcb = sb("bcb", [R, 1])
        cols = {name: sb(name, [P, 2]) for name in ("ln_g", "ln_b", "w1_b", "v1_b", "dt_b", "D_p", "ln2_g", "ln2_b")}
        half_v1b = sb("half_v1b", [P, 2])
        conv = sb("conv", [P, 2, 3])
        half_conv = sb("half_conv", [P, 2, 3])
        ff1b = sb("ff1b", [P, FB])
        A_log = sb("A_log", [P, 2, N])
        A = sb("A", [P, 2, N])
        A_neg = sb("A_neg", [P, 2, N])
        g1 = sb("g1", [P, D])
        b1 = sb("b1", [P, D])
        w2b = sb("w2b", [P, D])
        endb = sb("endb", [P, D])
        pick = sb("pick", [R, 2 * N], BF16)

        hb = [sb(f"hb{q}", [P, TJ + 1, D]) for q in range(2)]
        bn = sb("bn", [P, TJ + 1, 6])
        mv = sb("mv", [P, TJ + 1, 2])
        rstd = sb("rstd", [P, TJ + 1])
        rstd_n = sb("rstd_n", [P, TJ + 1])
        xh = sb("xh", [P, TJ + 1, D])
        xn = sb("xn", [P, TJ + 1, D])
        xres = [sb(f"xres{q}", [P, TJ, D]) for q in range(2)]
        hres = sb("hres", [P, TJ, D])
        xmT = sb("xmT", [P, 2, T + 1])
        x1 = sb("x1", [P, 2, T + 2])
        after = sb("after", [P, 2])
        cv = sb("cv", [P, 2, T])
        th = sb("th", [P, 2, T])
        xc = [sb(f"xc{q}", [P, 2, T]) for q in range(2)]
        xs = sb("xs", [P, 2, T])
        dt = [sb(f"dt{q}", [P, 2, T]) for q in range(2)]
        dtx = [sb(f"dtx{q}", [P, 2, T]) for q in range(2)]
        vg = [sb(f"vg{q}", [P, 2, T]) for q in range(2)]
        bcf = sb("bcf", [R, T])
        bcs = [sb(f"bcs{q}", [R, T], BF16) for q in range(2)]
        a = [sb(f"a{s}", [P, 2, T]) for s in range(RING)]
        hs = [sb(f"hs{s}", [P, 2, T]) for s in range(RING)]
        bs = [sb(f"bs{s}", [P, T]) for s in range(2)]
        cs = [sb(f"cs{s}", [P, T]) for s in range(RING)]
        zlast = sb("zlast", [P, N, 2])
        carry = sb("carry", [P, N, 2])
        yv = sb("yv", [P, 2, T])
        x2 = sb("x2", [P, TJ, D])
        bn2 = sb("bn2", [P, TJ, 6])
        mv2 = sb("mv2", [P, TJ, 2])
        rstd2 = sb("rstd2", [P, TJ])
        xn2 = sb("xn2", [P, TJ, D])
        xn2T = sb("xn2T", [P, 2, T])
        hid = sb("hid", [P, FB, T])
        h_new = sb("h_new", [P, TJ, D])

        bB, bC, yp, tp, mm = bank[0], bank[1], bank[2:4], bank[4:6], bank[6:8]

        loaded, pick_step, cleared, consts, A_done = (
            sem("loaded"), sem("pick_step"), sem("cleared"), sem("consts"), sem("A_done"))
        h_loaded = [sem(f"h_loaded{q}") for q in range(2)]
        bn_done, stats_ready, rstd_step, xh_ready, xn_ready, affine_ready, res_ready = (
            sem("bn_done"), sem("stats_ready"), sem("rstd_step"), sem("xh_ready"), sem("xn_ready"),
            sem("affine_ready"), sem("res_ready"))
        bnn_done, statsn_ready, xm_ready = sem("bnn_done"), sem("statsn_ready"), sem("xm_ready")
        xmT_psum, xmT_ready = sem("xmT_psum"), sem("xmT_ready")
        x1carry_ready, x1_psum, x1_ready, x1after_ready = (
            sem("x1carry_ready"), sem("x1_psum"), sem("x1_ready"), sem("x1after_ready"))
        conv_step, th_ready, xc_ready = sem("conv_step"), sem("th_ready"), sem("xc_ready")
        dt_psum, xs_ready, na_ready, ln1p_step, dt_ready, dtx_ready = (
            sem("dt_psum"), sem("xs_ready"), sem("na_ready"), sem("ln1p_step"), sem("dt_ready"), sem("dtx_ready"))
        bc_psum, bcf_ready, part_ready, rest_ready = sem("bc_psum"), sem("bcf_ready"), sem("part_ready"), sem("rest_ready")
        vg_psum, vb_ready, vth_ready, vg_ready = sem("vg_psum"), sem("vb_ready"), sem("vth_ready"), sem("vg_ready")
        B_psum, C_psum, u_ready, bs_ready, cs_ready, a_ready = (
            sem("B_psum"), sem("C_psum"), sem("u_ready"), sem("bs_ready"), sem("cs_ready"), sem("a_ready"))
        hres_loaded = sem("hres_loaded")
        scan_done = [sem(f"scan_done{f}") for f in range(2)]
        zlast_saved, g_ready, red_done = sem("zlast_saved"), sem("g_ready"), sem("red_done")
        carry_ready = [sem(f"carry_ready{m}") for m in range(2)]
        y_ready, yv_ready, mo_psum, x2_ready = sem("y_ready"), sem("yv_ready"), sem("mo_psum"), sem("x2_ready")
        bn2_done, stats2_ready, rstd2_step, xn2_ready, x2res_ready = (
            sem("bn2_done"), sem("stats2_ready"), sem("rstd2_step"), sem("xn2_ready"), sem("x2res_ready"))
        xn2T_psum, xn2T_ready, ff1_psum, hid_ready, ff2_psum, hnew_ready, h_stored = (
            sem("xn2T_psum"), sem("xn2T_ready"), sem("ff1_psum"), sem("hid_ready"), sem("ff2_psum"),
            sem("hnew_ready"), sem("h_stored"))
        block = ctx.enter_context(nc.Block())
        hin, hout = chunk_view(h_in), chunk_view(h_out)
        CONST = 3

        loads = []
        for name in ("w1_w", "v1_w", "w2_w", "dt_w"):
            loads.append((mats[name][:, :, :], w[name].rearrange("(k p) n -> p k n", p=P)))
        loads.append((ff1[:, :, :], w["ff1_w"].rearrange("(k p) n -> p k n", p=P)))
        loads.append((ff2[:, :, :], w["ff2_w"].rearrange("(k p) n -> p k n", p=P)))
        for part in range(3):
            for m, name in enumerate(("Bp", "Cp")):
                loads.append((bcw[:, :, part, m * N:(m + 1) * N], w[name + "_w"].rearrange("(k p) n -> p k n", p=P)))
                r0 = (2 * part + m) * N
                loads.append((bcb[r0:r0 + N, :], w[name + "_b"]))
        for name in cols:
            loads.append((cols[name][:, :], w[name]))
        loads.append((conv[:, :, :], w["conv_w"].rearrange("(k p) o x -> p k (o x)", p=P)))
        loads.append((ff1b[:, :], w["ff1_b"]))
        loads.append((A_log[:, :, :], w["A_log"].rearrange("(k p) n -> p k n", p=P)))
        for tile, name in ((g1[:, :], "ln1_g"), (b1[:, :], "ln1_b"), (w2b[:, :], "w2_b"), (endb[:, :], "ff2_b"), (hres[:, 0, :], "moe_bias")):
            loads.append((tile, w[name].partition_broadcast(P)))
        LOADED = 16 * len(loads)

        @block.sync
        def _(sp):
            for dst, src in loads:
                sp.dma_start(dst, src).then_inc(loaded, 16)

            def load(fc, fq):
                wait(sp, xh_ready, fc - 1)
                sp.dma_start(hb[fq][:, 0:TJ, :], one(hin, fc)).then_inc(h_loaded[fq], 16)
                nxt = one(hin, (fc + 1) % chunks)
                sp.dma_start(hb[fq][0:1, TJ, :], nxt[0:1, 0, :]).then_inc(h_loaded[fq], 16)

            def store(c):
                sp.wait_ge(hnew_ready, c * 2 + 2)
                sp.dma_start(one(hout, c), h_new[:, :, :]).then_inc(h_stored, 16)

            def reload(c):
                wait(sp, x2res_ready, c * 2)
                if isinstance(c, int) and c == 0:
                    sp.wait_ge(consts, 3)
                sp.dma_start(hres[:, :, :], one(hin, c)).then_inc(hres_loaded, 16)

            def body(c, q, first, last):
                if not last:
                    load(c + 1, 1 - q)
                if not first:
                    reload(c - 1)
                if past(c, 2):
                    store(c - 2)

            sweep(sp, chunks, load, body)
            reload(chunks - 1)
            store(chunks - 2)
            store(chunks - 1)
            sp.wait_ge(h_stored, 16 * chunks)

        @block.gpsimd
        def _(pool):
            nc.gpsimd.memset(pick[:, :], 0.0).then_inc(pick_step, 1)
            for part in range(3):
                pool.wait_ge(pick_step, part + 1)
                nc.gpsimd.affine_select(out=pick[:, :], in_=pick[:, :], compare_op=ALU.not_equal, fill=1.0,
                                        base=-2 * N * part, pattern=[[-1, 2 * N]],
                                        channel_multiplier=1).then_inc(pick_step, 1)
            pool.wait_ge(pick_step, 4)
            nc.gpsimd.memset(mv[:, :, :], 1.0).then_inc(cleared, 1)
            nc.gpsimd.memset(x1[:, :, :], 0.0).then_inc(cleared, 1)
            nc.gpsimd.memset(zlast[:, :, :], 0.0).then_inc(cleared, 1)
            pool.wait_ge(cleared, 3)
            pool.wait_ge(loaded, LOADED)
            nc.gpsimd.tensor_tensor(endb[:, :], endb[:, :], hres[:, 0, :], ALU.add).then_inc(consts, 1)
            nc.gpsimd.tensor_scalar(half_v1b[:, :], cols["v1_b"][:, :], 0.5, None, ALU.mult).then_inc(consts, 1)
            nc.gpsimd.tensor_scalar(half_conv[:, :, :], conv[:, :, :], 0.5, None, ALU.mult).then_inc(consts, 1)
            pool.wait_ge(consts, 3)

            def front(fc, fq, k=None):
                if k in (None, 0):
                    pool.wait_ge(stats_ready, fc + 1)
                    wait(pool, xn_ready, fc)
                    wait(pool, xm_ready, fc)
                    base = fc * 8
                    seq = [
                        lambda: nc.gpsimd.tensor_tensor(rstd[:, :], mv[:, :, 1], core.eps[:, 0:mv.shape[1]], ALU.add),
                        lambda: nc.gpsimd.tensor_tensor(rstd[:, :], rstd[:, :], core.neg_half[:, 0:TJ + 1], ALU.pow),
                        lambda: nc.gpsimd.tensor_tensor(rstd_n[:, :], mv[:, :, 1], rstd[:, :], ALU.mult),
                        lambda: nc.gpsimd.tensor_tensor(rstd_n[:, :], rstd_n[:, :], rstd[:, :], ALU.mult),
                        lambda: nc.gpsimd.tensor_tensor(rstd_n[:, :], rstd_n[:, :], core.eps[:, 0:TJ + 1], ALU.add),
                        lambda: nc.gpsimd.tensor_tensor(rstd_n[:, :], rstd_n[:, :], core.neg_half[:, 0:TJ + 1], ALU.pow),
                    ]
                    for m, op in enumerate(seq):
                        op().then_inc(rstd_step, 1)
                        if m + 1 < len(seq):
                            pool.wait_ge(rstd_step, base + m + 1)
                if k in (None, 1):
                    pool.wait_ge(xn_ready, fc + 1)
                    nc.gpsimd.tensor_tensor(xn[:, 0:TJ, :], xn[:, 0:TJ, :],
                                            b1[:, :].unsqueeze(1).to_broadcast([P, TJ, D]), ALU.add)
                    nc.gpsimd.tensor_tensor(xn[0:1, TJ, :], xn[0:1, TJ, :], b1[0:1, :], ALU.add).then_inc(affine_ready, 1)
                if k in (None, 5):
                    wait(pool, x2_ready, (fc - 1) * 2)
                    nc.gpsimd.tensor_tensor(xres[fq][:, :, :], xh[:, 0:TJ, :],
                                            w2b[:, :].unsqueeze(1).to_broadcast([P, TJ, D]), ALU.add).then_inc(res_ready, 1)
                if k in (None, 2):
                    pool.wait_ge(statsn_ready, fc + 1)
                    nc.gpsimd.tensor_tensor(rstd_n[:, :], mv[:, :, 1], core.eps[:, 0:mv.shape[1]], ALU.add).then_inc(rstd_step, 1)
                    pool.wait_ge(rstd_step, fc * 8 + 7)
                    nc.gpsimd.tensor_tensor(rstd_n[:, :], rstd_n[:, :], core.neg_half[:, 0:TJ + 1],
                                            ALU.pow).then_inc(rstd_step, 1)

            def fin(c, q, k):
                if k == 3:
                    pool.wait_ge(stats2_ready, c + 1)
                    wait(pool, xn2_ready, c)
                    nc.gpsimd.tensor_tensor(rstd2[:, :], mv2[:, :, 1], core.eps[:, 0:mv2.shape[1]], ALU.add).then_inc(rstd2_step, 1)
                    pool.wait_ge(rstd2_step, c * 2 + 1)
                    nc.gpsimd.tensor_tensor(rstd2[:, :], rstd2[:, :], core.neg_half[:, 0:TJ],
                                            ALU.pow).then_inc(rstd2_step, 1)
                if k == 4:
                    pool.wait_ge(xn2_ready, c + 1)
                    pool.wait_ge(hres_loaded, c * 16 + 16)
                    nc.gpsimd.tensor_tensor(x2[:, :, :], x2[:, :, :], hres[:, :, :], ALU.add).then_inc(x2res_ready, 1)
                if k == 6:
                    pool.wait_ge(x2res_ready, c * 2 + 1)
                    nc.gpsimd.tensor_tensor(x2[:, :, :], x2[:, :, :], endb[:, :].unsqueeze(1).to_broadcast([P, TJ, D]),
                                            ALU.add).then_inc(x2res_ready, 1)

            def body(c, q, first, last):
                for n in range(N):
                    for f in range(2):
                        pool.wait_ge(scan_done[f], c * N + n + 1)
                    if n in (0, 8):
                        pool.wait_ge(carry_ready[n // 8], c + 1)
                    hold(pool, passed)
                    nc.gpsimd.tensor_copy(zlast[:, n, :], hs[n % RING][:, :, T - 1]).then_inc(zlast_saved, 1)
                    pool.wait_ge(zlast_saved, c * N + n + 1)
                    pool.wait_ge(cs_ready, c * N + n + 1)
                    nc.gpsimd.tensor_tensor(hs[n % RING][:, :, :], hs[n % RING][:, :, :],
                                            cs[n % RING][:, :].unsqueeze(1).to_broadcast([P, 2, T]),
                                            ALU.mult).then_inc(g_ready, 1)
                    if past(c, 2):
                        fin(c - 2, q, N + n)
                    if not first:
                        fin(c - 1, 1 - q, n)
                    if not last:
                        front(c + 1, 1 - q, n)

            sweep(pool, chunks, front, body)
            for k in range(2 * N):
                fin(chunks - 2, 0, N + k)
                fin(chunks - 1, 1, k)

        @block.vector
        def _(dve):
            dve.wait_ge(loaded, LOADED)
            dve.wait_ge(consts, CONST)
            dve.wait_ge(A_done, 1)
            nc.vector.tensor_scalar(A_neg[:, :, :], A[:, :, :], -1.0, None, ALU.mult).then_inc(A_done, 1)

            def tiles(t, j):
                return t[:, j, :] if j < TJ else t[0:1, j, :]

            def front(fc, fq, k=None):
                if k in (None, 0):
                    dve.wait_ge(h_loaded[fq], (fc - fq) * 16 + 32)
                    wait(dve, statsn_ready, fc)
                    for j in range(TJ + 1):
                        last = nc.vector.bn_stats(tiles(bn, j), tiles(hb[fq], j))
                    last.then_inc(bn_done, 1)
                    dve.wait_ge(bn_done, fc + 1)
                    wait(dve, rstd_step, fc * 8)
                    hold(dve, passed)
                    for j in range(TJ + 1):
                        last = nc.vector.bn_aggr(tiles(mv, j), tiles(bn, j))
                    last.then_inc(stats_ready, 1)
                if k in (None, 1):
                    dve.wait_ge(stats_ready, fc + 1)
                    dve.wait_ge(rstd_step, fc * 8 + 6)
                    wait(dve, res_ready, fc)
                    wait(dve, xmT_psum, fc * 3)
                    for j in range(TJ + 1):
                        one_row = slice(0, P if j < TJ else 1)
                        last = nc.vector.tensor_scalar(tiles(xh, j), tiles(hb[fq], j), mv[one_row, j, 0:1],
                                                       rstd[one_row, j:j + 1], ALU.subtract, ALU.mult)
                    last.then_inc(xh_ready, 1)
                    dve.wait_ge(xh_ready, fc + 1)
                    for j in range(TJ + 1):
                        one_row = slice(0, P if j < TJ else 1)
                        last = nc.vector.scalar_tensor_tensor(tiles(xn, j), tiles(xh, j), rstd_n[one_row, j:j + 1],
                                                              g1[one_row, :], ALU.mult, ALU.mult)
                    last.then_inc(xn_ready, 1)
                if k in (None, 2):
                    dve.wait_ge(affine_ready, fc + 1)
                    for j in range(TJ + 1):
                        last = nc.vector.bn_stats(tiles(bn, j), tiles(xn, j))
                    last.then_inc(bnn_done, 1)
                    dve.wait_ge(bnn_done, fc + 1)
                    hold(dve, passed)
                    for j in range(TJ + 1):
                        last = nc.vector.bn_aggr(tiles(mv, j), tiles(bn, j))
                    last.then_inc(statsn_ready, 1)
                if k in (None, 3):
                    dve.wait_ge(statsn_ready, fc + 1)
                    dve.wait_ge(rstd_step, fc * 8 + 8)
                    for j in range(TJ + 1):
                        one_row = slice(0, P if j < TJ else 1)
                        last = nc.vector.tensor_scalar(tiles(xn, j), tiles(xn, j), mv[one_row, j, 0:1],
                                                       rstd_n[one_row, j:j + 1], ALU.subtract, ALU.mult)
                    last.then_inc(xm_ready, 1)
                if k in (None, 5):
                    wait(dve, x1_ready, fc * 3)
                    wait(dve, conv_step, fc * 3)
                    nc.vector.tensor_scalar(x1[:, :, 0:1], x1[:, :, T:T + 1], core.keep[:, bass.ds(fc, 1)], None,
                                            ALU.mult).then_inc(x1carry_ready, 1)
                if k in (None, 6):
                    dve.wait_ge(x1_ready, fc * 3 + 3)
                    dve.wait_ge(x1carry_ready, fc + 1)
                    nc.vector.tensor_scalar(x1[:, :, T + 1:T + 2], after[:, :].unsqueeze(2),
                                            core.keep[:, bass.ds(fc + 1, 1)], None, ALU.mult).then_inc(x1after_ready, 1)
                    dve.wait_ge(x1after_ready, fc + 1)
                    wait(dve, xc_ready, fc)
                    for f in range(2):
                        last = nc.vector.tensor_scalar(cv[:, f, :], x1[:, f, 0:T], half_conv[:, f, 0:1], None, ALU.mult)
                    last.then_inc(conv_step, 1)
                    for m in range(1, 3):
                        dve.wait_ge(conv_step, fc * 3 + m)
                        for f in range(2):
                            last = nc.vector.scalar_tensor_tensor(cv[:, f, :], x1[:, f, m:m + T], half_conv[:, f, m:m + 1],
                                                                  cv[:, f, :], ALU.mult, ALU.add)
                        last.then_inc(conv_step, 1)
                if k in (None, 8):
                    dve.wait_ge(th_ready, fc + 1)
                    wait(dve, y_ready, fc - 1)
                    nc.vector.scalar_tensor_tensor(xc[fq][:, :, :], th[:, :, :], 1.0, cv[:, :, :], ALU.add,
                                                   ALU.mult).then_inc(xc_ready, 1)
                if k in (None, 10):
                    dve.wait_ge(xs_ready, fc * 2 + 2)
                    wait(dve, dt_ready, fc)
                    dve.wait_ge(xc_ready, fc + 1)
                    nc.vector.scalar_tensor_tensor(cv[:, :, :], xs[:, :, :], -1.0, xs[:, :, :], ALU.mult,
                                                   ALU.min).then_inc(na_ready, 1)
                if k in (None, 11):
                    dve.wait_ge(ln1p_step, fc * 2 + 2)
                    wait(dve, a_ready, (fc - 1) * N)
                    nc.vector.scalar_tensor_tensor(dt[fq][:, :, :], xs[:, :, :], 0.0, cv[:, :, :], ALU.max,
                                                   ALU.add).then_inc(dt_ready, 1)
                    dve.wait_ge(dt_ready, fc + 1)
                    nc.vector.tensor_tensor(dtx[fq][:, :, :], dt[fq][:, :, :], xc[fq][:, :, :],
                                            ALU.mult).then_inc(dtx_ready, 1)
                if k in (None, 12):
                    dve.wait_ge(part_ready, fc * 3 + 1)
                    lo = 2 * N
                    nc.vector.tensor_tensor(bcf[lo:2 * lo, :], bcf[lo:2 * lo, :], bcs[fq][lo:2 * lo, :], ALU.subtract)
                    nc.vector.tensor_tensor(bcf[2 * lo:R, :], bcf[2 * lo:R, :], bcs[fq][2 * lo:R, :],
                                            ALU.subtract).then_inc(rest_ready, 1)
                if k in (None, 13):
                    dve.wait_ge(vth_ready, fc + 1)
                    wait(dve, yv_ready, fc - 1)
                    nc.vector.scalar_tensor_tensor(vg[fq][:, :, :], th[:, :, :], 1.0, cv[:, :, :], ALU.add,
                                                   ALU.mult).then_inc(vg_ready, 1)
                if k in (None, 14):
                    dve.wait_ge(part_ready, fc * 3 + 2)
                    lo = 4 * N
                    nc.vector.tensor_tensor(bcf[lo:R, :], bcf[lo:R, :], bcs[fq][lo:R, :],
                                            ALU.subtract).then_inc(rest_ready, 1)

            def fin(c, q, k):
                if k == 1:
                    dve.wait_ge(red_done, (c + 1) * N)
                    wait(dve, mo_psum, c * 2)
                    for f in range(2):
                        ins = nc.vector.scalar_tensor_tensor(yv[:, f, :], xc[q][:, f, :], cols["D_p"][:, f:f + 1],
                                                             yp[f][:, :], ALU.mult, ALU.add)
                    ins.then_inc(y_ready, 1)
                    dve.wait_ge(y_ready, c + 1)
                    nc.vector.tensor_tensor(yv[:, :, :], yv[:, :, :], vg[q][:, :, :], ALU.mult).then_inc(yv_ready, 1)
                if k == 3:
                    wait(dve, hnew_ready, c * 2)
                    dve.wait_ge(res_ready, c + 1)
                    for m in range(2):
                        dve.wait_ge(mo_psum, c * 2 + m + 1)
                        nc.vector.tensor_tensor(x2[:, 2 * m:2 * m + 2, :], mm[m][:, :].rearrange("p (j d) -> p j d", j=2),
                                                xres[q][:, 2 * m:2 * m + 2, :], ALU.add).then_inc(x2_ready, 1)
                    dve.wait_ge(x2_ready, c * 2 + 2)
                    for j in range(TJ):
                        ins = nc.vector.bn_stats(bn2[:, j, :], x2[:, j, :])
                    ins.then_inc(bn2_done, 1)
                    dve.wait_ge(bn2_done, c + 1)
                    wait(dve, rstd2_step, c * 2)
                    hold(dve, passed)
                    for j in range(TJ):
                        ins = nc.vector.bn_aggr(mv2[:, j, :], bn2[:, j, :])
                    ins.then_inc(stats2_ready, 1)
                if k == 4:
                    dve.wait_ge(stats2_ready, c + 1)
                    dve.wait_ge(rstd2_step, c * 2 + 2)
                    wait(dve, xn2T_psum, c * 2)
                    for j in range(TJ):
                        ins = nc.vector.tensor_scalar(xn2[:, j, :], x2[:, j, :], mv2[:, j, 0:1], rstd2[:, j:j + 1],
                                                      ALU.subtract, ALU.mult)
                    ins.then_inc(xn2_ready, 1)
                if k == LATE + 1:
                    wait(dve, h_stored, c * 16)
                    dve.wait_ge(x2res_ready, c * 2 + 2)
                    for m in range(2):
                        dve.wait_ge(ff2_psum, c * 2 + m + 1)
                        nc.vector.tensor_tensor(h_new[:, 2 * m:2 * m + 2, :],
                                                tp[m][:, :].rearrange("p (j d) -> p j d", j=2),
                                                x2[:, 2 * m:2 * m + 2, :], ALU.add).then_inc(hnew_ready, 1)

            def carry_half(c, m):
                wait(dve, zlast_saved, (c - 1) * N + N // 2 if m == 0 else c * N)
                nc.vector.tensor_scalar(carry[:, m * 8:(m + 1) * 8, :], zlast[:, m * 8:(m + 1) * 8, :],
                                        core.keep[:, bass.ds(c, 1)], None, ALU.mult).then_inc(carry_ready[m], 1)

            def body(c, q, first, last):
                for n in range(N):
                    s = n % RING
                    if n in (0, 8):
                        dve.wait_ge(carry_ready[n // 8], c + 1)
                    if n == 0:
                        dve.wait_ge(dtx_ready, c + 1)
                    dve.wait_ge(bs_ready, c * N + n + 1)
                    wait(dve, red_done, c * N + n - RING + 1)
                    nc.vector.tensor_tensor(hs[s][:, :, :], dtx[q][:, :, :], bs[n % 2][:, :].unsqueeze(1).to_broadcast([P, 2, T]),
                                            ALU.mult).then_inc(u_ready, 1)
                    dve.wait_ge(u_ready, c * N + n + 1)
                    dve.wait_ge(a_ready, c * N + n + 1)
                    for f in range(2):
                        nc.vector.tensor_tensor_scan(hs[s][:, f, :], a[s][:, f, :], hs[s][:, f, :], carry[:, n, f:f + 1],
                                                     ALU.mult, ALU.add).then_inc(scan_done[f], 1)
                    if past(c, 2):
                        fin(c - 2, q, N + n)
                    if not first:
                        fin(c - 1, 1 - q, n)
                    if n == 4:
                        carry_half(c, 1)
                    if not last:
                        front(c + 1, 1 - q, n)
                        if n == 12:
                            carry_half(c + 1, 0)

            def front0(fc, fq):
                front(fc, fq)
                carry_half(0, 0)

            sweep(dve, chunks, front0, body)
            for k in range(2 * N):
                fin(chunks - 2, 0, N + k)
                fin(chunks - 1, 1, k)

        @block.scalar
        def _(act):
            act.wait_ge(loaded, LOADED)
            act.wait_ge(consts, CONST)
            nc.scalar.activation(A[:, :, :], A_log[:, :, :], ACT.Exp).then_inc(A_done, 1)
            act.wait_ge(A_done, 2)

            def front(fc, fq, k=None):
                if k in (None, 4):
                    wait(act, vg_psum, fc * 2)
                    for f in range(2):
                        act.wait_ge(xmT_psum, fc * 3 + f + 1)
                        nc.scalar.activation(xmT[:, f, 0:T], tp[f][:, :], ACT.Identity, bias=cols["ln_b"][:, f:f + 1],
                                             scale=cols["ln_g"][:, f:f + 1]).then_inc(xmT_ready, 1)
                    act.wait_ge(xmT_psum, fc * 3 + 3)
                    for f in range(2):
                        last = nc.scalar.activation(xmT[:, f, T:T + 1], mm[0][:, f:f + 1], ACT.Identity,
                                                    bias=cols["ln_b"][:, f:f + 1], scale=cols["ln_g"][:, f:f + 1])
                    last.then_inc(xmT_ready, 1)
                if k in (None, 5):
                    act.wait_ge(x1carry_ready, fc + 1)
                    wait(act, conv_step, fc * 3)
                    wait(act, x1after_ready, fc)
                    for f in range(2):
                        act.wait_ge(x1_psum, fc * 3 + f + 1)
                        nc.scalar.activation(x1[:, f, 1:T + 1], mm[f][:, :], ACT.Identity,
                                             bias=cols["w1_b"][:, f:f + 1]).then_inc(x1_ready, 1)
                    act.wait_ge(x1_psum, fc * 3 + 3)
                    for f in range(2):
                        last = nc.scalar.activation(after[:, f:f + 1], tp[0][:, f:f + 1], ACT.Identity,
                                                    bias=cols["w1_b"][:, f:f + 1])
                    last.then_inc(x1_ready, 1)
                if k in (None, 7):
                    act.wait_ge(conv_step, fc * 3 + 3)
                    wait(act, vg_ready, fc)
                    nc.scalar.activation(th[:, :, :], cv[:, :, :], ACT.Tanh).then_inc(th_ready, 1)
                if k in (None, 9):
                    wait(act, dt_ready, fc)
                    for f in range(2):
                        act.wait_ge(dt_psum, fc * 2 + f + 1)
                        nc.scalar.activation(xs[:, f, :], mm[f][:, :], ACT.Identity,
                                             bias=cols["dt_b"][:, f:f + 1]).then_inc(xs_ready, 1)
                if k in (None, 10):
                    act.wait_ge(bc_psum, fc + 1)
                    wait(act, part_ready, fc * 3)
                    nc.scalar.activation(bcf[:, :], mm[0][0:R, :], ACT.Identity, bias=bcb[:, :]).then_inc(bcf_ready, 1)
                    act.wait_ge(na_ready, fc + 1)
                    nc.scalar.activation(cv[:, :, :], cv[:, :, :], ACT.Exp).then_inc(ln1p_step, 1)
                    act.wait_ge(ln1p_step, fc * 2 + 1)
                    nc.scalar.activation(cv[:, :, :], cv[:, :, :], ACT.Ln, bias=core.ones[:, 0:1]).then_inc(ln1p_step, 1)
                if k in (None, 11):
                    act.wait_ge(bcf_ready, fc + 1)
                    wait(act, C_psum, (fc - 1) * N)
                    nc.scalar.copy(bcs[fq][:, :], bcf[:, :]).then_inc(part_ready, 1)
                if k in (None, 12):
                    act.wait_ge(dt_ready, fc + 1)
                    act.wait_ge(xc_ready, fc + 1)
                    for f in range(2):
                        act.wait_ge(vg_psum, fc * 2 + f + 1)
                        last = nc.scalar.activation(cv[:, f, :], mm[f][:, :], ACT.Identity, bias=half_v1b[:, f:f + 1],
                                                    scale=0.5)
                        last.then_inc(vb_ready, 1)
                    act.wait_ge(vb_ready, fc * 2 + 2)
                    nc.scalar.activation(th[:, :, :], cv[:, :, :], ACT.Tanh).then_inc(vth_ready, 1)
                if k in (None, 13):
                    act.wait_ge(rest_ready, fc * 2 + 1)
                    lo = 2 * N
                    nc.scalar.copy(bcs[fq][lo:2 * lo, :], bcf[lo:2 * lo, :])
                    nc.scalar.copy(bcs[fq][2 * lo:R, :], bcf[2 * lo:R, :]).then_inc(part_ready, 1)
                if k in (None, 15):
                    act.wait_ge(rest_ready, fc * 2 + 2)
                    lo = 4 * N
                    nc.scalar.copy(bcs[fq][lo:R, :], bcf[lo:R, :]).then_inc(part_ready, 1)

            def fin(c, q, k):
                if k == 5:
                    wait(act, ff1_psum, c * FB)
                    for f in range(2):
                        act.wait_ge(xn2T_psum, c * 2 + f + 1)
                        nc.scalar.activation(xn2T[:, f, :], tp[f][:, :], ACT.Identity, bias=cols["ln2_b"][:, f:f + 1],
                                             scale=cols["ln2_g"][:, f:f + 1]).then_inc(xn2T_ready, 1)
                if k == 8:
                    wait(act, ff2_psum, c * 2)
                    for m in range(FB):
                        act.wait_ge(ff1_psum, c * FB + m + 1)
                        nc.scalar.activation(hid[:, m, :], bank[6 - m % 4 // 2 * 2 + m % 2][:, :], ACT.Gelu,
                                             bias=ff1b[:, m:m + 1]).then_inc(hid_ready, 1)

            def decay(c, q, n):
                s = n % RING
                if n == 0:
                    act.wait_ge(dt_ready, c + 1)
                for f in range(2):
                    wait(act, scan_done[f], c * N + n - RING + 1)
                wait(act, g_ready, c * N + n - RING + 1)
                wait(act, u_ready, c * N + n - 1)
                act.wait_ge(B_psum, c * N + n + 1)
                nc.scalar.copy(bs[n % 2][:, :], bB[:, :]).then_inc(bs_ready, 1)
                for f in range(2):
                    last = nc.scalar.activation(a[s][:, f, :], dt[q][:, f, :], ACT.Exp, scale=A_neg[:, f, n:n + 1])
                last.then_inc(a_ready, 1)
                act.wait_ge(C_psum, c * N + n + 1)
                nc.scalar.copy(cs[s][:, :], bC[:, :]).then_inc(cs_ready, 1)

            def body(c, q, first, last):
                for n in range(N):
                    if n + AHEAD < N:
                        decay(c, q, n + AHEAD)
                    if not last:
                        front(c + 1, 1 - q, n)
                    if past(c, 2):
                        fin(c - 2, q, N + n)
                    if not first:
                        fin(c - 1, 1 - q, n)
                    if n + 1 == N and not last:
                        for m in range(AHEAD):
                            decay(c + 1, 1 - q, m)

            def front0(fc, fq):
                front(fc, fq)
                for m in range(AHEAD):
                    decay(0, 0, m)

            sweep(act, chunks, front0, body)
            for k in range(2 * N):
                fin(chunks - 2, 0, N + k)
                fin(chunks - 1, 1, k)

        @block.tensor
        def _(pe):
            pe.wait_ge(loaded, LOADED)
            pe.wait_ge(consts, CONST)

            def widen(name, out, rhs, f):
                for kk in range(2):
                    last = nc.tensor.matmul(out, mats[name][:, kk, f * P:(f + 1) * P], rhs(kk), start=(kk == 0),
                                            stop=(kk == 1))
                return last

            def front(fc, fq, k=None):
                if k in (None, 4):
                    pe.wait_ge(xm_ready, fc + 1)
                    wait(pe, hnew_ready, (fc - 2) * 2)
                    wait(pe, x1_ready, fc * 3)
                    wait(pe, x2_ready, (fc - 1) * 2)
                    wait(pe, vb_ready, fc * 2)
                    for f in range(2):
                        for j in range(TJ):
                            last = nc.tensor.transpose(tp[f][:, j * P:(j + 1) * P], xn[:, j, f * P:(f + 1) * P],
                                                       core.ident[:, :])
                        last.then_inc(xmT_psum, 1)
                    for f in range(2):
                        last = nc.tensor.transpose(mm[0][:, f:f + 1], xn[0:1, TJ, f * P:(f + 1) * P],
                                                   core.ident[0:1, 0:1])
                    last.then_inc(xmT_psum, 1)
                if k in (None, 5):
                    pe.wait_ge(xmT_ready, fc * 3 + 3)
                    for f in range(2):
                        widen("w1_w", mm[f][:, :], lambda kk: xmT[:, kk, 0:T], f).then_inc(x1_psum, 1)
                    for f in range(2):
                        last = widen("w1_w", tp[0][:, f:f + 1], lambda kk: xmT[:, kk, T:T + 1], f)
                    last.then_inc(x1_psum, 1)
                if k in (None, 9):
                    pe.wait_ge(xc_ready, fc + 1)
                    pe.wait_ge(x1_ready, fc * 3 + 3)
                    wait(pe, hid_ready, (fc - 1) * FB)
                    for f in range(2):
                        widen("dt_w", mm[f][:, :], lambda kk: xc[fq][:, kk, :], f).then_inc(dt_psum, 1)
                if k in (None, 10):
                    pe.wait_ge(xs_ready, fc * 2 + 1)
                    for kk in range(2):
                        last = nc.tensor.matmul(mm[0][0:R, :], bcw[:, kk, :, :].rearrange("p a n -> p (a n)"),
                                                xc[fq][:, kk, :], start=(kk == 0), stop=(kk == 1))
                    last.then_inc(bc_psum, 1)
                if k in (None, 11):
                    pe.wait_ge(xs_ready, fc * 2 + 2)
                    pe.wait_ge(bcf_ready, fc + 1)
                    for f in range(2):
                        widen("v1_w", mm[f][:, :], lambda kk: xmT[:, kk, 0:T], f).then_inc(vg_psum, 1)

            def fin(c, q, k, fronts):
                if k == 2:
                    pe.wait_ge(yv_ready, c + 1)
                    pe.wait_ge(vb_ready, min(c + 2, chunks) * 2 if isinstance(c, int) else c * 2 + 4)
                    for m in range(2):
                        for j in range(2):
                            t0 = (2 * m + j) * P
                            for f in range(2):
                                last = nc.tensor.matmul(mm[m][:, j * D:(j + 1) * D], yv[:, f, t0:t0 + P],
                                                        mats["w2_w"][:, f, :], start=(f == 0), stop=(f == 1))
                        last.then_inc(mo_psum, 1)
                if k == 5:
                    pe.wait_ge(xn2_ready, c + 1)
                    pe.wait_ge(x1_ready, fronts * 3)
                    wait(pe, hnew_ready, c * 2)
                    for f in range(2):
                        for j in range(TJ):
                            last = nc.tensor.transpose(tp[f][:, j * P:(j + 1) * P], xn2[:, j, f * P:(f + 1) * P],
                                                       core.ident[:, :])
                        last.then_inc(xn2T_psum, 1)
                if k in (6, 7, 8):
                    pe.wait_ge(xn2T_ready, c * 2 + 2)
                    pe.wait_ge(x2_ready, c * 2 + 2)
                    for m in range(2 * (k - 6), 2 * (k - 6) + 2):
                        wait(pe, hid_ready, c * FB + max(m - 3, 0))
                        for kk in range(2):
                            last = nc.tensor.matmul(bank[6 - m % 4 // 2 * 2 + m % 2][:, :], ff1[:, kk, m * P:(m + 1) * P], xn2T[:, kk, :],
                                                    start=(kk == 0), stop=(kk == 1))
                        last.then_inc(ff1_psum, 1)
                if k in FF2_AT:
                    m, j = divmod(FF2_AT.index(k), 2)
                    if k == FF2_AT[0]:
                        pe.wait_ge(hid_ready, c * FB + FB)
                    t0 = (2 * m + j) * P
                    for g in range(FB):
                        last = nc.tensor.matmul(tp[m][:, j * D:(j + 1) * D], hid[:, g, t0:t0 + P], ff2[:, g, :],
                                                start=(g == 0), stop=(g == FB - 1))
                    if j == 1:
                        last.then_inc(ff2_psum, 1)

            def spread(c, q, n):
                if n == 0:
                    pe.wait_ge(part_ready, c * 3 + 3)
                wait(pe, bs_ready, c * N + n)
                nc.tensor.matmul(bB[:, :], pick[:, n:n + 1].to_broadcast([R, P]), bcs[q][:, :], start=True,
                                 stop=True).then_inc(B_psum, 1)
                wait(pe, cs_ready, c * N + n)
                nc.tensor.matmul(bC[:, :], pick[:, N + n:N + n + 1].to_broadcast([R, P]), bcs[q][:, :], start=True, stop=True).then_inc(C_psum, 1)

            def reduce(c, n):
                if n == 0:
                    wait(pe, y_ready, c)
                pe.wait_ge(g_ready, c * N + n + 1)
                for f in range(2):
                    last = nc.tensor.matmul(yp[f][:, :], core.ident[:, :], hs[n % RING][:, f, :], start=(n == 0),
                                            stop=(n == N - 1))
                last.then_inc(red_done, 1)

            def body(c, q, first, last):
                fronts = c + 1 if last else c + 2
                for n in range(N):
                    if n + AHEAD < N:
                        spread(c, q, n + AHEAD)
                    elif n + 1 == N and not last:
                        front(c + 1, 1 - q, n)
                        for m in range(AHEAD):
                            spread(c + 1, 1 - q, m)
                    if n > 0:
                        reduce(c, n - 1)
                    elif not first:
                        reduce(c - 1, N - 1)
                    if not last and n + 1 < N:
                        front(c + 1, 1 - q, n)
                    if past(c, 2):
                        fin(c - 2, q, N + n, fronts)
                    if not first:
                        fin(c - 1, 1 - q, n, fronts)

            def front0(fc, fq):
                front(fc, fq)
                for m in range(AHEAD):
                    spread(0, 0, m)

            sweep(pe, chunks, front0, body)
            reduce(chunks - 1, N - 1)
            for k in range(2 * N):
                fin(chunks - 2, 0, N + k, chunks)
                fin(chunks - 1, 1, k, chunks)


def moe_phase(core, bias, weights, indices, w1, w2, h_io, h_out):
    nc, bank = core.nc, core.bank
    tokens, K = weights.shape
    E, _, FF = w1.shape
    NT = tokens // P
    NB = tokens // T
    FB = FF // P
    with ExitStack() as ctx:
        def sb(name, shape, dt=F32):
            return ctx.enter_context(nc.sbuf_tensor("m_" + name, shape, dt))

        def sem(name):
            return nc.alloc_semaphore(name="m_" + name)

        passed = sem("passed")

        acc = sb("acc", [P, NT, D])
        bias_b = sb("bias_b", [P, D])
        x = sb("x", [P, NT, D])
        bn = sb("bn", [P, NT, 6])
        mv = sb("mv", [P, NT, 2])
        rstd = sb("rstd", [P, NT])
        xT = sb("xT", [P, 2, tokens])
        wk = sb("wk", [P, NT, K])
        ik = sb("ik", [P, NT, K], I32)
        ikf = sb("ikf", [P, NT, K])
        e_i = sb("e_i", [P, E], I32)
        e_f = sb("e_f", [P, E])
        eq = sb("eq", [P, NT, E])
        cw = sb("cw", [P, NT, E])
        w1s = [sb(f"w1s{s}", [P, 2, FF]) for s in range(2)]
        w2s = [sb(f"w2s{s}", [P, FB, D]) for s in range(2)]
        hid = [sb(f"hid{s}", [P, FB, T]) for s in range(2)]
        cwe = sb("cwe", [P, NT])

        loaded, step_done, iota_done, rstd_step, x_ready, xT_psum, xT_ready, cw_ready = (
            sem("loaded"), sem("step_done"), sem("iota_done"), sem("rstd_step"), sem("x_ready"), sem("xT_psum"),
            sem("xT_ready"), sem("cw_ready"))
        w_loaded = [sem(f"w_loaded{s}") for s in range(2)]
        ff1_psum, hid_ready, ff2_psum, acc_step, cwe_ready, stored = (
            sem("ff1_psum"), sem("hid_ready"), sem("ff2_psum"), sem("acc_step"), sem("cwe_ready"), sem("stored"))
        block = ctx.enter_context(nc.Block())
        rows = h_io[0:tokens, :].rearrange("(j p) d -> p j d", p=P)
        rows_out = h_out[0:tokens, :].rearrange("(j p) d -> p j d", p=P)

        @block.sync
        def _(sp):
            sp.dma_start(acc[:, :, :], rows).then_inc(loaded, 16)
            sp.dma_start(bias_b[:, :], bias.partition_broadcast(P)).then_inc(loaded, 16)
            sp.dma_start(wk[:, :, :], weights.rearrange("(j p) k -> p j k", p=P)).then_inc(loaded, 16)
            sp.dma_start(ik[:, :, :], indices.rearrange("(j p) k -> p j k", p=P)).then_inc(loaded, 16)
            def turn(i):
                for s in range(2):
                    e = i * 2 + s
                    wait(sp, ff2_psum, i * (2 * NT))
                    sp.dma_start(w1s[s][:, :, :], w1[bass.ds(e, 1), :, :].rearrange("o (k p) n -> p (o k) n", p=P)
                                 ).then_inc(w_loaded[s], 16)
                    sp.dma_start(w2s[s][:, :, :], w2[bass.ds(e, 1), :, :].rearrange("o (g p) n -> p (o g) n", p=P)
                                 ).then_inc(w_loaded[s], 16)

            repeat(sp, E // 2, turn)
            sp.wait_ge(acc_step, E * NT)
            sp.dma_start(rows_out, acc[:, :, :]).then_inc(stored, 16)
            sp.wait_ge(stored, 16)

        @block.gpsimd
        def _(pool):
            nc.gpsimd.iota(e_i[:, :], pattern=[[1, E]], base=0, channel_multiplier=0).then_inc(iota_done, 1)
            pool.wait_ge(step_done, 3)
            nc.gpsimd.tensor_tensor(rstd[:, :], mv[:, :, 1], core.eps[:, 0:mv.shape[1]], ALU.add).then_inc(rstd_step, 1)
            pool.wait_ge(rstd_step, 1)
            nc.gpsimd.tensor_tensor(rstd[:, :], rstd[:, :], core.neg_half[:, 0:NT], ALU.pow).then_inc(rstd_step, 1)

        @block.vector
        def _(dve):
            steps = [0]

            def step(ins):
                ins.then_inc(step_done, 1)
                steps[0] += 1
                dve.wait_ge(step_done, steps[0])

            dve.wait_ge(loaded, 64)
            step(nc.vector.tensor_tensor(x[:, :, :], acc[:, :, :], bias_b[:, :].unsqueeze(1).to_broadcast([P, NT, D]),
                                         ALU.subtract))
            for j in range(NT):
                last = nc.vector.bn_stats(bn[:, j, :], x[:, j, :])
            step(last)
            hold(dve, passed)
            for j in range(NT):
                last = nc.vector.bn_aggr(mv[:, j, :], bn[:, j, :])
            step(last)
            dve.wait_ge(rstd_step, 2)
            for j in range(NT):
                last = nc.vector.tensor_scalar(x[:, j, :], x[:, j, :], mv[:, j, 0:1], rstd[:, j:j + 1], ALU.subtract,
                                               ALU.mult)
            last.then_inc(x_ready, 1)
            dve.wait_ge(iota_done, 1)
            nc.vector.tensor_copy(e_f[:, :], e_i[:, :])
            step(nc.vector.tensor_copy(ikf[:, :, :], ik[:, :, :]))
            for k in range(K):
                out = cw if k == 0 else eq
                step(nc.vector.tensor_tensor(out[:, :, :], ikf[:, :, k:k + 1].to_broadcast([P, NT, E]),
                                             e_f[:, :].unsqueeze(1).to_broadcast([P, NT, E]), ALU.is_equal))
                step(nc.vector.tensor_tensor(out[:, :, :], out[:, :, :], wk[:, :, k:k + 1].to_broadcast([P, NT, E]),
                                             ALU.mult))
                if k:
                    step(nc.vector.tensor_tensor(cw[:, :, :], cw[:, :, :], eq[:, :, :], ALU.add))
            def turn(e):
                wait(dve, acc_step, e * NT)
                nc.vector.tensor_copy(cwe[:, :].unsqueeze(2), cw[:, :, bass.ds(e, 1)]).then_inc(cwe_ready, 1)
                wait(dve, cwe_ready, e + 1)
                for j in range(NT):
                    wait(dve, ff2_psum, e * NT + j + 1)
                    nc.vector.scalar_tensor_tensor(acc[:, j, :], bank[4 + j % 4][:, 0:D], cwe[:, j:j + 1], acc[:, j, :],
                                                   ALU.mult, ALU.add).then_inc(acc_step, 1)

            repeat(dve, E, turn)

        @block.scalar
        def _(act):
            for m in range(2 * NB):
                act.wait_ge(xT_psum, m + 1)
                f, b = m % 2, m // 2
                nc.scalar.copy(xT[:, f, b * T:(b + 1) * T], bank[m % 4][:, :]).then_inc(xT_ready, 1)
            def turn(e):
                for b in range(NB):
                    for g in range(FB):
                        t = b * FB + g
                        wait(act, ff1_psum, e * (NB * FB) + t + 1)
                        if g == 0:
                            wait(act, ff2_psum, e * NT)
                        nc.scalar.activation(hid[b][:, g, :], bank[t % 4][:, :], ACT.Gelu).then_inc(hid_ready, 1)

            repeat(act, E, turn)

        @block.tensor
        def _(pe):
            pe.wait_ge(x_ready, 1)
            for m in range(2 * NB):
                f, b = m % 2, m // 2
                for j in range(TJ):
                    last = nc.tensor.transpose(bank[m % 4][:, j * P:(j + 1) * P], x[:, b * TJ + j, f * P:(f + 1) * P],
                                               core.ident[:, :])
                last.then_inc(xT_psum, 1)
            pe.wait_ge(xT_ready, 2 * NB)
            def turn(i):
                for s in range(2):
                    e = i * 2 + s
                    wait(pe, w_loaded[s], i * 32 + 32)
                    for b in range(NB):
                        for g in range(FB):
                            t = b * FB + g
                            if t >= 4:
                                wait(pe, hid_ready, e * (NB * FB) + t - 3)
                            else:
                                wait(pe, hid_ready, e * (NB * FB))
                            for kk in range(2):
                                last = nc.tensor.matmul(bank[t % 4][:, :], w1s[s][:, kk, g * P:(g + 1) * P],
                                                        xT[:, kk, b * T:(b + 1) * T], start=(kk == 0), stop=(kk == 1))
                            last.then_inc(ff1_psum, 1)
                    for j in range(NT):
                        b = j // TJ
                        wait(pe, hid_ready, e * (NB * FB) + (b + 1) * FB)
                        if j >= 4:
                            wait(pe, acc_step, e * NT + j - 3)
                        else:
                            wait(pe, acc_step, e * NT)
                        t0 = (j % TJ) * P
                        for g in range(FB):
                            last = nc.tensor.matmul(bank[4 + j % 4][:, 0:D], hid[b][:, g, t0:t0 + P], w2s[s][:, g, :],
                                                    start=(g == 0), stop=(g == FB - 1))
                        last.then_inc(ff2_psum, 1)

            repeat(pe, E // 2, turn)


def tower(nc, args, out, phases=9):
    ids = args["x"]
    tokens = ids.shape[0] * ids.shape[1]
    chunks = tokens // T
    seq = 2048
    h0 = nc.dram_tensor("h0", (tokens, D), F32, kind="Internal").ap()
    h1 = nc.dram_tensor("h1", (tokens, D), F32, kind="Internal").ap()
    h2 = nc.dram_tensor("h2", (tokens, D), F32, kind="Internal").ap()
    with ExitStack() as ctx:
        core = Core(nc, ctx, chunks, seq // T)
        with nc.cleanup_on_exit():
            build_constants(core)
        with nc.cleanup_on_exit():
            embedding_phase(core, ids, args["L0_tok_ab_n"], args["L0_tok_proj_wT"],
                            args["L0_tok_proj_b"], h0)
        if phases > 1:
            with nc.cleanup_on_exit():
                attention_phase(core, args["L0_attn_Wq"], args["L0_attn_Wf"], args["L0_attn_Wi"],
                                args["L0_attn_Wo"], h0, h1)
        if phases > 2:
            with nc.cleanup_on_exit():
                ffn_phase(core, args["L0_ffn_gate_wT"], args["L0_ffn_down_T"], args["L0_ffn_down_bT"],
                          args["L0_ffn_up_T"], args["L0_ffn_up_b"], h1, h2)
        if phases > 3:
            w = {name[len("L1_attn_"):]: ap for name, ap in args.items() if name.startswith("L1_attn_")}
            w["moe_bias"] = args["L1_ffn_bias"]
            with nc.cleanup_on_exit():
                ssm_phase(core, w, h2, out)
        if phases > 4:
            with nc.cleanup_on_exit():
                moe_phase(core, args["L1_ffn_bias"], args["L1_ffn_expert_weights"], args["L1_ffn_expert_indices"],
                          args["L1_ffn_w1"], args["L1_ffn_w2"], out, out)


def lay_out(inputs):
    import numpy as np

    a = {name: np.asarray(x) for name, x in inputs.items()}
    a["x"] = a["x"].reshape(-1, P)
    a["L0_tok_proj_wT"] = a.pop("L0_tok_proj_w").T
    a["L0_tok_ab_n"] = np.concatenate([a.pop("L0_tok_a_n"), a.pop("L0_tok_b_n")], axis=1)
    a["L0_attn_Wi"] = a["L0_attn_Wi"].reshape(D, 2, 8, 4, 4).transpose(0, 1, 3, 2, 4).reshape(D, D)
    a["L0_attn_Wo"] = a["L0_attn_Wo"].reshape(2, 8, 4, 4, D).transpose(0, 2, 1, 3, 4).reshape(D, D)
    a["L0_ffn_gate_wT"] = a.pop("L0_ffn_gate_w").T
    a["L0_ffn_down_T"] = a.pop("L0_ffn_down_w").transpose(2, 0, 1)
    a["L0_ffn_down_bT"] = a.pop("L0_ffn_down_b").T
    a["L0_ffn_up_T"] = a.pop("L0_ffn_up_w").transpose(2, 0, 1)
    for name in ("ln_g", "ln_b", "w1_b", "v1_b", "dt_b", "D_p", "ln2_g", "ln2_b", "ff1_b"):
        a["L1_attn_" + name] = a["L1_attn_" + name].reshape(-1, P).T
    for name in ("Bp_b", "Cp_b"):
        a["L1_attn_" + name] = a["L1_attn_" + name].reshape(-1, 1)
    del a["L1_ffn_scores"]
    return {name: np.ascontiguousarray(x) for name, x in a.items()}


def kernel(**inputs):
    import concourse.bacc as bacc
    from concourse.bass_utils import run_bass_kernel_spmd

    batch, seq = inputs["x"].shape
    nc = bacc.Bacc("TRN2", target_bir_lowering=False, num_devices=1)
    arrays, args = {}, {}
    for name, a in lay_out(inputs).items():
        arrays[f"in_{name}"] = a
        args[name] = nc.dram_tensor(f"in_{name}", a.shape, mybir.dt.from_np(a.dtype), kind="ExternalInput").ap()
    out = nc.dram_tensor("out_0", (batch * seq, D), F32, kind="ExternalOutput").ap()
    tower(nc, args, out)
    result = run_bass_kernel_spmd(nc, [arrays], core_ids=[0])
    return result.results[0]["out_0"].reshape(batch, seq, D)
```

```python
from contextlib import ExitStack

import concourse.bass as bass
from concourse import mybir

F32 = mybir.dt.float32
BF16 = mybir.dt.bfloat16
I32 = mybir.dt.int32
ALU = mybir.AluOpType
ACT = mybir.ActivationFunctionType
AX = mybir.AxisListType

P = 128
D = 256
T = 512
TJ = T // P
EPS = 1e-5
PI = 3.141592653589793


def wait(eng, sem, value):
    if not (isinstance(value, int) and value <= 0):
        eng.wait_ge(sem, value)


def hold(eng, passed):
    eng.sem_inc(passed, 1)


def repeat(eng, n, body):
    body(0)
    if n > 1:
        with eng.Fori(1, n) as i:
            body(i)


def sweep(eng, chunks, front, body):
    front(0, 0)
    body(0, 0, True, False)
    body(1, 1, False, False)
    if chunks > 4:
        with eng.Fori(1, chunks // 2 - 1) as i:
            body(i * 2, 0, False, False)
            body(i * 2 + 1, 1, False, False)
    body(chunks - 2, 0, False, False)
    body(chunks - 1, 1, False, True)


def chunk_view(h):
    return h.rearrange("(c j p) d -> c p j d", j=TJ, p=P)


def one(view, c):
    return view[bass.ds(c, 1), :, :, :].rearrange("o p j d -> p (o j) d")


def past(c, n):
    return not isinstance(c, int) or c >= n


class Core:

    def __init__(self, nc, ctx, chunks, chunks_per_batch):
        self.nc = nc
        self.chunks = chunks
        self.bank = [ctx.enter_context(nc.psum_tensor(f"bank{i}", [P, T], F32)) for i in range(8)]
        sb = lambda name, shape, dt=F32: ctx.enter_context(nc.sbuf_tensor(name, shape, dt))
        self.ident = sb("ident", [P, P])
        self.ident_b = sb("ident_b", [P, P], BF16)
        self.neg_half = sb("neg_half", [P, 8])
        self.eps = sb("eps", [P, 8])
        self.ones = sb("ones", [P, P])
        self.keep = sb("keep", [P, chunks + 1])
        self.chunks_per_batch = chunks_per_batch


def build_constants(core):
    nc = core.nc
    with ExitStack() as ctx:
        filled = nc.alloc_semaphore(name="const_filled")
        block = ctx.enter_context(nc.Block())

        @block.gpsimd
        def _(pool):
            nc.gpsimd.memset(core.ident[:, :], 0.0).then_inc(filled, 1)
            nc.gpsimd.memset(core.ident_b[:, :], 0.0).then_inc(filled, 1)
            nc.gpsimd.memset(core.ones[:, :], 1.0).then_inc(filled, 1)
            nc.gpsimd.memset(core.neg_half[:, :], -0.5).then_inc(filled, 1)
            nc.gpsimd.memset(core.keep[:, :], 1.0).then_inc(filled, 1)
            nc.gpsimd.memset(core.eps[:, :], EPS).then_inc(filled, 1)
            pool.wait_ge(filled, 6)
            for m in (core.ident, core.ident_b):
                nc.gpsimd.affine_select(out=m[:, :], in_=m[:, :], compare_op=ALU.not_equal, fill=1.0, base=0,
                                        pattern=[[-1, P]], channel_multiplier=1)
            nc.gpsimd.memset(core.keep[:, 0::core.chunks_per_batch], 0.0).then_inc(filled, 1)
            pool.wait_ge(filled, 7)


def embedding_phase(core, ids, ab_n, proj_wT, proj_b, h_out):
    nc, bank, chunks = core.nc, core.bank, core.chunks
    V, NF = ab_n.shape[0], ab_n.shape[1] // 2
    tiles = ids.shape[0]
    GATHERED = 16 * TJ
    MAGIC = 1.5 * 2.0 ** 23
    with ExitStack() as ctx:
        def sb(name, shape, dt=F32):
            return ctx.enter_context(nc.sbuf_tensor("e_" + name, shape, dt))

        def sem(name):
            return nc.alloc_semaphore(name="e_" + name)

        passed = sem("passed")

        ids_row = sb("ids_row", [tiles, P], I32)
        ids_f = sb("ids_f", [tiles, P])
        idT_f = sb("idT_f", [P, tiles])
        idT_i = sb("idT_i", [P, tiles], I32)
        freq_i = sb("freq_i", [P, NF], I32)
        freq = sb("freq", [P, NF])
        half_pi = sb("half_pi", [P, 1])
        w2 = sb("w2", [2 * NF, D])
        bias = sb("bias", [P, D])
        idx = [sb(f"idx{q}", [P, TJ], I32) for q in range(2)]
        gath = [sb(f"gath{q}", [P, TJ, 2 * NF]) for q in range(2)]
        idc = [sb(f"idc{q}", [P, TJ]) for q in range(2)]
        prod = [sb(f"prod{q}", [P, TJ, NF]) for q in range(2)]
        turns = [sb(f"turns{q}", [P, TJ, NF]) for q in range(2)]
        trig = [sb(f"trig{q}", [P, TJ, 2 * NF]) for q in range(2)]
        emb = [sb(f"emb{q}", [P, TJ, 2 * NF]) for q in range(2)]
        embT = [sb(f"embT{q}", [2 * NF, T]) for q in range(2)]
        hbuf = [sb(f"hbuf{q}", [P, TJ, D]) for q in range(2)]

        loaded, consts, ids_cast, ids_turned, ids_ready = (
            sem("loaded"), sem("consts"), sem("ids_cast"), sem("ids_turned"), sem("ids_ready"))
        idx_ready = sem("idx_ready")
        gathered = [sem(f"gathered{q}") for q in range(2)]
        step_done = sem("step_done")
        phase_ready = sem("phase_ready")
        trig_ready = sem("trig_ready")
        emb_ready = sem("emb_ready")
        embT_psum = sem("embT_psum")
        embT_ready = sem("embT_ready")
        h_psum = sem("h_psum")
        h_ready = sem("h_ready")
        stored = [sem(f"stored{q}") for q in range(2)]
        block = ctx.enter_context(nc.Block())
        hv = chunk_view(h_out)

        @block.sync
        def _(sp):
            sp.dma_start(ids_row[:, :], ids).then_inc(loaded, 16)
            sp.dma_start(w2[0:NF, :], proj_wT).then_inc(loaded, 16)
            sp.dma_start(w2[NF:2 * NF, :], proj_wT).then_inc(loaded, 16)
            sp.dma_start(bias[:, :], proj_b.partition_broadcast(P)).then_inc(loaded, 16)

            def store(c, q):
                sp.wait_ge(h_ready, c * 2 + 2)
                sp.dma_start(one(hv, c), hbuf[q][:, :, :]).then_inc(stored[q], 16)

            def body(c, q, first, last):
                if not first:
                    store(c - 1, 1 - q)

            sweep(sp, chunks, lambda fc, fq: None, body)
            store(chunks - 1, 1)
            for q in range(2):
                sp.wait_ge(stored[q], 8 * chunks)

        @block.gpsimd
        def _(pool):
            nc.gpsimd.iota(freq_i[:, :], pattern=[[1, NF]], base=1, channel_multiplier=0).then_inc(consts, 1)
            nc.gpsimd.memset(half_pi[:, :], PI / 2).then_inc(consts, 1)

            def front(fc, fq):
                pool.wait_ge(idx_ready, fc + 1)
                wait(pool, emb_ready, fc - 1)
                hold(pool, passed)
                for j in range(TJ):
                    off = bass.IndirectOffsetOnAxis(ap=idx[fq][:, j:j + 1], axis=0)
                    nc.gpsimd.indirect_dma_start(gath[fq][:, j, :], None, ab_n, off).then_inc(gathered[fq], 16)

            def body(c, q, first, last):
                if not last:
                    front(c + 1, 1 - q)

            sweep(pool, chunks, front, body)

        @block.vector
        def _(dve):
            dve.wait_ge(loaded, 64)
            nc.vector.tensor_copy(ids_f[:, :], ids_row[:, :]).then_inc(ids_cast, 1)
            dve.wait_ge(consts, 2)
            nc.vector.tensor_copy(freq[:, :], freq_i[:, :])
            dve.wait_ge(ids_turned, 1)
            nc.vector.tensor_copy(idT_f[:, :], bank[0][:, 0:tiles])
            nc.vector.tensor_copy(idT_i[:, :], bank[0][:, 0:tiles]).then_inc(ids_ready, 1)
            dve.wait_ge(ids_ready, 1)

            def front(fc, fq):
                wait(dve, gathered[fq], (fc - fq) * (GATHERED // 2))
                nc.vector.tensor_copy(idx[fq][:, :], idT_i[:, bass.ds(fc * TJ, TJ)]).then_inc(idx_ready, 1)
                nc.vector.tensor_copy(idc[fq][:, :], idT_f[:, bass.ds(fc * TJ, TJ)]).then_inc(step_done, 1)
                dve.wait_ge(step_done, fc * 4 + 1)
                wait(dve, trig_ready, fc - 1)
                nc.vector.tensor_tensor(prod[fq][:, :, :], freq[:, :].unsqueeze(1).to_broadcast([P, TJ, NF]),
                                        idc[fq][:, :].unsqueeze(2).to_broadcast([P, TJ, NF]),
                                        ALU.mult).then_inc(step_done, 1)
                dve.wait_ge(step_done, fc * 4 + 2)
                nc.vector.tensor_scalar(turns[fq][:, :, :], prod[fq][:, :, :], 1.0 / V, MAGIC, ALU.mult,
                                        ALU.add).then_inc(step_done, 1)
                dve.wait_ge(step_done, fc * 4 + 3)
                nc.vector.tensor_scalar(turns[fq][:, :, :], turns[fq][:, :, :], MAGIC, float(V), ALU.subtract,
                                        ALU.mult).then_inc(step_done, 1)
                dve.wait_ge(step_done, fc * 4 + 4)
                nc.vector.tensor_tensor(prod[fq][:, :, :], prod[fq][:, :, :], turns[fq][:, :, :],
                                        ALU.subtract).then_inc(phase_ready, 1)
                dve.wait_ge(phase_ready, fc * 2 + 1)
                nc.vector.scalar_tensor_tensor(turns[fq][:, :, :], prod[fq][:, :, :], -1.0, prod[fq][:, :, :],
                                               ALU.mult, ALU.max).then_inc(phase_ready, 1)

            def finish(c, q):
                wait(dve, stored[q], (c - q) * 8)
                for m in range(2):
                    dve.wait_ge(h_psum, c * 2 + m + 1)
                    nc.vector.tensor_tensor(hbuf[q][:, 2 * m:2 * m + 2, :],
                                            bank[2 + 2 * q + m][:, :].rearrange("p (j d) -> p j d", j=2),
                                            bias[:, :].unsqueeze(1).to_broadcast([P, 2, D]),
                                            ALU.add).then_inc(h_ready, 1)

            def body(c, q, first, last):
                if not last:
                    front(c + 1, 1 - q)
                dve.wait_ge(gathered[q], (c - q) * (GATHERED // 2) + GATHERED)
                dve.wait_ge(trig_ready, c + 1)
                wait(dve, embT_psum, c - 1)
                nc.vector.tensor_tensor(emb[q][:, :, :], gath[q][:, :, :], trig[q][:, :, :],
                                        ALU.mult).then_inc(emb_ready, 1)
                if not first:
                    finish(c - 1, 1 - q)

            sweep(dve, chunks, front, body)
            finish(chunks - 1, 1)

        @block.scalar
        def _(act):
            act.wait_ge(consts, 2)

            def front(fc, fq):
                act.wait_ge(phase_ready, fc * 2 + 2)
                wait(act, emb_ready, fc - 1)
                nc.scalar.activation(trig[fq][:, :, 0:NF], turns[fq][:, :, :], ACT.Sin, bias=half_pi[:, :],
                                     scale=-2.0 * PI / V)
                nc.scalar.activation(trig[fq][:, :, NF:2 * NF], prod[fq][:, :, :], ACT.Sin,
                                     scale=2.0 * PI / V).then_inc(trig_ready, 1)

            def body(c, q, first, last):
                if not last:
                    front(c + 1, 1 - q)
                act.wait_ge(embT_psum, c + 1)
                wait(act, h_psum, (c - 1) * 2)
                nc.scalar.copy(embT[q][:, :], bank[q][:, :]).then_inc(embT_ready, 1)

            sweep(act, chunks, front, body)

        @block.tensor
        def _(pe):
            pe.wait_ge(ids_cast, 1)
            nc.tensor.transpose(bank[0][:, 0:tiles], ids_f[:, :], core.ident[0:tiles, 0:tiles]).then_inc(ids_turned, 1)
            pe.wait_ge(loaded, 64)
            pe.wait_ge(ids_ready, 1)

            def project(c, q):
                pe.wait_ge(embT_ready, c + 1)
                wait(pe, h_ready, (c - 1) * 2)
                for m in range(2):
                    for j in range(2):
                        t0 = (2 * m + j) * P
                        last = nc.tensor.matmul(bank[2 + 2 * q + m][:, j * D:(j + 1) * D], embT[q][:, t0:t0 + P],
                                                w2[:, :], start=True, stop=True)
                    last.then_inc(h_psum, 1)

            def body(c, q, first, last):
                if not first:
                    project(c - 1, 1 - q)
                pe.wait_ge(emb_ready, c + 1)
                wait(pe, embT_ready, c - 1)
                for j in range(TJ):
                    last = nc.tensor.transpose(bank[q][:, j * P:(j + 1) * P], emb[q][:, j, :], core.ident[:, :])
                last.then_inc(embT_psum, 1)

            sweep(pe, chunks, lambda fc, fq: None, body)
            project(chunks - 1, 1)


def attention_phase(core, Wq, Wf, Wi, Wo, h_in, h_out):
    nc, bank, chunks = core.nc, core.bank, core.chunks
    H, DK = 16, D // 16
    DV = DK
    SCALE = DK ** -0.5
    HH = H // 2
    G = 4
    L = DV // G
    GR = HH * L
    RING = 4
    AT = dict(
        stats=5, norm=6, dv=7, o=1, vq=2, rows=3,
        rstd=5, rest1=7, rest2=10,
        x_copy=6, v_copy=6, hi=7, mid=9, lo=11,
        x_T=6, v=6, sum_q=0, wo=2,
    )
    LOGIT_AT, MAX_AT, EXP_AT, SOFT_AT = (6, 7, 9, 11), (8, 10, 11, 13), (8, 9, 11, 13), (8, 10, 12, 14)
    QP_T_AT, QP_AT = (8, 10, 12, 14), (8, 10, 12, 14)
    STACKED = 16 * 3 * G
    with ExitStack() as ctx:
        def sb(name, shape, dt=F32):
            return ctx.enter_context(nc.sbuf_tensor("a_" + name, shape, dt))

        def sem(name):
            return nc.alloc_semaphore(name="a_" + name)

        passed = sem("passed")

        wqf = sb("wqf", [P, 2, 2 * D])
        wi = sb("wi", [P, 2, D])
        wo = sb("wo", [P, 2, D])
        head = sb("head", [P, HH])
        gather = sb("gather", [P, DV, G, HH, L])
        head_sq = sb("head_sq", [P, G, HH, L])
        pick = sb("pick", [3 * HH * L, L, HH, DK], BF16)
        hb = [sb(f"hb{q}", [P, TJ, D]) for q in range(2)]
        h_new = sb("h_new", [P, TJ, D])
        bn = sb("bn", [P, TJ, 6])
        mv = sb("mv", [P, TJ, 2])
        rstd = sb("rstd", [P, TJ])
        xh = sb("xh", [P, TJ, D])
        xT = sb("xT", [P, 2, T])
        v = sb("v", [P, 2, T + 1])
        dv = sb("dv", [P, 2, T])
        dvs = [sb(f"dvs{m}", [P, 2, T], BF16) for m in range(3)]
        stack = [sb(f"stack{q}", [3 * GR, G, 2, T], BF16) for q in range(2)]
        ex = [sb(f"ex{s}", [P, 2, D]) for s in range(2)]
        nmx = [sb(f"nmx{s}", [P, 2]) for s in range(2)]
        sums = [sb(f"sums{s}", [P, 2]) for s in range(2)]
        rsum = [sb(f"rsum{s}", [P, 2]) for s in range(2)]
        qp = [sb(f"qp{q}", [P, 2, 2, T]) for q in range(2)]
        vq = sb("vq", [P, 2, T])
        z = [sb(f"z{s}", [P, 2, T]) for s in range(RING)]
        zlast = sb("zlast", [P, DV, 2])
        carry = sb("carry", [P, DV, 2])
        oT = sb("oT", [P, 2, T])

        bc, op, tp, mm = bank[0:2], bank[2:4], bank[4:6], bank[6:8]

        loaded, sel_step, consts = sem("loaded"), sem("sel_step"), sem("consts")
        h_loaded = [sem(f"h_loaded{q}") for q in range(2)]
        bn_done, stats_ready, var_eps, rstd_ready, xh_ready = (
            sem("bn_done"), sem("stats_ready"), sem("var_eps"), sem("rstd_ready"), sem("xh_ready"))
        xT_psum, xT_ready = sem("xT_psum"), sem("xT_ready")
        vcarry_ready, v_psum, v_ready = sem("vcarry_ready"), sem("v_psum"), sem("v_ready")
        dv_ready, hi_ready, mid_ready, lo_ready = sem("dv_ready"), sem("hi_ready"), sem("mid_ready"), sem("lo_ready")
        rest1_ready, rest2_ready = sem("rest1_ready"), sem("rest2_ready")
        lg_psum = [sem(f"lg_psum{s}") for s in range(2)]
        nmx_ready = sem("nmx_ready")
        exp_done = [sem(f"exp_done{s}") for s in range(2)]
        rsum_ready = sem("rsum_ready")
        qp_ready = sem("qp_ready")
        qpT_psum = [sem(f"qpT_psum{s}") for s in range(2)]
        qpT_ready = [sem(f"qpT_ready{s}") for s in range(2)]
        sumq_psum, vq_ready = sem("sumq_psum"), sem("vq_ready")
        bc_psum = [sem(f"bc_psum{f}") for f in range(2)]
        scan_done = [sem(f"scan_done{f}") for f in range(2)]
        zlast_saved, g_ready = sem("zlast_saved"), sem("g_ready")
        red_done = sem("red_done")
        stacked = [sem(f"stacked{q}") for q in range(2)]
        carry_ready = [sem(f"carry_ready{m}") for m in range(2)]
        oT_ready, ap_psum, hnew_ready, h_stored = sem("oT_ready"), sem("ap_psum"), sem("hnew_ready"), sem("h_stored")
        block = ctx.enter_context(nc.Block())
        hin, hout = chunk_view(h_in), chunk_view(h_out)

        @block.sync
        def _(sp):
            for k in range(2):
                sp.dma_start(wqf[:, k, 0:D], Wq[k * P:(k + 1) * P, :]).then_inc(loaded, 16)
                sp.dma_start(wqf[:, k, D:2 * D], Wf[k * P:(k + 1) * P, :]).then_inc(loaded, 16)
                sp.dma_start(wi[:, k, :], Wi[k * P:(k + 1) * P, :]).then_inc(loaded, 16)
                sp.dma_start(wo[:, k, :], Wo[k * P:(k + 1) * P, :]).then_inc(loaded, 16)

            def load(fc, fq):
                if not isinstance(fc, int) or fc >= 2:
                    sp.wait_ge(hnew_ready, (fc - 1) * 2)
                sp.dma_start(hb[fq][:, :, :], one(hin, fc)).then_inc(h_loaded[fq], 16)

            def store(c):
                sp.wait_ge(hnew_ready, c * 2 + 2)
                sp.dma_start(one(hout, c), h_new[:, :, :]).then_inc(h_stored, 16)

            def restack(fc, fq):
                if past(fc, 2):
                    sp.wait_ge(bc_psum[1], (fc - 1) * DV)
                    hold(sp, passed)
                for m, ready in enumerate((hi_ready, mid_ready, lo_ready)):
                    sp.wait_ge(ready, fc + 1)
                    for g in range(G):
                        sp.dma_start(stack[fq][m * GR:(m + 1) * GR, g, :, :],
                                     dvs[m][g * GR:(g + 1) * GR, :, :]).then_inc(stacked[fq], 16)

            def body(c, q, first, last):
                if not last:
                    load(c + 1, 1 - q)
                if not first:
                    store(c - 1)
                if not last:
                    restack(c + 1, 1 - q)

            def front0(fc, fq):
                load(fc, fq)
                restack(fc, fq)

            sweep(sp, chunks, front0, body)
            store(chunks - 1)
            sp.wait_ge(h_stored, 16 * chunks)

        @block.gpsimd
        def _(pool):
            nc.gpsimd.memset(head[:, :], 1.0).then_inc(sel_step, 1)
            nc.gpsimd.memset(gather[:, :, :, :, :], 0.0).then_inc(sel_step, 1)
            nc.gpsimd.memset(pick[:, :, :, :], 0.0).then_inc(sel_step, 1)
            nc.gpsimd.memset(v[:, :, :], 0.0).then_inc(sel_step, 1)
            nc.gpsimd.memset(zlast[:, :, :], 0.0).then_inc(sel_step, 1)
            pool.wait_ge(sel_step, 5)
            nc.gpsimd.affine_select(out=head[:, :], in_=head[:, :], compare_op=ALU.is_ge, fill=0.0, base=0,
                                    pattern=[[-DK, HH]], channel_multiplier=1).then_inc(sel_step, 1)
            pool.wait_ge(sel_step, 6)
            nc.gpsimd.affine_select(out=head[:, :], in_=head[:, :], compare_op=ALU.is_ge, fill=0.0, base=DK - 1,
                                    pattern=[[DK, HH]], channel_multiplier=-1).then_inc(sel_step, 1)
            for m in range(3):
                pool.wait_ge(sel_step, 7 + m)
                nc.gpsimd.affine_select(out=pick[:, :, :, :], in_=pick[:, :, :, :], compare_op=ALU.not_equal,
                                        fill=1.0, base=-m * GR, pattern=[[-1, L], [-L, HH], [0, DK]],
                                        channel_multiplier=1).then_inc(sel_step, 1)
            pool.wait_ge(sel_step, 10)
            for vi in range(DV):
                nc.gpsimd.tensor_copy(gather[:, vi, vi // L, :, vi % L], head[:, :]).then_inc(consts, 1)
            for g in range(G):
                last = nc.gpsimd.tensor_copy(head_sq[:, g, :, :], head[:, :].unsqueeze(2).to_broadcast([P, HH, L]))
            last.then_inc(consts, 1)

            def front(fc, fq, k=None):
                if k in (None, AT["rstd"]):
                    pool.wait_ge(stats_ready, fc + 1)
                    wait(pool, xh_ready, fc)
                    nc.gpsimd.tensor_tensor(rstd[:, :], mv[:, :, 1], core.eps[:, 0:mv.shape[1]], ALU.add).then_inc(var_eps, 1)
                    pool.wait_ge(var_eps, fc + 1)
                    nc.gpsimd.tensor_tensor(rstd[:, :], rstd[:, :], core.neg_half[:, 0:TJ],
                                            ALU.pow).then_inc(rstd_ready, 1)
                if k in (None, AT["rest1"]):
                    pool.wait_ge(hi_ready, fc + 1)
                    nc.gpsimd.tensor_tensor(dv[:, :, :], dv[:, :, :], dvs[0][:, :, :],
                                            ALU.subtract).then_inc(rest1_ready, 1)
                if k in (None, AT["rest2"]):
                    pool.wait_ge(mid_ready, fc + 1)
                    nc.gpsimd.tensor_tensor(dv[:, :, :], dv[:, :, :], dvs[1][:, :, :],
                                            ALU.subtract).then_inc(rest2_ready, 1)

            def body(c, q, first, last):
                for vi in range(DV):
                    for f in range(2):
                        pool.wait_ge(scan_done[f], c * DV + vi + 1)
                    if vi in (0, 8):
                        pool.wait_ge(carry_ready[vi // 8], c + 1)
                    hold(pool, passed)
                    nc.gpsimd.tensor_copy(zlast[:, vi, :], z[vi % RING][:, :, T - 1]).then_inc(zlast_saved, 1)
                    pool.wait_ge(zlast_saved, c * DV + vi + 1)
                    if vi == 0:
                        for s in range(2):
                            pool.wait_ge(qpT_ready[s], c * 2 + 2)
                    nc.gpsimd.tensor_tensor(z[vi % RING][:, :, :], z[vi % RING][:, :, :], qp[q][:, 0, :, :],
                                            ALU.mult).then_inc(g_ready, 1)
                    if not last:
                        front(c + 1, 1 - q, vi)

            sweep(pool, chunks, front, body)

        @block.vector
        def _(dve):
            dve.wait_ge(consts, DV + 1)

            def front(fc, fq, k=None):
                if k in (None, AT["stats"]):
                    dve.wait_ge(h_loaded[fq], h_count(fc, fq))
                    for j in range(TJ):
                        last = nc.vector.bn_stats(bn[:, j, :], hb[fq][:, j, :])
                    last.then_inc(bn_done, 1)
                    dve.wait_ge(bn_done, fc + 1)
                    wait(dve, rstd_ready, fc)
                    hold(dve, passed)
                    for j in range(TJ):
                        last = nc.vector.bn_aggr(mv[:, j, :], bn[:, j, :])
                    last.then_inc(stats_ready, 1)
                if k in (None, AT["norm"]):
                    dve.wait_ge(rstd_ready, fc + 1)
                    dve.wait_ge(stats_ready, fc + 1)
                    wait(dve, xT_psum, fc * 2)
                    for j in range(TJ):
                        last = nc.vector.tensor_scalar(xh[:, j, :], hb[fq][:, j, :], mv[:, j, 0:1], rstd[:, j:j + 1],
                                                       ALU.subtract, ALU.mult)
                    last.then_inc(xh_ready, 1)
                    wait(dve, v_ready, fc * 2)
                    nc.vector.tensor_scalar(v[:, :, 0:1], v[:, :, T:T + 1], core.keep[:, bass.ds(fc, 1)], None,
                                            ALU.mult).then_inc(vcarry_ready, 1)
                if k in (None, AT["dv"]):
                    dve.wait_ge(v_ready, fc * 2 + 2)
                    dve.wait_ge(vcarry_ready, fc + 1)
                    wait(dve, lo_ready, fc)
                    nc.vector.tensor_tensor(dv[:, :, :], v[:, :, 0:T], v[:, :, 1:T + 1],
                                            ALU.subtract).then_inc(dv_ready, 1)
                for j in range(TJ):
                    s = j % 2
                    if k in (None, MAX_AT[j]):
                        dve.wait_ge(lg_psum[s], fc * 2 + j // 2 + 1)
                        wait(dve, exp_done[s], fc * 2 + j // 2)
                        nc.vector.tensor_reduce(nmx[s][:, :], mm[s][:, :].rearrange("p (w d) -> p w d", w=2), AX.X,
                                                ALU.max, negate=True).then_inc(nmx_ready, 1)
                    if k in (None, SOFT_AT[j]):
                        dve.wait_ge(exp_done[s], fc * 2 + j // 2 + 1)
                        nc.vector.reciprocal(rsum[s][:, :], sums[s][:, :]).then_inc(rsum_ready, 1)
                        dve.wait_ge(rsum_ready, fc * TJ + j + 1)
                        nc.vector.tensor_scalar(ex[s][:, 0, :], ex[s][:, 0, :], rsum[s][:, 0:1], SCALE, ALU.mult,
                                                ALU.mult)
                        nc.vector.tensor_scalar(ex[s][:, 1, :], ex[s][:, 1, :], rsum[s][:, 1:2], None,
                                                ALU.mult).then_inc(qp_ready, 1)

            def carry_half(c, m):
                wait(dve, zlast_saved, (c - 1) * DV + DV // 2 * (m + 1) if m == 0 else c * DV)
                nc.vector.tensor_scalar(carry[:, m * 8:(m + 1) * 8, :], zlast[:, m * 8:(m + 1) * 8, :],
                                        core.keep[:, bass.ds(c, 1)], None, ALU.mult).then_inc(carry_ready[m], 1)

            def finish_scan(c):
                dve.wait_ge(red_done, (c + 1) * DV)
                wait(dve, ap_psum, c * 2)
                for f in range(2):
                    last = nc.vector.tensor_tensor(oT[:, f, :], op[f][:, :], vq[:, f, :], ALU.add)
                last.then_inc(oT_ready, 1)

            def finish_rows(c, q):
                wait(dve, h_stored, c * 16)
                for m in range(2):
                    dve.wait_ge(ap_psum, c * 2 + m + 1)
                    nc.vector.tensor_tensor(h_new[:, 2 * m:2 * m + 2, :],
                                            mm[m][:, :].rearrange("p (j d) -> p j d", j=2),
                                            hb[q][:, 2 * m:2 * m + 2, :], ALU.add).then_inc(hnew_ready, 1)

            def body(c, q, first, last):
                for vi in range(DV):
                    s = vi % RING
                    if vi == 0:
                        for s2 in range(2):
                            dve.wait_ge(qpT_ready[s2], c * 2 + 2)
                    wait(dve, red_done, c * DV + vi - RING + 1)
                    if vi in (0, 8):
                        dve.wait_ge(carry_ready[vi // 8], c + 1)
                    for f in range(2):
                        dve.wait_ge(bc_psum[f], c * DV + vi + 1)
                        nc.vector.tensor_tensor_scan(z[s][:, f, :], bc[f][:, :], qp[q][:, 1, f, :],
                                                     carry[:, vi, f:f + 1], ALU.add,
                                                     ALU.mult).then_inc(scan_done[f], 1)
                    if vi == AT["o"] and not first:
                        finish_scan(c - 1)
                    if vi == AT["vq"]:
                        dve.wait_ge(sumq_psum, c * 2 + 2)
                        wait(dve, oT_ready, c)
                        for f in range(2):
                            ins = nc.vector.tensor_tensor(vq[:, f, :], mm[f][:, :], v[:, f, 1:T + 1], ALU.mult)
                        ins.then_inc(vq_ready, 1)
                    if vi == AT["rows"] and not first:
                        finish_rows(c - 1, 1 - q)
                    if vi == 4:
                        carry_half(c, 1)
                    if not last:
                        front(c + 1, 1 - q, vi)
                        if vi == 12:
                            carry_half(c + 1, 0)

            def front0(fc, fq):
                front(fc, fq)
                carry_half(0, 0)

            def h_count(fc, fq):
                return (fc - fq) * 8 + 16

            sweep(dve, chunks, front0, body)
            finish_scan(chunks - 1)
            finish_rows(chunks - 1, 1)

        @block.scalar
        def _(act):
            act.wait_ge(consts, DV + 1)

            def front(fc, fq, k=None):
                if k in (None, AT["x_copy"]):
                    for f in range(2):
                        act.wait_ge(xT_psum, fc * 2 + f + 1)
                        wait(act, lg_psum[1], fc * 2)
                        nc.scalar.copy(xT[:, f, :], tp[f][:, :]).then_inc(xT_ready, 1)
                if k in (None, AT["v_copy"]):
                    act.wait_ge(vcarry_ready, fc + 1)
                    wait(act, vq_ready, fc)
                    for f in range(2):
                        act.wait_ge(v_psum, fc * 2 + f + 1)
                        nc.scalar.copy(v[:, f, 1:T + 1], mm[f][:, :]).then_inc(v_ready, 1)
                if k in (None, AT["hi"]):
                    act.wait_ge(dv_ready, fc + 1)
                    wait(act, rest2_ready, fc)
                    if past(fc, 1):
                        act.wait_ge(stacked[1 - fq], (fc + fq) * (STACKED // 2))
                    nc.scalar.copy(dvs[0][:, :, :], dv[:, :, :]).then_inc(hi_ready, 1)
                if k in (None, AT["mid"]):
                    act.wait_ge(rest1_ready, fc + 1)
                    nc.scalar.copy(dvs[1][:, :, :], dv[:, :, :]).then_inc(mid_ready, 1)
                if k in (None, AT["lo"]):
                    act.wait_ge(rest2_ready, fc + 1)
                    nc.scalar.copy(dvs[2][:, :, :], dv[:, :, :]).then_inc(lo_ready, 1)
                for j in range(TJ):
                    s = j % 2
                    if k in (None, EXP_AT[j]):
                        act.wait_ge(nmx_ready, fc * TJ + j + 1)
                        act.wait_ge(lg_psum[s], fc * 2 + j // 2 + 1)
                        wait(act, qpT_psum[s], fc * 2 + j // 2)
                        wait(act, rsum_ready, fc * TJ + j - 1)
                        for w in range(2):
                            last = nc.scalar.activation(ex[s][:, w, :], mm[s][:, w * D:(w + 1) * D], ACT.Exp,
                                                        bias=nmx[s][:, w:w + 1], accum_out=sums[s][:, w:w + 1])
                        last.then_inc(exp_done[s], 1)
                    if k in (None, QP_AT[j]):
                        act.wait_ge(qpT_psum[s], fc * 2 + j // 2 + 1)
                        if j == 0 and (not isinstance(fc, int) or fc >= 2):
                            act.wait_ge(g_ready, (fc - 1) * DV)
                            act.wait_ge(sumq_psum, (fc - 1) * 2)
                        nc.scalar.copy(qp[fq][:, :, :, j * P:(j + 1) * P],
                                       tp[s][:, :].rearrange("p (w f t) -> p w f t", w=2, f=2)
                                       ).then_inc(qpT_ready[s], 1)

            def body(c, q, first, last):
                for vi in range(DV):
                    if not last:
                        front(c + 1, 1 - q, vi)

            sweep(act, chunks, front, body)

        @block.tensor
        def _(pe):
            pe.wait_ge(loaded, 8 * 16)
            pe.wait_ge(consts, DV + 1)

            def front(fc, fq, k=None):
                if k in (None, AT["x_T"]):
                    pe.wait_ge(xh_ready, fc + 1)
                    for f in range(2):
                        wait(pe, qpT_ready[f], fc * 2)
                        for j in range(TJ):
                            last = nc.tensor.transpose(tp[f][:, j * P:(j + 1) * P], xh[:, j, f * P:(f + 1) * P],
                                                       core.ident[:, :])
                        last.then_inc(xT_psum, 1)
                if k in (None, AT["v"]):
                    pe.wait_ge(xT_ready, fc * 2 + 2)
                    if not isinstance(fc, int) or fc >= 2:
                        pe.wait_ge(hnew_ready, (fc - 1) * 2)
                    elif fc == 1:
                        pe.wait_ge(vq_ready, 1)
                    for f in range(2):
                        for kk in range(2):
                            last = nc.tensor.matmul(mm[f][:, :], wi[:, kk, f * P:(f + 1) * P], xT[:, kk, :],
                                                    start=(kk == 0), stop=(kk == 1))
                        last.then_inc(v_psum, 1)
                for j in range(TJ):
                    s = j % 2
                    if k in (None, LOGIT_AT[j]):
                        if j < 2:
                            pe.wait_ge(v_ready, fc * 2 + s + 1)
                        wait(pe, exp_done[s], fc * 2 + j // 2)
                        for kk in range(2):
                            last = nc.tensor.matmul(mm[s][:, :], xT[:, kk, j * P:(j + 1) * P], wqf[:, kk, :],
                                                    start=(kk == 0), stop=(kk == 1))
                        last.then_inc(lg_psum[s], 1)
                    if k in (None, QP_T_AT[j]):
                        pe.wait_ge(qp_ready, fc * TJ + j + 1)
                        wait(pe, qpT_ready[s], fc * 2 + j // 2)
                        for w in range(2):
                            for f in range(2):
                                last = nc.tensor.transpose(tp[s][:, (2 * w + f) * P:(2 * w + f + 1) * P],
                                                           ex[s][:, w, f * P:(f + 1) * P], core.ident[:, :])
                        last.then_inc(qpT_psum[s], 1)

            def spread_dv(c, q, vi):
                if vi == 0:
                    pe.wait_ge(stacked[q], (c - q) * (STACKED // 2) + STACKED)
                for f in range(2):
                    wait(pe, scan_done[f], c * DV + vi)
                    nc.tensor.matmul(bc[f][:, :], pick[:, vi % L, :, :].rearrange("p h k -> p (h k)"),
                                     stack[q][:, vi // L, f, :], start=True, stop=True).then_inc(bc_psum[f], 1)

            def reduce(c, vi):
                if vi == 0:
                    wait(pe, oT_ready, c)
                pe.wait_ge(g_ready, c * DV + vi + 1)
                for f in range(2):
                    last = nc.tensor.matmul(op[f][:, :], gather[:, vi, :, :, :].rearrange("p g h l -> p (g h l)"), z[vi % RING][:, f, :],
                                            start=(vi == 0), stop=(vi == DV - 1))
                last.then_inc(red_done, 1)

            def project(c):
                pe.wait_ge(oT_ready, c + 1)
                for m in range(2):
                    for j in range(2):
                        t0 = (2 * m + j) * P
                        for f in range(2):
                            last = nc.tensor.matmul(mm[m][:, j * D:(j + 1) * D], oT[:, f, t0:t0 + P], wo[:, f, :],
                                                    start=(f == 0), stop=(f == 1))
                    last.then_inc(ap_psum, 1)

            def body(c, q, first, last):
                for vi in range(DV):
                    if vi + 1 < DV:
                        spread_dv(c, q, vi + 1)
                    elif not last:
                        front(c + 1, 1 - q, vi)
                        spread_dv(c + 1, 1 - q, 0)
                    if vi > 0:
                        reduce(c, vi - 1)
                    elif not first:
                        reduce(c - 1, DV - 1)
                    if vi == AT["sum_q"]:
                        for s in range(2):
                            pe.wait_ge(exp_done[s], c * 2 + 2)
                        for f in range(2):
                            ins = nc.tensor.matmul(mm[f][:, :], head_sq[:, :, :, :].rearrange("p g h l -> p (g h l)"),
                                                   qp[q][:, 0, f, :], start=True, stop=True)
                        ins.then_inc(sumq_psum, 2)
                    if vi == AT["wo"] and not first:
                        pe.wait_ge(vq_ready, c + 1)
                        project(c - 1)
                    if not last and vi + 1 < DV:
                        front(c + 1, 1 - q, vi)

            def front0(fc, fq):
                front(fc, fq)
                for s in range(2):
                    pe.wait_ge(qpT_ready[s], 2)
                spread_dv(0, 0, 0)

            sweep(pe, chunks, front0, body)
            reduce(chunks - 1, DV - 1)
            project(chunks - 1)


def ffn_phase(core, gate_wT, down_T, down_bT, up_T, up_b, h_in, h_out):
    nc, bank, chunks = core.nc, core.bank, core.chunks
    NC = core.chunks_per_batch
    S = NC * T
    E = gate_wT.shape[1]
    C = down_T.shape[2]
    batches = chunks // NC
    with ExitStack() as ctx:
        def sb(name, shape, dt=F32):
            return ctx.enter_context(nc.sbuf_tensor("f_" + name, shape, dt))

        def sem(name):
            return nc.alloc_semaphore(name="f_" + name)

        passed = sem("passed")

        gw = sb("gw", [P, 2, E])
        dw = sb("dw", [P, 2, E, C])
        db = sb("db", [2 * C, E])
        uw = sb("uw", [2 * C, E, D])
        ub = sb("ub", [E, D])
        lower = sb("lower", [P, E, E])
        hb = [sb(f"hb{q}", [P, NC, TJ, D]) for q in range(2)]
        bn = sb("bn", [P, TJ, 6])
        mv = sb("mv", [P, TJ, 2])
        rstd = sb("rstd", [P, TJ])
        xh = [sb(f"xh{s}", [P, TJ, D]) for s in range(2)]
        xT = [sb(f"xT{q}", [P, 2, S]) for q in range(2)]
        sums = sb("sums", [P, 2, NC])
        pooled = sb("pooled", [P, 2])
        pooled_b = sb("pooled_b", [P, 2, P])
        g8 = sb("g8", [P, E])
        small = sb("small", [P, 8])
        cmp_a = sb("cmp_a", [P, E, E])
        cmp_b = sb("cmp_b", [P, E, E])
        rank = sb("rank", [P, E])
        sel = sb("sel", [P, 2, E])
        selg = sb("selg", [P, 2, E])
        wsum = sb("wsum", [P, E])
        wsumT = sb("wsumT", [E, P])
        upb = sb("upb", [P, D])
        rows = sb("rows", [2 * C, 2, E])
        prod = sb("prod", [2 * C, E])
        bsel = [sb(f"bsel{q}", [2 * C, 1]) for q in range(2)]
        wd = [sb(f"wd{q}", [P, 2, 2, C]) for q in range(2)]
        wu = [sb(f"wu{q}", [2 * C, D]) for q in range(2)]
        hid = [sb(f"hid{s}", [2 * C, T]) for s in range(2)]
        h_new = [sb(f"h_new{s}", [P, TJ, D]) for s in range(2)]

        loaded, lower_step = sem("loaded"), sem("lower_step")
        h_loaded = [sem(f"h_loaded{q}") for q in range(2)]
        bn_done, stats_ready, var_eps, rstd_ready, xh_ready = (
            sem("bn_done"), sem("stats_ready"), sem("var_eps"), sem("rstd_ready"), sem("xh_ready"))
        xT_psum, xT_ready = sem("xT_psum"), sem("xT_ready")
        gate_step, pooled_ready, gate_psum, gate_exp = (
            sem("gate_step"), sem("pooled_ready"), sem("gate_psum"), sem("gate_exp"))
        wsum_psum, chosen = sem("wsum_psum"), sem("chosen")
        upb_psum, upb_ready, biased = sem("upb_psum"), sem("upb_ready"), sem("biased")
        hid_psum, hid_ready, up_psum, hnew_ready = sem("hid_psum"), sem("hid_ready"), sem("up_psum"), sem("hnew_ready")
        stored = [sem(f"stored{s}") for s in range(2)]
        block = ctx.enter_context(nc.Block())
        hin, hout = chunk_view(h_in), chunk_view(h_out)
        GATE_STEPS = 18 + 3 * E

        @block.sync
        def _(sp):
            for k in range(2):
                sp.dma_start(gw[:, k, :], gate_wT[k * P:(k + 1) * P, :]).then_inc(loaded, 16)
                sp.dma_start(dw[:, k, :, :], down_T[k * P:(k + 1) * P, :, :]).then_inc(loaded, 16)
                sp.dma_start(db[k * C:(k + 1) * C, :], down_bT).then_inc(loaded, 16)
                sp.dma_start(uw[k * C:(k + 1) * C, :, :], up_T).then_inc(loaded, 16)
            sp.dma_start(ub[:, :], up_b).then_inc(loaded, 16)

            def load(b, q):
                wait(sp, hnew_ready, (b - 1) * (2 * NC))
                for m in range(NC):
                    sp.dma_start(hb[q][:, m, :, :], one(hin, b * NC + m)).then_inc(h_loaded[q], 16)

            def body(b, q, first, last):
                if not last:
                    load(b + 1, 1 - q)
                for m in range(NC):
                    sp.wait_ge(hnew_ready, b * (2 * NC) + 2 * m + 2)
                    sp.dma_start(one(hout, b * NC + m), h_new[m % 2][:, :, :]).then_inc(stored[m % 2], 16)

            sweep(sp, batches, load, body)
            for s in range(2):
                sp.wait_ge(stored[s], 16 * chunks // 2)

        @block.gpsimd
        def _(pool):
            nc.gpsimd.memset(lower[:, :, :], 1.0).then_inc(lower_step, 1)
            pool.wait_ge(lower_step, 1)
            nc.gpsimd.affine_select(out=lower[:, :, :], in_=lower[:, :, :], compare_op=ALU.is_gt, fill=0.0, base=0,
                                    pattern=[[1, E], [-1, E]], channel_multiplier=0).then_inc(lower_step, 1)
            def scale(b, m):
                c = b * NC + m
                pool.wait_ge(stats_ready, c + 1)
                wait(pool, xh_ready, c)
                nc.gpsimd.tensor_tensor(rstd[:, :], mv[:, :, 1], core.eps[:, 0:mv.shape[1]], ALU.add).then_inc(var_eps, 1)
                pool.wait_ge(var_eps, c + 1)
                nc.gpsimd.tensor_tensor(rstd[:, :], rstd[:, :], core.neg_half[:, 0:TJ],
                                        ALU.pow).then_inc(rstd_ready, 1)

            def front(b, q):
                for m in range(NC):
                    scale(b, m)

            def body(b, q, first, last):
                if not last:
                    scale(b + 1, 0)
                for m in range(NC):
                    if not last and m + 1 < NC:
                        scale(b + 1, m + 1)
                    pool.wait_ge(upb_ready, b + 1)
                    pool.wait_ge(xh_ready, b * NC + m + 1)
                    nc.gpsimd.tensor_tensor(hb[q][:, m, :, :], hb[q][:, m, :, :],
                                            upb[:, :].unsqueeze(1).to_broadcast([P, TJ, D]), ALU.add).then_inc(biased, 1)

            sweep(pool, batches, front, body)

        @block.vector
        def _(dve):
            dve.wait_ge(loaded, 9 * 16)
            dve.wait_ge(lower_step, 2)
            def normalise(b, q, m):
                c = b * NC + m
                if m == 0:
                    dve.wait_ge(h_loaded[q], (b - q) * (8 * NC) + 16 * NC)
                for j in range(TJ):
                    last = nc.vector.bn_stats(bn[:, j, :], hb[q][:, m, j, :])
                last.then_inc(bn_done, 1)
                dve.wait_ge(bn_done, c + 1)
                wait(dve, rstd_ready, c)
                hold(dve, passed)
                for j in range(TJ):
                    last = nc.vector.bn_aggr(mv[:, j, :], bn[:, j, :])
                last.then_inc(stats_ready, 1)
                dve.wait_ge(stats_ready, c + 1)
                dve.wait_ge(rstd_ready, c + 1)
                wait(dve, xT_psum, (c - 1) * 2)
                for j in range(TJ):
                    last = nc.vector.tensor_scalar(xh[m % 2][:, j, :], hb[q][:, m, j, :], mv[:, j, 0:1],
                                                   rstd[:, j:j + 1], ALU.subtract, ALU.mult)
                last.then_inc(xh_ready, 1)

            def choose(b, q):
                steps = [0]

                def step(ins):
                    ins.then_inc(gate_step, 1)
                    steps[0] += 1
                    wait(dve, gate_step, b * GATE_STEPS + steps[0])

                wait(dve, xT_ready, b * (2 * NC) + 2 * NC)
                wait(dve, gate_psum, b)
                step(nc.vector.tensor_reduce(pooled[:, :], sums[:, :, :], AX.X, ALU.add))
                for k in range(2):
                    last = nc.vector.tensor_scalar(pooled_b[:, k, :], core.ones[:, :], pooled[:, k:k + 1], 1.0 / S,
                                                   ALU.mult, ALU.mult)
                last.then_inc(pooled_ready, 1)
                wait(dve, gate_psum, b + 1)
                step(nc.vector.tensor_reduce(small[:, 0:1], bank[2][:, 0:E], AX.X, ALU.max, negate=True))
                wait(dve, gate_exp, b + 1)
                step(nc.vector.reciprocal(small[:, 2:3], small[:, 1:2]))
                step(nc.vector.tensor_scalar(g8[:, :], g8[:, :], small[:, 2:3], None, ALU.mult))
                g_of_j = g8[:, :].unsqueeze(1).to_broadcast([P, E, E])
                g_of_e = g8[:, :].unsqueeze(2).to_broadcast([P, E, E])
                nc.vector.tensor_tensor(cmp_a[:, :, :], g_of_j, g_of_e, ALU.is_gt)
                step(nc.vector.tensor_tensor(cmp_b[:, :, :], g_of_j, g_of_e, ALU.is_equal))
                step(nc.vector.tensor_tensor(cmp_b[:, :, :], cmp_b[:, :, :], lower[:, :, :], ALU.mult))
                step(nc.vector.tensor_tensor(cmp_a[:, :, :], cmp_a[:, :, :], cmp_b[:, :, :], ALU.add))
                step(nc.vector.tensor_reduce(rank[:, :], cmp_a[:, :, :], AX.X, ALU.add))
                for k in range(2):
                    last = nc.vector.tensor_scalar(sel[:, k, :], rank[:, :], float(k), None, ALU.is_equal)
                step(last)
                step(nc.vector.tensor_tensor(selg[:, :, :], sel[:, :, :], g8[:, :].unsqueeze(1).to_broadcast([P, 2, E]),
                                             ALU.mult))
                step(nc.vector.tensor_reduce(small[:, 3:5], selg[:, :, :], AX.X, ALU.add))
                step(nc.vector.tensor_tensor(small[:, 5:6], small[:, 3:4], small[:, 4:5], ALU.add))
                step(nc.vector.tensor_scalar(small[:, 5:6], small[:, 5:6], 1e-8, None, ALU.add))
                step(nc.vector.reciprocal(small[:, 6:7], small[:, 5:6]))
                step(nc.vector.tensor_scalar(selg[:, :, :], selg[:, :, :], small[:, 6:7], None, ALU.mult))
                step(nc.vector.tensor_tensor(wsum[:, :], selg[:, 0, :], selg[:, 1, :], ALU.add))
                for k in range(2):
                    nc.vector.tensor_copy(rows[k * C:(k + 1) * C, 0, :], sel[k * C:(k + 1) * C, k, :])
                    last = nc.vector.tensor_copy(rows[k * C:(k + 1) * C, 1, :], selg[k * C:(k + 1) * C, k, :])
                step(last)
                wait(dve, up_psum, (b - 1) * (2 * NC))
                wait(dve, hid_ready, (b - 1) * NC)
                for e in range(E):
                    for out, term, factor in ((wd[q][:, :, 0, :], dw[:, :, e, :], sel[:, 0, e:e + 1]),
                                              (wd[q][:, :, 1, :], dw[:, :, e, :], sel[:, 1, e:e + 1]),
                                              (wu[q][:, :], uw[:, e, :], rows[:, 1, e:e + 1])):
                        wait(dve, gate_step, b * GATE_STEPS + steps[0] - 2)
                        if e == 0:
                            ins = nc.vector.tensor_scalar(out, term, factor, None, ALU.mult)
                        else:
                            ins = nc.vector.scalar_tensor_tensor(out, term, factor, out, ALU.mult, ALU.add)
                        ins.then_inc(gate_step, 1)
                        steps[0] += 1
                step(nc.vector.tensor_tensor(prod[:, :], rows[:, 0, :], db[:, :], ALU.mult))
                assert steps[0] == GATE_STEPS, steps
                nc.vector.tensor_reduce(bsel[q][:, :], prod[:, :], AX.X, ALU.add).then_inc(chosen, 1)
                wait(dve, wsum_psum, b + 1)
                nc.vector.tensor_copy(wsumT[:, :], bank[2][0:E, P:2 * P]).then_inc(chosen, 1)

            def finish(b, q, m):
                wait(dve, stored[m % 2], b * (8 * NC) + 16 * (m // 2))
                dve.wait_ge(biased, b * NC + m + 1)
                for r in range(2):
                    dve.wait_ge(up_psum, b * (2 * NC) + 2 * m + r + 1)
                    nc.vector.tensor_tensor(h_new[m % 2][:, 2 * r:2 * r + 2, :],
                                            bank[5 + r][:, :].rearrange("p (j d) -> p j d", j=2),
                                            hb[q][:, m, 2 * r:2 * r + 2, :], ALU.add).then_inc(hnew_ready, 1)

            def front(b, q):
                for m in range(NC):
                    normalise(b, q, m)
                choose(b, q)

            def body(b, q, first, last):
                if not last:
                    normalise(b + 1, 1 - q, 0)
                for m in range(NC):
                    if not last and m + 1 < NC:
                        normalise(b + 1, 1 - q, m + 1)
                    finish(b, q, m)
                if not last:
                    choose(b + 1, 1 - q)

            sweep(dve, batches, front, body)

        @block.scalar
        def _(act):
            def copy(b, q, m):
                for f in range(2):
                    act.wait_ge(xT_psum, b * (2 * NC) + 2 * m + f + 1)
                    if m == 0:
                        wait(act, hid_psum, (b - 1) * NC)
                        wait(act, pooled_ready, b)
                    nc.scalar.activation(xT[q][:, f, m * T:(m + 1) * T], bank[f][:, :], ACT.Copy,
                                         accum_out=sums[:, f, m:m + 1]).then_inc(xT_ready, 1)

            def gate(b):
                act.wait_ge(gate_step, b * GATE_STEPS + 2)
                wait(act, wsum_psum, b)
                nc.scalar.activation(g8[:, :], bank[2][:, 0:E], ACT.Exp, bias=small[:, 0:1],
                                     accum_out=small[:, 1:2]).then_inc(gate_exp, 1)

            def front(b, q):
                for m in range(NC):
                    copy(b, q, m)
                gate(b)

            def body(b, q, first, last):
                act.wait_ge(chosen, b * 2 + 1)
                act.wait_ge(upb_psum, b + 1)
                wait(act, biased, b * NC)
                nc.scalar.copy(upb[:, :], bank[7][:, 0:D]).then_inc(upb_ready, 1)
                for m in range(NC):
                    act.wait_ge(hid_psum, b * NC + m + 1)
                    wait(act, up_psum, b * (2 * NC) + 2 * (m - 1))
                    nc.scalar.activation(hid[m % 2][:, :], bank[3 + m % 2][:, :], ACT.Gelu,
                                         bias=bsel[q][:, :]).then_inc(hid_ready, 1)
                    if not last:
                        copy(b + 1, 1 - q, m)
                if not last:
                    gate(b + 1)

            sweep(act, batches, front, body)

        @block.tensor
        def _(pe):
            pe.wait_ge(loaded, 9 * 16)
            def turn_over(b, q, m):
                pe.wait_ge(xh_ready, b * NC + m + 1)
                for f in range(2):
                    wait(pe, xT_ready, b * (2 * NC) + 2 * m + f - 1)
                    for j in range(TJ):
                        last = nc.tensor.transpose(bank[f][:, j * P:(j + 1) * P],
                                                   xh[m % 2][:, j, f * P:(f + 1) * P], core.ident[:, :])
                    last.then_inc(xT_psum, 1)

            def gate(b):
                pe.wait_ge(pooled_ready, b + 1)
                wait(pe, chosen, b * 2)
                for k in range(2):
                    last = nc.tensor.matmul(bank[2][:, 0:E], pooled_b[:, k, :], gw[:, k, :], start=(k == 0),
                                            stop=(k == 1))
                last.then_inc(gate_psum, 1)
                pe.wait_ge(gate_step, b * GATE_STEPS + 16)
                nc.tensor.transpose(bank[2][0:E, P:2 * P], wsum[:, :], core.ident[:, :]).then_inc(wsum_psum, 1)

            def down(b, q, m):
                wait(pe, hid_ready, b * NC + m - 1)
                for k in range(2):
                    last = nc.tensor.matmul(bank[3 + m % 2][:, :], wd[q][:, k, :, :].rearrange("p k c -> p (k c)"),
                                            xT[q][:, k, m * T:(m + 1) * T], start=(k == 0), stop=(k == 1))
                last.then_inc(hid_psum, 1)

            def up(b, q, m):
                pe.wait_ge(hid_ready, b * NC + m + 1)
                for r in range(2):
                    wait(pe, hnew_ready, b * (2 * NC) + 2 * m + r - 1)
                    for j in range(2):
                        t0 = (2 * r + j) * P
                        last = nc.tensor.matmul(bank[5 + r][:, j * D:(j + 1) * D], hid[m % 2][:, t0:t0 + P], wu[q][:, :],
                                                start=True, stop=True)
                    last.then_inc(up_psum, 1)

            def front(b, q):
                for m in range(NC):
                    turn_over(b, q, m)
                gate(b)

            def body(b, q, first, last):
                pe.wait_ge(chosen, b * 2 + 2)
                wait(pe, upb_ready, b)
                nc.tensor.matmul(bank[7][:, 0:D], wsumT[:, :], ub[:, :], start=True, stop=True).then_inc(upb_psum, 1)
                for m in range(NC):
                    down(b, q, m)
                    if m:
                        up(b, q, m - 1)
                    if not last:
                        turn_over(b + 1, 1 - q, m)
                up(b, q, NC - 1)
                if not last:
                    gate(b + 1)

            sweep(pe, batches, front, body)


def ssm_phase(core, w, h_in, h_out):
    nc, bank, chunks = core.nc, core.bank, core.chunks
    N = w["A_log"].shape[1]
    FB = w["ff1_w"].shape[1] // P
    R = 3 * 2 * N
    LAG = 2
    AHEAD = 2
    AT = dict(
        ln1_stats=-9, ln1=-6, lnn_stats=-5, lnn=-3, x1_first=1, conv=3, silu=5, abs_dt=8,
        softplus=10, rest_mid=9, gate=11, rest_lo=11, y=2, x2=4, ln2=6, h_new=16,
        dtx=9, gated=2, rstd=-9, affine=-7, rstd_n=-5, x_res=4, rstd2=4, add_h=6, add_b=7,
        xm_copy=0, x1_copy=1, conv_tanh=3, dt_copy=7, bc_copy=6, log=8, part_hi=7, gate_tanh=9,
        part_mid=10, part_lo=13, xn2_copy=7,
        xm_T=0, w1=1, dt=7, bc=6, v1=9, w2=2, xn2_T=7,
    )
    FF1_AT, GELU_AT, FF2_AT = (8, 11, 12), (11, 12), (13, 13, 14, 14)
    RING = 4
    with ExitStack() as ctx:
        def sb(name, shape, dt=F32):
            return ctx.enter_context(nc.sbuf_tensor("s_" + name, shape, dt))

        def sem(name):
            return nc.alloc_semaphore(name="s_" + name)

        passed = sem("passed")

        mats = {name: sb(name, [P, 2, D]) for name in ("w1_w", "v1_w", "w2_w", "dt_w")}
        ff1 = sb("ff1", [P, 2, FB * P])
        ff2 = sb("ff2", [P, FB, D])
        bcw = sb("bcw", [P, 2, 3, 2 * N])
        bcb = sb("bcb", [R, 1])
        cols = {name: sb(name, [P, 2]) for name in ("ln_g", "ln_b", "w1_b", "v1_b", "dt_b", "D_p", "ln2_g", "ln2_b")}
        half_v1b = sb("half_v1b", [P, 2])
        conv = sb("conv", [P, 2, 3])
        half_conv = sb("half_conv", [P, 2, 3])
        ff1b = sb("ff1b", [P, FB])
        A_log = sb("A_log", [P, 2, N])
        A = sb("A", [P, 2, N])
        A_neg = sb("A_neg", [P, 2, N])
        g1 = sb("g1", [P, D])
        b1 = sb("b1", [P, D])
        w2b = sb("w2b", [P, D])
        endb = sb("endb", [P, D])
        pick = sb("pick", [R, 2 * N], BF16)

        hb = [sb(f"hb{q}", [P, TJ + 1, D]) for q in range(2)]
        bn = sb("bn", [P, TJ + 1, 6])
        mv = sb("mv", [P, TJ + 1, 2])
        rstd = sb("rstd", [P, TJ + 1])
        rstd_n = sb("rstd_n", [P, TJ + 1])
        xh = sb("xh", [P, TJ + 1, D])
        xn = sb("xn", [P, TJ + 1, D])
        xres = [sb(f"xres{q}", [P, TJ, D]) for q in range(2)]
        hres = sb("hres", [P, TJ, D])
        xmT = sb("xmT", [P, 2, T + 1])
        x1 = sb("x1", [P, 2, T + 2])
        after = sb("after", [P, 2])
        cv = sb("cv", [P, 2, T])
        th = sb("th", [P, 2, T])
        xc = [sb(f"xc{q}", [P, 2, T]) for q in range(2)]
        xs = sb("xs", [P, 2, T])
        dt = [sb(f"dt{q}", [P, 2, T]) for q in range(2)]
        dtx = [sb(f"dtx{q}", [P, 2, T]) for q in range(2)]
        vg = [sb(f"vg{q}", [P, 2, T]) for q in range(2)]
        bcf = sb("bcf", [R, T])
        bcs = [sb(f"bcs{q}", [R, T], BF16) for q in range(2)]
        a = [sb(f"a{s}", [P, 2, T]) for s in range(RING)]
        hs = [sb(f"hs{s}", [P, 2, T]) for s in range(RING)]
        bs = [sb(f"bs{s}", [P, T]) for s in range(2)]
        cs = [sb(f"cs{s}", [P, T]) for s in range(RING)]
        zlast = sb("zlast", [P, N, 2])
        carry = sb("carry", [P, N, 2])
        yv = sb("yv", [P, 2, T])
        x2 = sb("x2", [P, TJ, D])
        bn2 = sb("bn2", [P, TJ, 6])
        mv2 = sb("mv2", [P, TJ, 2])
        rstd2 = sb("rstd2", [P, TJ])
        xn2 = sb("xn2", [P, TJ, D])
        xn2T = sb("xn2T", [P, 2, T])
        hid = sb("hid", [P, FB, T])
        h_new = sb("h_new", [P, TJ, D])

        bB, bC, yp, tp, mm = bank[0], bank[1], bank[2:4], bank[4:6], bank[6:8]

        loaded, pick_step, cleared, consts, A_done = (
            sem("loaded"), sem("pick_step"), sem("cleared"), sem("consts"), sem("A_done"))
        h_loaded = [sem(f"h_loaded{q}") for q in range(2)]
        bn_done, stats_ready, rstd_step, xh_ready, xn_ready, affine_ready, res_ready = (
            sem("bn_done"), sem("stats_ready"), sem("rstd_step"), sem("xh_ready"), sem("xn_ready"),
            sem("affine_ready"), sem("res_ready"))
        bnn_done, statsn_ready, xm_ready = sem("bnn_done"), sem("statsn_ready"), sem("xm_ready")
        xmT_psum, xmT_ready = sem("xmT_psum"), sem("xmT_ready")
        x1carry_ready, x1_psum, x1_ready, x1after_ready = (
            sem("x1carry_ready"), sem("x1_psum"), sem("x1_ready"), sem("x1after_ready"))
        conv_step, th_ready, xc_ready = sem("conv_step"), sem("th_ready"), sem("xc_ready")
        dt_psum, xs_ready, na_ready, ln1p_step, dt_ready, dtx_ready = (
            sem("dt_psum"), sem("xs_ready"), sem("na_ready"), sem("ln1p_step"), sem("dt_ready"), sem("dtx_ready"))
        bc_psum, bcf_ready, part_ready, rest_ready = sem("bc_psum"), sem("bcf_ready"), sem("part_ready"), sem("rest_ready")
        vg_psum, vb_ready, vth_ready, vg_ready = sem("vg_psum"), sem("vb_ready"), sem("vth_ready"), sem("vg_ready")
        B_psum, C_psum, u_ready, bs_ready, cs_ready, a_ready = (
            sem("B_psum"), sem("C_psum"), sem("u_ready"), sem("bs_ready"), sem("cs_ready"), sem("a_ready"))
        hres_loaded = sem("hres_loaded")
        scan_done = [sem(f"scan_done{f}") for f in range(2)]
        zlast_saved, g_ready, red_done = sem("zlast_saved"), sem("g_ready"), sem("red_done")
        carry_ready = [sem(f"carry_ready{m}") for m in range(2)]
        y_ready, yv_ready, mo_psum, x2_ready = sem("y_ready"), sem("yv_ready"), sem("mo_psum"), sem("x2_ready")
        bn2_done, stats2_ready, rstd2_step, xn2_ready, x2res_ready = (
            sem("bn2_done"), sem("stats2_ready"), sem("rstd2_step"), sem("xn2_ready"), sem("x2res_ready"))
        xn2T_psum, xn2T_ready, ff1_psum, hid_ready, ff2_psum, hnew_ready, h_stored = (
            sem("xn2T_psum"), sem("xn2T_ready"), sem("ff1_psum"), sem("hid_ready"), sem("ff2_psum"),
            sem("hnew_ready"), sem("h_stored"))
        block = ctx.enter_context(nc.Block())
        hin, hout = chunk_view(h_in), chunk_view(h_out)
        CONST = 3

        def further(c):
            return not isinstance(c, int) or c + 2 < chunks

        def fronts01(front):
            def both(fc, fq):
                front(0, 0)
                for n in range(N):
                    front(1, 1, n - N)
            return both

        loads = []
        for name in ("w1_w", "v1_w", "w2_w", "dt_w"):
            loads.append((mats[name][:, :, :], w[name].rearrange("(k p) n -> p k n", p=P)))
        loads.append((ff1[:, :, :], w["ff1_w"].rearrange("(k p) n -> p k n", p=P)))
        loads.append((ff2[:, :, :], w["ff2_w"].rearrange("(k p) n -> p k n", p=P)))
        for part in range(3):
            for m, name in enumerate(("Bp", "Cp")):
                loads.append((bcw[:, :, part, m * N:(m + 1) * N], w[name + "_w"].rearrange("(k p) n -> p k n", p=P)))
                r0 = (2 * part + m) * N
                loads.append((bcb[r0:r0 + N, :], w[name + "_b"]))
        for name in cols:
            loads.append((cols[name][:, :], w[name]))
        loads.append((conv[:, :, :], w["conv_w"].rearrange("(k p) o x -> p k (o x)", p=P)))
        loads.append((ff1b[:, :], w["ff1_b"]))
        loads.append((A_log[:, :, :], w["A_log"].rearrange("(k p) n -> p k n", p=P)))
        for tile, name in ((g1[:, :], "ln1_g"), (b1[:, :], "ln1_b"), (w2b[:, :], "w2_b"), (endb[:, :], "ff2_b"), (hres[:, 0, :], "moe_bias")):
            loads.append((tile, w[name].partition_broadcast(P)))
        LOADED = 16 * len(loads)

        @block.sync
        def _(sp):
            for dst, src in loads:
                sp.dma_start(dst, src).then_inc(loaded, 16)

            def load(fc, fq):
                wait(sp, xh_ready, fc - 1)
                sp.dma_start(hb[fq][:, 0:TJ, :], one(hin, fc)).then_inc(h_loaded[fq], 16)
                nxt = one(hin, (fc + 1) % chunks)
                sp.dma_start(hb[fq][0:1, TJ, :], nxt[0:1, 0, :]).then_inc(h_loaded[fq], 16)

            def store(c):
                sp.wait_ge(hnew_ready, c * 2 + 2)
                sp.dma_start(one(hout, c), h_new[:, :, :]).then_inc(h_stored, 16)

            def reload(c):
                wait(sp, x2res_ready, c * 2)
                if isinstance(c, int) and c == 0:
                    sp.wait_ge(consts, 3)
                sp.dma_start(hres[:, :, :], one(hin, c)).then_inc(hres_loaded, 16)

            def body(c, q, first, last):
                if further(c):
                    load(c + 2, q)
                if not first:
                    reload(c - 1)
                if past(c, 2):
                    store(c - 2)

            load(0, 0)
            sweep(sp, chunks, lambda fc, fq: load(1, 1), body)
            reload(chunks - 1)
            store(chunks - 2)
            store(chunks - 1)
            sp.wait_ge(h_stored, 16 * chunks)

        @block.gpsimd
        def _(pool):
            nc.gpsimd.memset(pick[:, :], 0.0).then_inc(pick_step, 1)
            for part in range(3):
                pool.wait_ge(pick_step, part + 1)
                nc.gpsimd.affine_select(out=pick[:, :], in_=pick[:, :], compare_op=ALU.not_equal, fill=1.0,
                                        base=-2 * N * part, pattern=[[-1, 2 * N]],
                                        channel_multiplier=1).then_inc(pick_step, 1)
            pool.wait_ge(pick_step, 4)
            nc.gpsimd.memset(mv[:, :, :], 1.0).then_inc(cleared, 1)
            nc.gpsimd.memset(x1[:, :, :], 0.0).then_inc(cleared, 1)
            nc.gpsimd.memset(zlast[:, :, :], 0.0).then_inc(cleared, 1)
            pool.wait_ge(cleared, 3)
            pool.wait_ge(loaded, LOADED)
            nc.gpsimd.tensor_tensor(endb[:, :], endb[:, :], hres[:, 0, :], ALU.add).then_inc(consts, 1)
            nc.gpsimd.tensor_scalar(half_v1b[:, :], cols["v1_b"][:, :], 0.5, None, ALU.mult).then_inc(consts, 1)
            nc.gpsimd.tensor_scalar(half_conv[:, :, :], conv[:, :, :], 0.5, None, ALU.mult).then_inc(consts, 1)
            pool.wait_ge(consts, 3)

            def front(fc, fq, k=None):
                if k in (None, AT["rstd"]):
                    pool.wait_ge(stats_ready, fc + 1)
                    wait(pool, xn_ready, fc)
                    wait(pool, xm_ready, fc)
                    base = fc * 8
                    seq = [
                        lambda: nc.gpsimd.tensor_tensor(rstd[:, :], mv[:, :, 1], core.eps[:, 0:mv.shape[1]], ALU.add),
                        lambda: nc.gpsimd.tensor_tensor(rstd[:, :], rstd[:, :], core.neg_half[:, 0:TJ + 1], ALU.pow),
                        lambda: nc.gpsimd.tensor_tensor(rstd_n[:, :], mv[:, :, 1], rstd[:, :], ALU.mult),
                        lambda: nc.gpsimd.tensor_tensor(rstd_n[:, :], rstd_n[:, :], rstd[:, :], ALU.mult),
                        lambda: nc.gpsimd.tensor_tensor(rstd_n[:, :], rstd_n[:, :], core.eps[:, 0:TJ + 1], ALU.add),
                        lambda: nc.gpsimd.tensor_tensor(rstd_n[:, :], rstd_n[:, :], core.neg_half[:, 0:TJ + 1], ALU.pow),
                    ]
                    for m, op in enumerate(seq):
                        op().then_inc(rstd_step, 1)
                        if m + 1 < len(seq):
                            pool.wait_ge(rstd_step, base + m + 1)
                if k in (None, AT["affine"]):
                    pool.wait_ge(xn_ready, fc + 1)
                    nc.gpsimd.tensor_tensor(xn[:, 0:TJ, :], xn[:, 0:TJ, :],
                                            b1[:, :].unsqueeze(1).to_broadcast([P, TJ, D]), ALU.add)
                    nc.gpsimd.tensor_tensor(xn[0:1, TJ, :], xn[0:1, TJ, :], b1[0:1, :], ALU.add).then_inc(affine_ready, 1)
                if k in (None, AT["x_res"]):
                    wait(pool, x2_ready, (fc - 1) * 2)
                    nc.gpsimd.tensor_tensor(xres[fq][:, :, :], xh[:, 0:TJ, :],
                                            w2b[:, :].unsqueeze(1).to_broadcast([P, TJ, D]), ALU.add).then_inc(res_ready, 1)
                if k in (None, AT["rstd_n"]):
                    pool.wait_ge(statsn_ready, fc + 1)
                    nc.gpsimd.tensor_tensor(rstd_n[:, :], mv[:, :, 1], core.eps[:, 0:mv.shape[1]], ALU.add).then_inc(rstd_step, 1)
                    pool.wait_ge(rstd_step, fc * 8 + 7)
                    nc.gpsimd.tensor_tensor(rstd_n[:, :], rstd_n[:, :], core.neg_half[:, 0:TJ + 1],
                                            ALU.pow).then_inc(rstd_step, 1)

                if k in (None, AT["dtx"]):
                    pool.wait_ge(dt_ready, fc + 1)
                    pool.wait_ge(xc_ready, fc + 1)
                    wait(pool, u_ready, (fc - 1) * N)
                    nc.gpsimd.tensor_tensor(dtx[fq][:, :, :], dt[fq][:, :, :], xc[fq][:, :, :],
                                            ALU.mult).then_inc(dtx_ready, 1)

            def fin(c, q, k):
                if k == AT["gated"]:
                    pool.wait_ge(y_ready, c + 1)
                    pool.wait_ge(vg_ready, c + 1)
                    nc.gpsimd.tensor_tensor(yv[:, :, :], yv[:, :, :], vg[q][:, :, :], ALU.mult).then_inc(yv_ready, 1)
                if k == AT["rstd2"]:
                    pool.wait_ge(stats2_ready, c + 1)
                    wait(pool, xn2_ready, c)
                    nc.gpsimd.tensor_tensor(rstd2[:, :], mv2[:, :, 1], core.eps[:, 0:mv2.shape[1]], ALU.add).then_inc(rstd2_step, 1)
                    pool.wait_ge(rstd2_step, c * 2 + 1)
                    nc.gpsimd.tensor_tensor(rstd2[:, :], rstd2[:, :], core.neg_half[:, 0:TJ],
                                            ALU.pow).then_inc(rstd2_step, 1)
                if k == AT["add_h"]:
                    pool.wait_ge(xn2_ready, c + 1)
                    pool.wait_ge(hres_loaded, c * 16 + 16)
                    nc.gpsimd.tensor_tensor(x2[:, :, :], x2[:, :, :], hres[:, :, :], ALU.add).then_inc(x2res_ready, 1)
                if k == AT["add_b"]:
                    pool.wait_ge(x2res_ready, c * 2 + 1)
                    nc.gpsimd.tensor_tensor(x2[:, :, :], x2[:, :, :], endb[:, :].unsqueeze(1).to_broadcast([P, TJ, D]),
                                            ALU.add).then_inc(x2res_ready, 1)

            def body(c, q, first, last):
                for n in range(N):
                    for f in range(2):
                        pool.wait_ge(scan_done[f], c * N + n + 1)
                    if n in (0, 8):
                        pool.wait_ge(carry_ready[n // 8], c + 1)
                    hold(pool, passed)
                    nc.gpsimd.tensor_copy(zlast[:, n, :], hs[n % RING][:, :, T - 1]).then_inc(zlast_saved, 1)
                    pool.wait_ge(zlast_saved, c * N + n + 1)
                    pool.wait_ge(cs_ready, c * N + n + 1)
                    nc.gpsimd.tensor_tensor(hs[n % RING][:, :, :], hs[n % RING][:, :, :],
                                            cs[n % RING][:, :].unsqueeze(1).to_broadcast([P, 2, T]),
                                            ALU.mult).then_inc(g_ready, 1)
                    if past(c, 2):
                        fin(c - 2, q, N + n)
                    if not first:
                        fin(c - 1, 1 - q, n)
                    if not last:
                        front(c + 1, 1 - q, n)
                    if further(c):
                        front(c + 2, q, n - N)

            sweep(pool, chunks, fronts01(front), body)
            for k in range(2 * N):
                fin(chunks - 2, 0, N + k)
                fin(chunks - 1, 1, k)

        @block.vector
        def _(dve):
            dve.wait_ge(loaded, LOADED)
            dve.wait_ge(consts, CONST)
            dve.wait_ge(A_done, 1)
            nc.vector.tensor_scalar(A_neg[:, :, :], A[:, :, :], -1.0, None, ALU.mult).then_inc(A_done, 1)

            def tiles(t, j):
                return t[:, j, :] if j < TJ else t[0:1, j, :]

            def front(fc, fq, k=None):
                if k in (None, AT["ln1_stats"]):
                    dve.wait_ge(h_loaded[fq], (fc - fq) * 16 + 32)
                    wait(dve, statsn_ready, fc)
                    for j in range(TJ + 1):
                        last = nc.vector.bn_stats(tiles(bn, j), tiles(hb[fq], j))
                    last.then_inc(bn_done, 1)
                    dve.wait_ge(bn_done, fc + 1)
                    wait(dve, rstd_step, fc * 8)
                    hold(dve, passed)
                    for j in range(TJ + 1):
                        last = nc.vector.bn_aggr(tiles(mv, j), tiles(bn, j))
                    last.then_inc(stats_ready, 1)
                if k in (None, AT["ln1"]):
                    dve.wait_ge(stats_ready, fc + 1)
                    dve.wait_ge(rstd_step, fc * 8 + 6)
                    wait(dve, res_ready, fc)
                    wait(dve, xmT_psum, fc * 3)
                    for j in range(TJ + 1):
                        one_row = slice(0, P if j < TJ else 1)
                        last = nc.vector.tensor_scalar(tiles(xh, j), tiles(hb[fq], j), mv[one_row, j, 0:1],
                                                       rstd[one_row, j:j + 1], ALU.subtract, ALU.mult)
                    last.then_inc(xh_ready, 1)
                    dve.wait_ge(xh_ready, fc + 1)
                    for j in range(TJ + 1):
                        one_row = slice(0, P if j < TJ else 1)
                        last = nc.vector.scalar_tensor_tensor(tiles(xn, j), tiles(xh, j), rstd_n[one_row, j:j + 1],
                                                              g1[one_row, :], ALU.mult, ALU.mult)
                    last.then_inc(xn_ready, 1)
                if k in (None, AT["lnn_stats"]):
                    dve.wait_ge(affine_ready, fc + 1)
                    for j in range(TJ + 1):
                        last = nc.vector.bn_stats(tiles(bn, j), tiles(xn, j))
                    last.then_inc(bnn_done, 1)
                    dve.wait_ge(bnn_done, fc + 1)
                    hold(dve, passed)
                    for j in range(TJ + 1):
                        last = nc.vector.bn_aggr(tiles(mv, j), tiles(bn, j))
                    last.then_inc(statsn_ready, 1)
                if k in (None, AT["lnn"]):
                    dve.wait_ge(statsn_ready, fc + 1)
                    dve.wait_ge(rstd_step, fc * 8 + 8)
                    for j in range(TJ + 1):
                        one_row = slice(0, P if j < TJ else 1)
                        last = nc.vector.tensor_scalar(tiles(xn, j), tiles(xn, j), mv[one_row, j, 0:1],
                                                       rstd_n[one_row, j:j + 1], ALU.subtract, ALU.mult)
                    last.then_inc(xm_ready, 1)
                if k in (None, AT["x1_first"]):
                    wait(dve, x1_ready, fc * 3)
                    wait(dve, conv_step, fc * 3)
                    nc.vector.tensor_scalar(x1[:, :, 0:1], x1[:, :, T:T + 1], core.keep[:, bass.ds(fc, 1)], None,
                                            ALU.mult).then_inc(x1carry_ready, 1)
                if k in (None, AT["conv"]):
                    dve.wait_ge(x1_ready, fc * 3 + 3)
                    dve.wait_ge(x1carry_ready, fc + 1)
                    nc.vector.tensor_scalar(x1[:, :, T + 1:T + 2], after[:, :].unsqueeze(2),
                                            core.keep[:, bass.ds(fc + 1, 1)], None, ALU.mult).then_inc(x1after_ready, 1)
                    dve.wait_ge(x1after_ready, fc + 1)
                    wait(dve, xc_ready, fc)
                    for f in range(2):
                        last = nc.vector.tensor_scalar(cv[:, f, :], x1[:, f, 0:T], half_conv[:, f, 0:1], None, ALU.mult)
                    last.then_inc(conv_step, 1)
                    for m in range(1, 3):
                        dve.wait_ge(conv_step, fc * 3 + m)
                        for f in range(2):
                            last = nc.vector.scalar_tensor_tensor(cv[:, f, :], x1[:, f, m:m + T], half_conv[:, f, m:m + 1],
                                                                  cv[:, f, :], ALU.mult, ALU.add)
                        last.then_inc(conv_step, 1)
                if k in (None, AT["silu"]):
                    dve.wait_ge(th_ready, fc + 1)
                    wait(dve, y_ready, fc - 1)
                    nc.vector.scalar_tensor_tensor(xc[fq][:, :, :], th[:, :, :], 1.0, cv[:, :, :], ALU.add,
                                                   ALU.mult).then_inc(xc_ready, 1)
                if k in (None, AT["abs_dt"]):
                    dve.wait_ge(xs_ready, fc * 2 + 2)
                    wait(dve, dt_ready, fc)
                    dve.wait_ge(xc_ready, fc + 1)
                    nc.vector.scalar_tensor_tensor(cv[:, :, :], xs[:, :, :], -1.0, xs[:, :, :], ALU.mult,
                                                   ALU.min).then_inc(na_ready, 1)
                if k in (None, AT["softplus"]):
                    dve.wait_ge(ln1p_step, fc * 2 + 2)
                    wait(dve, a_ready, (fc - 1) * N)
                    nc.vector.scalar_tensor_tensor(dt[fq][:, :, :], xs[:, :, :], 0.0, cv[:, :, :], ALU.max,
                                                   ALU.add).then_inc(dt_ready, 1)
                if k in (None, AT["rest_mid"]):
                    dve.wait_ge(part_ready, fc * 3 + 1)
                    lo = 2 * N
                    nc.vector.tensor_tensor(bcf[lo:2 * lo, :], bcf[lo:2 * lo, :], bcs[fq][lo:2 * lo, :], ALU.subtract)
                    nc.vector.tensor_tensor(bcf[2 * lo:R, :], bcf[2 * lo:R, :], bcs[fq][2 * lo:R, :],
                                            ALU.subtract).then_inc(rest_ready, 1)
                if k in (None, AT["gate"]):
                    dve.wait_ge(vth_ready, fc + 1)
                    wait(dve, yv_ready, fc - 1)
                    nc.vector.scalar_tensor_tensor(vg[fq][:, :, :], th[:, :, :], 1.0, cv[:, :, :], ALU.add,
                                                   ALU.mult).then_inc(vg_ready, 1)
                if k in (None, AT["rest_lo"]):
                    dve.wait_ge(part_ready, fc * 3 + 2)
                    lo = 4 * N
                    nc.vector.tensor_tensor(bcf[lo:R, :], bcf[lo:R, :], bcs[fq][lo:R, :],
                                            ALU.subtract).then_inc(rest_ready, 1)

            def fin(c, q, k):
                if k == AT["y"]:
                    dve.wait_ge(red_done, (c + 1) * N)
                    wait(dve, mo_psum, c * 2)
                    for f in range(2):
                        ins = nc.vector.scalar_tensor_tensor(yv[:, f, :], xc[q][:, f, :], cols["D_p"][:, f:f + 1],
                                                             yp[f][:, :], ALU.mult, ALU.add)
                    ins.then_inc(y_ready, 1)
                if k == AT["x2"]:
                    wait(dve, hnew_ready, c * 2)
                    dve.wait_ge(res_ready, c + 1)
                    for m in range(2):
                        dve.wait_ge(mo_psum, c * 2 + m + 1)
                        nc.vector.tensor_tensor(x2[:, 2 * m:2 * m + 2, :], mm[m][:, :].rearrange("p (j d) -> p j d", j=2),
                                                xres[q][:, 2 * m:2 * m + 2, :], ALU.add).then_inc(x2_ready, 1)
                    dve.wait_ge(x2_ready, c * 2 + 2)
                    for j in range(TJ):
                        ins = nc.vector.bn_stats(bn2[:, j, :], x2[:, j, :])
                    ins.then_inc(bn2_done, 1)
                    dve.wait_ge(bn2_done, c + 1)
                    wait(dve, rstd2_step, c * 2)
                    hold(dve, passed)
                    for j in range(TJ):
                        ins = nc.vector.bn_aggr(mv2[:, j, :], bn2[:, j, :])
                    ins.then_inc(stats2_ready, 1)
                if k == AT["ln2"]:
                    dve.wait_ge(stats2_ready, c + 1)
                    dve.wait_ge(rstd2_step, c * 2 + 2)
                    wait(dve, xn2T_psum, c * 2)
                    for j in range(TJ):
                        ins = nc.vector.tensor_scalar(xn2[:, j, :], x2[:, j, :], mv2[:, j, 0:1], rstd2[:, j:j + 1],
                                                      ALU.subtract, ALU.mult)
                    ins.then_inc(xn2_ready, 1)
                if k == AT["h_new"]:
                    wait(dve, h_stored, c * 16)
                    dve.wait_ge(x2res_ready, c * 2 + 2)
                    for m in range(2):
                        dve.wait_ge(ff2_psum, c * 2 + m + 1)
                        nc.vector.tensor_tensor(h_new[:, 2 * m:2 * m + 2, :],
                                                mm[m][:, :].rearrange("p (j d) -> p j d", j=2),
                                                x2[:, 2 * m:2 * m + 2, :], ALU.add).then_inc(hnew_ready, 1)

            def carry_half(c, m):
                wait(dve, zlast_saved, (c - 1) * N + N // 2 if m == 0 else c * N)
                nc.vector.tensor_scalar(carry[:, m * 8:(m + 1) * 8, :], zlast[:, m * 8:(m + 1) * 8, :],
                                        core.keep[:, bass.ds(c, 1)], None, ALU.mult).then_inc(carry_ready[m], 1)

            def body(c, q, first, last):
                for n in range(N):
                    s = n % RING
                    if n in (0, 8):
                        dve.wait_ge(carry_ready[n // 8], c + 1)
                    if n == 0:
                        dve.wait_ge(dtx_ready, c + 1)
                    dve.wait_ge(bs_ready, c * N + n + 1)
                    wait(dve, red_done, c * N + n - RING + 1)
                    nc.vector.tensor_tensor(hs[s][:, :, :], dtx[q][:, :, :], bs[n % 2][:, :].unsqueeze(1).to_broadcast([P, 2, T]),
                                            ALU.mult).then_inc(u_ready, 1)
                    dve.wait_ge(u_ready, c * N + n + 1)
                    dve.wait_ge(a_ready, c * N + n + 1)
                    for f in range(2):
                        nc.vector.tensor_tensor_scan(hs[s][:, f, :], a[s][:, f, :], hs[s][:, f, :], carry[:, n, f:f + 1],
                                                     ALU.mult, ALU.add).then_inc(scan_done[f], 1)
                    if past(c, 2):
                        fin(c - 2, q, N + n)
                    if not first:
                        fin(c - 1, 1 - q, n)
                    if n == 4:
                        carry_half(c, 1)
                    if not last:
                        front(c + 1, 1 - q, n)
                    if further(c):
                        front(c + 2, q, n - N)
                    if not last:
                        if n == 12:
                            carry_half(c + 1, 0)

            def front0(fc, fq):
                fronts01(front)(fc, fq)
                carry_half(0, 0)

            sweep(dve, chunks, front0, body)
            for k in range(2 * N):
                fin(chunks - 2, 0, N + k)
                fin(chunks - 1, 1, k)

        @block.scalar
        def _(act):
            act.wait_ge(loaded, LOADED)
            act.wait_ge(consts, CONST)
            nc.scalar.activation(A[:, :, :], A_log[:, :, :], ACT.Exp).then_inc(A_done, 1)
            act.wait_ge(A_done, 2)

            def front(fc, fq, k=None):
                if k in (None, AT["xm_copy"]):
                    wait(act, vg_psum, fc * 2)
                    for f in range(2):
                        act.wait_ge(xmT_psum, fc * 3 + f + 1)
                        nc.scalar.activation(xmT[:, f, 0:T], tp[f][:, :], ACT.Identity, bias=cols["ln_b"][:, f:f + 1],
                                             scale=cols["ln_g"][:, f:f + 1]).then_inc(xmT_ready, 1)
                    act.wait_ge(xmT_psum, fc * 3 + 3)
                    for f in range(2):
                        last = nc.scalar.activation(xmT[:, f, T:T + 1], mm[0][:, f:f + 1], ACT.Identity,
                                                    bias=cols["ln_b"][:, f:f + 1], scale=cols["ln_g"][:, f:f + 1])
                    last.then_inc(xmT_ready, 1)
                if k in (None, AT["x1_copy"]):
                    act.wait_ge(x1carry_ready, fc + 1)
                    wait(act, conv_step, fc * 3)
                    wait(act, x1after_ready, fc)
                    for f in range(2):
                        act.wait_ge(x1_psum, fc * 3 + f + 1)
                        nc.scalar.activation(x1[:, f, 1:T + 1], mm[f][:, :], ACT.Identity,
                                             bias=cols["w1_b"][:, f:f + 1]).then_inc(x1_ready, 1)
                    act.wait_ge(x1_psum, fc * 3 + 3)
                    for f in range(2):
                        last = nc.scalar.activation(after[:, f:f + 1], tp[0][:, f:f + 1], ACT.Identity,
                                                    bias=cols["w1_b"][:, f:f + 1])
                    last.then_inc(x1_ready, 1)
                if k in (None, AT["conv_tanh"]):
                    act.wait_ge(conv_step, fc * 3 + 3)
                    wait(act, vg_ready, fc)
                    nc.scalar.activation(th[:, :, :], cv[:, :, :], ACT.Tanh).then_inc(th_ready, 1)
                if k in (None, AT["bc_copy"]):
                    act.wait_ge(bc_psum, fc + 1)
                    wait(act, part_ready, fc * 3)
                    nc.scalar.activation(bcf[:, :], mm[0][0:R, :], ACT.Identity, bias=bcb[:, :]).then_inc(bcf_ready, 1)
                if k in (None, AT["dt_copy"]):
                    wait(act, dt_ready, fc)
                    for f in range(2):
                        act.wait_ge(dt_psum, fc * 2 + f + 1)
                        nc.scalar.activation(xs[:, f, :], mm[f][:, :], ACT.Identity,
                                             bias=cols["dt_b"][:, f:f + 1]).then_inc(xs_ready, 1)
                if k in (None, AT["log"]):
                    act.wait_ge(na_ready, fc + 1)
                    nc.scalar.activation(cv[:, :, :], cv[:, :, :], ACT.Exp).then_inc(ln1p_step, 1)
                    act.wait_ge(ln1p_step, fc * 2 + 1)
                    nc.scalar.activation(cv[:, :, :], cv[:, :, :], ACT.Ln, bias=core.ones[:, 0:1]).then_inc(ln1p_step, 1)
                if k in (None, AT["part_hi"]):
                    act.wait_ge(bcf_ready, fc + 1)
                    wait(act, C_psum, (fc - 1) * N)
                    nc.scalar.copy(bcs[fq][:, :], bcf[:, :]).then_inc(part_ready, 1)
                if k in (None, AT["gate_tanh"]):
                    act.wait_ge(dt_ready, fc + 1)
                    act.wait_ge(xc_ready, fc + 1)
                    for f in range(2):
                        act.wait_ge(vg_psum, fc * 2 + f + 1)
                        last = nc.scalar.activation(cv[:, f, :], mm[f][:, :], ACT.Identity, bias=half_v1b[:, f:f + 1],
                                                    scale=0.5)
                        last.then_inc(vb_ready, 1)
                    act.wait_ge(vb_ready, fc * 2 + 2)
                    nc.scalar.activation(th[:, :, :], cv[:, :, :], ACT.Tanh).then_inc(vth_ready, 1)
                if k in (None, AT["part_mid"]):
                    act.wait_ge(rest_ready, fc * 2 + 1)
                    lo = 2 * N
                    nc.scalar.copy(bcs[fq][lo:2 * lo, :], bcf[lo:2 * lo, :])
                    nc.scalar.copy(bcs[fq][2 * lo:R, :], bcf[2 * lo:R, :]).then_inc(part_ready, 1)
                if k in (None, AT["part_lo"]):
                    act.wait_ge(rest_ready, fc * 2 + 2)
                    lo = 4 * N
                    nc.scalar.copy(bcs[fq][lo:R, :], bcf[lo:R, :]).then_inc(part_ready, 1)

            def fin(c, q, k):
                if k == AT["xn2_copy"]:
                    wait(act, ff1_psum, c * FB)
                    for f in range(2):
                        act.wait_ge(xn2T_psum, c * 2 + f + 1)
                        nc.scalar.activation(xn2T[:, f, :], tp[f][:, :], ACT.Identity, bias=cols["ln2_b"][:, f:f + 1],
                                             scale=cols["ln2_g"][:, f:f + 1]).then_inc(xn2T_ready, 1)
                if k in GELU_AT:
                    wait(act, ff2_psum, c * 2)
                    for m in (range(4), range(4, FB))[GELU_AT.index(k)]:
                        act.wait_ge(ff1_psum, c * FB + m + 1)
                        nc.scalar.activation(hid[:, m, :], bank[4 + m % 4][:, :], ACT.Gelu,
                                             bias=ff1b[:, m:m + 1]).then_inc(hid_ready, 1)

            def decay(c, q, n):
                s = n % RING
                if n == 0:
                    act.wait_ge(dt_ready, c + 1)
                for f in range(2):
                    wait(act, scan_done[f], c * N + n - RING + 1)
                wait(act, g_ready, c * N + n - RING + 1)
                wait(act, u_ready, c * N + n - 1)
                act.wait_ge(B_psum, c * N + n + 1)
                nc.scalar.copy(bs[n % 2][:, :], bB[:, :]).then_inc(bs_ready, 1)
                for f in range(2):
                    last = nc.scalar.activation(a[s][:, f, :], dt[q][:, f, :], ACT.Exp, scale=A_neg[:, f, n:n + 1])
                last.then_inc(a_ready, 1)
                act.wait_ge(C_psum, c * N + n + 1)
                nc.scalar.copy(cs[s][:, :], bC[:, :]).then_inc(cs_ready, 1)

            def body(c, q, first, last):
                for n in range(N):
                    if n + AHEAD < N:
                        decay(c, q, n + AHEAD)
                    elif not last:
                        decay(c + 1, 1 - q, n + AHEAD - N)
                    if not last:
                        front(c + 1, 1 - q, n)
                    if past(c, 2):
                        fin(c - 2, q, N + n)
                    if not first:
                        fin(c - 1, 1 - q, n)
                    if further(c):
                        front(c + 2, q, n - N)

            def front0(fc, fq):
                fronts01(front)(fc, fq)
                for m in range(AHEAD):
                    decay(0, 0, m)

            sweep(act, chunks, front0, body)
            for k in range(2 * N):
                fin(chunks - 2, 0, N + k)
                fin(chunks - 1, 1, k)

        @block.tensor
        def _(pe):
            pe.wait_ge(loaded, LOADED)
            pe.wait_ge(consts, CONST)

            def widen(name, out, rhs, f):
                for kk in range(2):
                    last = nc.tensor.matmul(out, mats[name][:, kk, f * P:(f + 1) * P], rhs(kk), start=(kk == 0),
                                            stop=(kk == 1))
                return last

            def front(fc, fq, k=None):
                if k in (None, AT["xm_T"]):
                    pe.wait_ge(xm_ready, fc + 1)
                    wait(pe, hid_ready, (fc - 2) * FB)
                    wait(pe, hnew_ready, (fc - 2) * 2)
                    wait(pe, vb_ready, fc * 2)
                    for f in range(2):
                        for j in range(TJ):
                            last = nc.tensor.transpose(tp[f][:, j * P:(j + 1) * P], xn[:, j, f * P:(f + 1) * P],
                                                       core.ident[:, :])
                        last.then_inc(xmT_psum, 1)
                    for f in range(2):
                        last = nc.tensor.transpose(mm[0][:, f:f + 1], xn[0:1, TJ, f * P:(f + 1) * P],
                                                   core.ident[0:1, 0:1])
                    last.then_inc(xmT_psum, 1)
                if k in (None, AT["w1"]):
                    pe.wait_ge(xmT_ready, fc * 3 + 3)
                    for f in range(2):
                        widen("w1_w", mm[f][:, :], lambda kk: xmT[:, kk, 0:T], f).then_inc(x1_psum, 1)
                    for f in range(2):
                        last = widen("w1_w", tp[0][:, f:f + 1], lambda kk: xmT[:, kk, T:T + 1], f)
                    last.then_inc(x1_psum, 1)
                if k in (None, AT["bc"]):
                    pe.wait_ge(xc_ready, fc + 1)
                    pe.wait_ge(x1_ready, fc * 3 + 3)
                    wait(pe, x2_ready, (fc - 1) * 2)
                    for kk in range(2):
                        last = nc.tensor.matmul(mm[0][0:R, :], bcw[:, kk, :, :].rearrange("p a n -> p (a n)"),
                                                xc[fq][:, kk, :], start=(kk == 0), stop=(kk == 1))
                    last.then_inc(bc_psum, 1)
                if k in (None, AT["dt"]):
                    pe.wait_ge(bcf_ready, fc + 1)
                    for f in range(2):
                        widen("dt_w", mm[f][:, :], lambda kk: xc[fq][:, kk, :], f).then_inc(dt_psum, 1)
                if k in (None, AT["v1"]):
                    pe.wait_ge(xs_ready, fc * 2 + 2)
                    for f in range(2):
                        widen("v1_w", mm[f][:, :], lambda kk: xmT[:, kk, 0:T], f).then_inc(vg_psum, 1)

            def fin(c, q, k, fronts):
                if k == AT["w2"]:
                    pe.wait_ge(yv_ready, c + 1)
                    pe.wait_ge(x1_ready, fronts * 3)
                    wait(pe, hnew_ready, c * 2)
                    pe.wait_ge(vb_ready, c * 2 + 2)
                    for m in range(2):
                        for j in range(2):
                            t0 = (2 * m + j) * P
                            for f in range(2):
                                last = nc.tensor.matmul(mm[m][:, j * D:(j + 1) * D], yv[:, f, t0:t0 + P],
                                                        mats["w2_w"][:, f, :], start=(f == 0), stop=(f == 1))
                        last.then_inc(mo_psum, 1)
                if k == AT["xn2_T"]:
                    pe.wait_ge(xn2_ready, c + 1)
                    pe.wait_ge(x1_ready, fronts * 3)
                    for f in range(2):
                        for j in range(TJ):
                            last = nc.tensor.transpose(tp[f][:, j * P:(j + 1) * P], xn2[:, j, f * P:(f + 1) * P],
                                                       core.ident[:, :])
                        last.then_inc(xn2T_psum, 1)
                if k in FF1_AT:
                    pe.wait_ge(xn2T_ready, c * 2 + 2)
                    if k == FF1_AT[1]:
                        pe.wait_ge(x2_ready, c * 2 + 2)
                        pe.wait_ge(vb_ready, fronts * 2)
                    for m in range(FB)[2 * FF1_AT.index(k):][:2]:
                        if m >= 4:
                            pe.wait_ge(hid_ready, c * FB + m - 3)
                        for kk in range(2):
                            last = nc.tensor.matmul(bank[4 + m % 4][:, :], ff1[:, kk, m * P:(m + 1) * P], xn2T[:, kk, :],
                                                    start=(kk == 0), stop=(kk == 1))
                        last.then_inc(ff1_psum, 1)
                for tile in [t for t in range(TJ) if FF2_AT[t] == k]:
                    m, j = divmod(tile, 2)
                    if tile == 0:
                        pe.wait_ge(hid_ready, c * FB + FB)
                    t0 = (2 * m + j) * P
                    for g in range(FB):
                        last = nc.tensor.matmul(mm[m][:, j * D:(j + 1) * D], hid[:, g, t0:t0 + P], ff2[:, g, :],
                                                start=(g == 0), stop=(g == FB - 1))
                    if j == 1:
                        last.then_inc(ff2_psum, 1)

            def spread(c, q, n):
                if n == 0:
                    pe.wait_ge(part_ready, c * 3 + 3)
                wait(pe, bs_ready, c * N + n)
                nc.tensor.matmul(bB[:, :], pick[:, n:n + 1].to_broadcast([R, P]), bcs[q][:, :], start=True,
                                 stop=True).then_inc(B_psum, 1)
                wait(pe, cs_ready, c * N + n)
                nc.tensor.matmul(bC[:, :], pick[:, N + n:N + n + 1].to_broadcast([R, P]), bcs[q][:, :], start=True, stop=True).then_inc(C_psum, 1)

            def reduce(c, n):
                if n == 0:
                    wait(pe, y_ready, c)
                pe.wait_ge(g_ready, c * N + n + 1)
                for f in range(2):
                    last = nc.tensor.matmul(yp[f][:, :], core.ident[:, :], hs[n % RING][:, f, :], start=(n == 0),
                                            stop=(n == N - 1))
                last.then_inc(red_done, 1)

            def body(c, q, first, last):
                fronts = c + 1 if last else c + 2
                for n in range(N):
                    if n + AHEAD < N:
                        spread(c, q, n + AHEAD)
                    elif not last:
                        spread(c + 1, 1 - q, n + AHEAD - N)
                    if n >= LAG:
                        reduce(c, n - LAG)
                    elif not first:
                        reduce(c - 1, N + n - LAG)
                    if not last:
                        front(c + 1, 1 - q, n)
                    if past(c, 2):
                        fin(c - 2, q, N + n, fronts)
                    if not first:
                        fin(c - 1, 1 - q, n, fronts)
                    if further(c):
                        front(c + 2, q, n - N)

            def front0(fc, fq):
                fronts01(front)(fc, fq)
                for m in range(AHEAD):
                    spread(0, 0, m)

            sweep(pe, chunks, front0, body)
            for n in range(N - LAG, N):
                reduce(chunks - 1, n)
            for k in range(2 * N):
                fin(chunks - 2, 0, N + k, chunks)
                fin(chunks - 1, 1, k, chunks)


def moe_phase(core, bias, weights, indices, w1, w2, h_io, h_out):
    nc, bank = core.nc, core.bank
    tokens, K = weights.shape
    E, _, FF = w1.shape
    NT = tokens // P
    NB = tokens // T
    FB = FF // P
    with ExitStack() as ctx:
        def sb(name, shape, dt=F32):
            return ctx.enter_context(nc.sbuf_tensor("m_" + name, shape, dt))

        def sem(name):
            return nc.alloc_semaphore(name="m_" + name)

        passed = sem("passed")

        acc = sb("acc", [P, NT, D])
        bias_b = sb("bias_b", [P, D])
        x = sb("x", [P, NT, D])
        bn = sb("bn", [P, NT, 6])
        mv = sb("mv", [P, NT, 2])
        rstd = sb("rstd", [P, NT])
        xT = sb("xT", [P, 2, tokens])
        wk = sb("wk", [P, NT, K])
        ik = sb("ik", [P, NT, K], I32)
        ikf = sb("ikf", [P, NT, K])
        e_i = sb("e_i", [P, E], I32)
        e_f = sb("e_f", [P, E])
        eq = sb("eq", [P, NT, E])
        cw = sb("cw", [P, NT, E])
        w1s = [sb(f"w1s{s}", [P, 2, FF]) for s in range(2)]
        w2s = [sb(f"w2s{s}", [P, FB, D]) for s in range(2)]
        hid = [sb(f"hid{s}", [P, FB, T]) for s in range(2)]
        cwe = sb("cwe", [P, NT])

        loaded, step_done, iota_done, rstd_step, x_ready, xT_psum, xT_ready, cw_ready = (
            sem("loaded"), sem("step_done"), sem("iota_done"), sem("rstd_step"), sem("x_ready"), sem("xT_psum"),
            sem("xT_ready"), sem("cw_ready"))
        w_loaded = [sem(f"w_loaded{s}") for s in range(2)]
        ff1_psum, hid_ready, ff2_psum, acc_step, cwe_ready, stored = (
            sem("ff1_psum"), sem("hid_ready"), sem("ff2_psum"), sem("acc_step"), sem("cwe_ready"), sem("stored"))
        block = ctx.enter_context(nc.Block())
        rows = h_io[0:tokens, :].rearrange("(j p) d -> p j d", p=P)
        rows_out = h_out[0:tokens, :].rearrange("(j p) d -> p j d", p=P)

        @block.sync
        def _(sp):
            sp.dma_start(acc[:, :, :], rows).then_inc(loaded, 16)
            sp.dma_start(bias_b[:, :], bias.partition_broadcast(P)).then_inc(loaded, 16)
            sp.dma_start(wk[:, :, :], weights.rearrange("(j p) k -> p j k", p=P)).then_inc(loaded, 16)
            sp.dma_start(ik[:, :, :], indices.rearrange("(j p) k -> p j k", p=P)).then_inc(loaded, 16)
            def turn(i):
                for s in range(2):
                    e = i * 2 + s
                    wait(sp, ff2_psum, i * (2 * NT))
                    sp.dma_start(w1s[s][:, :, :], w1[bass.ds(e, 1), :, :].rearrange("o (k p) n -> p (o k) n", p=P)
                                 ).then_inc(w_loaded[s], 16)
                    sp.dma_start(w2s[s][:, :, :], w2[bass.ds(e, 1), :, :].rearrange("o (g p) n -> p (o g) n", p=P)
                                 ).then_inc(w_loaded[s], 16)

            repeat(sp, E // 2, turn)
            sp.wait_ge(acc_step, E * NT)
            sp.dma_start(rows_out, acc[:, :, :]).then_inc(stored, 16)
            sp.wait_ge(stored, 16)

        @block.gpsimd
        def _(pool):
            nc.gpsimd.iota(e_i[:, :], pattern=[[1, E]], base=0, channel_multiplier=0).then_inc(iota_done, 1)
            pool.wait_ge(step_done, 3)
            nc.gpsimd.tensor_tensor(rstd[:, :], mv[:, :, 1], core.eps[:, 0:mv.shape[1]], ALU.add).then_inc(rstd_step, 1)
            pool.wait_ge(rstd_step, 1)
            nc.gpsimd.tensor_tensor(rstd[:, :], rstd[:, :], core.neg_half[:, 0:NT], ALU.pow).then_inc(rstd_step, 1)

        @block.vector
        def _(dve):
            steps = [0]

            def step(ins):
                ins.then_inc(step_done, 1)
                steps[0] += 1
                dve.wait_ge(step_done, steps[0])

            dve.wait_ge(loaded, 64)
            step(nc.vector.tensor_tensor(x[:, :, :], acc[:, :, :], bias_b[:, :].unsqueeze(1).to_broadcast([P, NT, D]),
                                         ALU.subtract))
            for j in range(NT):
                last = nc.vector.bn_stats(bn[:, j, :], x[:, j, :])
            step(last)
            hold(dve, passed)
            for j in range(NT):
                last = nc.vector.bn_aggr(mv[:, j, :], bn[:, j, :])
            step(last)
            dve.wait_ge(rstd_step, 2)
            for j in range(NT):
                last = nc.vector.tensor_scalar(x[:, j, :], x[:, j, :], mv[:, j, 0:1], rstd[:, j:j + 1], ALU.subtract,
                                               ALU.mult)
            last.then_inc(x_ready, 1)
            dve.wait_ge(iota_done, 1)
            nc.vector.tensor_copy(e_f[:, :], e_i[:, :])
            step(nc.vector.tensor_copy(ikf[:, :, :], ik[:, :, :]))
            for k in range(K):
                out = cw if k == 0 else eq
                step(nc.vector.tensor_tensor(out[:, :, :], ikf[:, :, k:k + 1].to_broadcast([P, NT, E]),
                                             e_f[:, :].unsqueeze(1).to_broadcast([P, NT, E]), ALU.is_equal))
                step(nc.vector.tensor_tensor(out[:, :, :], out[:, :, :], wk[:, :, k:k + 1].to_broadcast([P, NT, E]),
                                             ALU.mult))
                if k:
                    step(nc.vector.tensor_tensor(cw[:, :, :], cw[:, :, :], eq[:, :, :], ALU.add))
            def turn(e):
                wait(dve, acc_step, e * NT)
                nc.vector.tensor_copy(cwe[:, :].unsqueeze(2), cw[:, :, bass.ds(e, 1)]).then_inc(cwe_ready, 1)
                wait(dve, cwe_ready, e + 1)
                for j in range(NT):
                    wait(dve, ff2_psum, e * NT + j + 1)
                    nc.vector.scalar_tensor_tensor(acc[:, j, :], bank[4 + j % 4][:, 0:D], cwe[:, j:j + 1], acc[:, j, :],
                                                   ALU.mult, ALU.add).then_inc(acc_step, 1)

            repeat(dve, E, turn)

        @block.scalar
        def _(act):
            for m in range(2 * NB):
                act.wait_ge(xT_psum, m + 1)
                f, b = m % 2, m // 2
                nc.scalar.copy(xT[:, f, b * T:(b + 1) * T], bank[m % 4][:, :]).then_inc(xT_ready, 1)
            def turn(e):
                for b in range(NB):
                    for g in range(FB):
                        t = b * FB + g
                        wait(act, ff1_psum, e * (NB * FB) + t + 1)
                        if g == 0:
                            wait(act, ff2_psum, e * NT)
                        nc.scalar.activation(hid[b][:, g, :], bank[t % 4][:, :], ACT.Gelu).then_inc(hid_ready, 1)

            repeat(act, E, turn)

        @block.tensor
        def _(pe):
            pe.wait_ge(x_ready, 1)
            for m in range(2 * NB):
                f, b = m % 2, m // 2
                for j in range(TJ):
                    last = nc.tensor.transpose(bank[m % 4][:, j * P:(j + 1) * P], x[:, b * TJ + j, f * P:(f + 1) * P],
                                               core.ident[:, :])
                last.then_inc(xT_psum, 1)
            pe.wait_ge(xT_ready, 2 * NB)
            def turn(i):
                for s in range(2):
                    e = i * 2 + s
                    wait(pe, w_loaded[s], i * 32 + 32)
                    for b in range(NB):
                        for g in range(FB):
                            t = b * FB + g
                            if t >= 4:
                                wait(pe, hid_ready, e * (NB * FB) + t - 3)
                            else:
                                wait(pe, hid_ready, e * (NB * FB))
                            for kk in range(2):
                                last = nc.tensor.matmul(bank[t % 4][:, :], w1s[s][:, kk, g * P:(g + 1) * P],
                                                        xT[:, kk, b * T:(b + 1) * T], start=(kk == 0), stop=(kk == 1))
                            last.then_inc(ff1_psum, 1)
                    for j in range(NT):
                        b = j // TJ
                        wait(pe, hid_ready, e * (NB * FB) + (b + 1) * FB)
                        if j >= 4:
                            wait(pe, acc_step, e * NT + j - 3)
                        else:
                            wait(pe, acc_step, e * NT)
                        t0 = (j % TJ) * P
                        for g in range(FB):
                            last = nc.tensor.matmul(bank[4 + j % 4][:, 0:D], hid[b][:, g, t0:t0 + P], w2s[s][:, g, :],
                                                    start=(g == 0), stop=(g == FB - 1))
                        last.then_inc(ff2_psum, 1)

            repeat(pe, E // 2, turn)


def tower(nc, args, out, phases=9):
    ids = args["x"]
    tokens = ids.shape[0] * ids.shape[1]
    chunks = tokens // T
    seq = 2048
    h0 = nc.dram_tensor("h0", (tokens, D), F32, kind="Internal").ap()
    h1 = nc.dram_tensor("h1", (tokens, D), F32, kind="Internal").ap()
    h2 = nc.dram_tensor("h2", (tokens, D), F32, kind="Internal").ap()
    with ExitStack() as ctx:
        core = Core(nc, ctx, chunks, seq // T)
        with nc.cleanup_on_exit():
            build_constants(core)
        with nc.cleanup_on_exit():
            embedding_phase(core, ids, args["L0_tok_ab_n"], args["L0_tok_proj_wT"],
                            args["L0_tok_proj_b"], h0)
        if phases > 1:
            with nc.cleanup_on_exit():
                attention_phase(core, args["L0_attn_Wq"], args["L0_attn_Wf"], args["L0_attn_Wi"],
                                args["L0_attn_Wo"], h0, h1)
        if phases > 2:
            with nc.cleanup_on_exit():
                ffn_phase(core, args["L0_ffn_gate_wT"], args["L0_ffn_down_T"], args["L0_ffn_down_bT"],
                          args["L0_ffn_up_T"], args["L0_ffn_up_b"], h1, h2)
        if phases > 3:
            w = {name[len("L1_attn_"):]: ap for name, ap in args.items() if name.startswith("L1_attn_")}
            w["moe_bias"] = args["L1_ffn_bias"]
            with nc.cleanup_on_exit():
                ssm_phase(core, w, h2, out)
        if phases > 4:
            with nc.cleanup_on_exit():
                moe_phase(core, args["L1_ffn_bias"], args["L1_ffn_expert_weights"], args["L1_ffn_expert_indices"],
                          args["L1_ffn_w1"], args["L1_ffn_w2"], out, out)


def lay_out(inputs):
    import numpy as np

    a = {name: np.asarray(x) for name, x in inputs.items()}
    a["x"] = a["x"].reshape(-1, P)
    a["L0_tok_proj_wT"] = a.pop("L0_tok_proj_w").T
    a["L0_tok_ab_n"] = np.concatenate([a.pop("L0_tok_a_n"), a.pop("L0_tok_b_n")], axis=1)
    a["L0_attn_Wi"] = a["L0_attn_Wi"].reshape(D, 2, 8, 4, 4).transpose(0, 1, 3, 2, 4).reshape(D, D)
    a["L0_attn_Wo"] = a["L0_attn_Wo"].reshape(2, 8, 4, 4, D).transpose(0, 2, 1, 3, 4).reshape(D, D)
    a["L0_ffn_gate_wT"] = a.pop("L0_ffn_gate_w").T
    a["L0_ffn_down_T"] = a.pop("L0_ffn_down_w").transpose(2, 0, 1)
    a["L0_ffn_down_bT"] = a.pop("L0_ffn_down_b").T
    a["L0_ffn_up_T"] = a.pop("L0_ffn_up_w").transpose(2, 0, 1)
    for name in ("ln_g", "ln_b", "w1_b", "v1_b", "dt_b", "D_p", "ln2_g", "ln2_b", "ff1_b"):
        a["L1_attn_" + name] = a["L1_attn_" + name].reshape(-1, P).T
    for name in ("Bp_b", "Cp_b"):
        a["L1_attn_" + name] = a["L1_attn_" + name].reshape(-1, 1)
    del a["L1_ffn_scores"]
    return {name: np.ascontiguousarray(x) for name, x in a.items()}


def kernel(**inputs):
    import concourse.bacc as bacc
    from concourse.bass_utils import run_bass_kernel_spmd

    batch, seq = inputs["x"].shape
    nc = bacc.Bacc("TRN2", target_bir_lowering=False, num_devices=1)
    arrays, args = {}, {}
    for name, a in lay_out(inputs).items():
        arrays[f"in_{name}"] = a
        args[name] = nc.dram_tensor(f"in_{name}", a.shape, mybir.dt.from_np(a.dtype), kind="ExternalInput").ap()
    out = nc.dram_tensor("out_0", (batch * seq, D), F32, kind="ExternalOutput").ap()
    tower(nc, args, out)
    result = run_bass_kernel_spmd(nc, [arrays], core_ids=[0])
    return result.results[0]["out_0"].reshape(batch, seq, D)
```
